# Optimizing a Trainium2 kernel written in Bass

```python
import numpy as np
import jax
import jax.numpy as jnp

def _softmax(x, axis=-1):
    return jax.nn.softmax(x, axis=axis)

def _gelu(x):
    return jax.nn.gelu(x, approximate=True)

def _silu(x):
    return jax.nn.silu(x)

def _sigmoid(x):
    return jax.nn.sigmoid(x)

def _layernorm(x, axis=-1, eps=1e-05):
    m = jnp.mean(x, axis=axis, keepdims=True)
    v = jnp.var(x, axis=axis, keepdims=True)
    return (x - m) / jnp.sqrt(v + eps)

def _scatter_add(tgt, idx, src, axis=0):
    return tgt.at[idx].add(src)

def _segment_sum(src, seg, n):
    return jax.ops.segment_sum(src, seg, n)
kernel_name = 'mk_decoder_preln_d1_seqx_r2_27ced6'

def setup_inputs(seed: int=0):
    np.random.seed(seed)
    _w = jnp.asarray

    def _rec_inputs():
        import jax
        import jax.numpy as jnp
        _rk = jax.random.key(seed)
        x = 7.22e-05 + 1 * jax.random.normal(jax.random.fold_in(_rk, 1), (4, 1024, 1024), jnp.float32)
        _lenS = 1024 - jax.random.randint(jax.random.fold_in(_rk, 7), (4,), 0, max(1, 1024 // 4) + 1, jnp.int32)
        _lenS2 = 1024 - jax.random.randint(jax.random.fold_in(_rk, 8), (4,), 0, max(1, 1024 // 4) + 1, jnp.int32)
        _ctx_1024P = jax.random.normal(jax.random.fold_in(_rk, 11), (4, 16, 512), jnp.float32)
        _ctx_1024c = jax.random.dirichlet(jax.random.fold_in(_rk, 511), 0.3 * jnp.ones((16,), jnp.float32), (4, 1024))
        _ctx_1024t = jnp.einsum('bsk,bkd->bsd', _ctx_1024c, _ctx_1024P)
        _ctx_1024t = _ctx_1024t * jax.lax.rsqrt(jnp.mean(jnp.square(_ctx_1024t)) + 1e-12) * 0.953939
        ctx_1024 = 2.81802e-05 + 1.00001 * (_ctx_1024t + 0.3 * jax.random.normal(jax.random.fold_in(_rk, 611), (4, 1024, 512), jnp.float32))
        return (x, ctx_1024)
    x, ctx_1024 = _rec_inputs()

    def _L0_attn_setup():
        import jax, jax.numpy as jnp
        import numpy as np
        import math
        H = 1024
        NH = 16
        HD = H // NH
        THETA = 10000.0

        def rotate_half(x):
            x1, x2 = (x[..., :HD // 2], x[..., HD // 2:])
            return jnp.concatenate((-x2, x1), axis=-1)

        def rope_tables(seq_len, dtype):
            inv_freq = 1.0 / THETA ** (np.arange(0, HD, 2, dtype=np.float32) / HD)
            t = np.arange(seq_len, dtype=np.float32)
            freqs = np.einsum('i,j->ij', t, inv_freq)
            emb = np.concatenate((freqs, freqs), axis=-1)
            return (jnp.asarray(np.cos(emb), dtype), jnp.asarray(np.sin(emb), dtype))
        key = jax.random.key(seed)
        ks = jax.random.split(key, 5)
        B, S = (2, 1024)
        scale = 1.0 / math.sqrt(H)
        return {'hidden_states': jax.random.normal(ks[0], (B, S, H), jnp.float32), 'Wq': jax.random.normal(ks[1], (H, H), jnp.float32) * scale, 'Wk': jax.random.normal(ks[2], (H, H), jnp.float32) * scale, 'Wv': jax.random.normal(ks[3], (H, H), jnp.float32) * scale, 'Wo': jax.random.normal(ks[4], (H, H), jnp.float32) * scale}
    _L0_attn_all = _L0_attn_setup()
    _L0_attn_in = {k: v for k, v in _L0_attn_all.items() if k in ('Wq', 'Wk', 'Wv', 'Wo')}
    del _L0_attn_all

    def _L0_xattn_setup():
        import jax, jax.numpy as jnp
        import numpy as np
        key = jax.random.key(seed)
        ks = jax.random.split(key, 6)
        B, L, N, C, D = (8, 256, 1024, 512, 128)
        return {'teacher_logits': jax.random.normal(ks[0], (B, L, N), dtype=jnp.float32), 'teacher_features': jax.random.normal(ks[1], (B, N, C), dtype=jnp.float32), 'Wq': jax.random.normal(ks[2], (D, C), dtype=jnp.float32) * (1.0 / np.sqrt(C)), 'bq': jnp.zeros((D,), dtype=jnp.float32), 'Wk': jax.random.normal(ks[3], (D, C), dtype=jnp.float32) * (1.0 / np.sqrt(C)), 'bk': jnp.zeros((D,), dtype=jnp.float32)}
    _L0_xattn_all = _L0_xattn_setup()
    _L0_xattn_in = {k: v for k, v in _L0_xattn_all.items() if k in ('Wq', 'bq', 'Wk', 'bk')}
    del _L0_xattn_all

    def _L0_ffn_setup():
        import jax, jax.numpy as jnp
        import numpy as np
        from jax import lax
        E = 64
        TOP_K = 8
        SEL_K = 4
        THRESH = 0.5
        H = 1024
        F_INT = 384
        B, S = (1, 1024)
        key = jax.random.key(seed)
        k0, k1, k2, k3, k4 = jax.random.split(key, 5)
        return {'hidden_states': jax.random.normal(k0, (B, S, H), jnp.float32), 'gate_weight': jax.random.normal(k1, (E, H), jnp.float32) * 0.02, 'gate_up_proj': jax.random.normal(k2, (E, 2 * F_INT, H), jnp.float32) * 0.02, 'down_proj': jax.random.normal(k3, (E, H, F_INT), jnp.float32) * 0.02, 'similarity': jax.random.uniform(k4, (E, E), jnp.float32)}
    _L0_ffn_all = _L0_ffn_setup()
    _L0_ffn_in = {k: v for k, v in _L0_ffn_all.items() if k in ('gate_weight', 'gate_up_proj', 'down_proj', 'similarity')}
    del _L0_ffn_all
    return {'x': x, 'ctx_1024': ctx_1024, 'L0_attn_Wq': _L0_attn_in['Wq'], 'L0_attn_Wk': _L0_attn_in['Wk'], 'L0_attn_Wv': _L0_attn_in['Wv'], 'L0_attn_Wo': _L0_attn_in['Wo'], 'L0_xattn_Wq': _L0_xattn_in['Wq'], 'L0_xattn_bq': _L0_xattn_in['bq'], 'L0_xattn_Wk': _L0_xattn_in['Wk'], 'L0_xattn_bk': _L0_xattn_in['bk'], 'L0_ffn_gate_weight': _L0_ffn_in['gate_weight'], 'L0_ffn_gate_up_proj': _L0_ffn_in['gate_up_proj'], 'L0_ffn_down_proj': _L0_ffn_in['down_proj'], 'L0_ffn_similarity': _L0_ffn_in['similarity']}

def reference(x, ctx_1024, L0_attn_Wq, L0_attn_Wk, L0_attn_Wv, L0_attn_Wo, L0_xattn_Wq, L0_xattn_bq, L0_xattn_Wk, L0_xattn_bk, L0_ffn_gate_weight, L0_ffn_gate_up_proj, L0_ffn_down_proj, L0_ffn_similarity):
    import jax
    import jax.numpy as jnp

    def _L0_attn_ref(hidden_states, Wq, Wk, Wv, Wo):
        import jax, jax.numpy as jnp
        import numpy as np
        import math
        H = 1024
        NH = 16
        HD = H // NH
        THETA = 10000.0

        def rotate_half(x):
            x1, x2 = (x[..., :HD // 2], x[..., HD // 2:])
            return jnp.concatenate((-x2, x1), axis=-1)

        def rope_tables(seq_len, dtype):
            inv_freq = 1.0 / THETA ** (np.arange(0, HD, 2, dtype=np.float32) / HD)
            t = np.arange(seq_len, dtype=np.float32)
            freqs = np.einsum('i,j->ij', t, inv_freq)
            emb = np.concatenate((freqs, freqs), axis=-1)
            return (jnp.asarray(np.cos(emb), dtype), jnp.asarray(np.sin(emb), dtype))
        B, S, _ = hidden_states.shape

        def proj(W):
            y = jnp.einsum('bsh,oh->bso', hidden_states, W)
            return y.reshape(B, S, NH, HD).transpose(0, 2, 1, 3)
        q, k, v = (proj(Wq), proj(Wk), proj(Wv))
        cos, sin = rope_tables(S, hidden_states.dtype)
        cos, sin = (cos[None, None], sin[None, None])
        q = q * cos + rotate_half(q) * sin
        k = k * cos + rotate_half(k) * sin
        scores = jnp.einsum('bhqd,bhkd->bhqk', q, k) / math.sqrt(HD)
        causal = jnp.triu(jnp.ones((S, S), bool), k=1)
        scores = jnp.where(causal, -jnp.inf, scores)
        attn = jax.nn.softmax(scores, axis=-1)
        out = jnp.einsum('bhqk,bhkd->bhqd', attn, v)
        out = out.transpose(0, 2, 1, 3).reshape(B, S, H)
        return jnp.einsum('bsh,oh->bso', out, Wo)

    def _L0_xattn_ref(teacher_logits, teacher_features, Wq, bq, Wk, bk):
        import jax, jax.numpy as jnp
        import numpy as np
        query = jnp.einsum('bnc,dc->bnd', teacher_features, Wq) + bq
        key = jnp.einsum('bnc,dc->bnd', teacher_features, Wk) + bk
        energy = jnp.einsum('bnd,bmd->bnm', query, key)
        attention = jax.nn.softmax(energy, axis=-1)
        x_m = jnp.einsum('bln,bmn->blm', teacher_logits, attention)
        return x_m

    def _L0_ffn_ref(hidden_states, gate_weight, gate_up_proj, down_proj, similarity):
        import jax, jax.numpy as jnp
        import numpy as np
        from jax import lax
        E = 64
        TOP_K = 8
        SEL_K = 4
        THRESH = 0.5
        H = 1024
        F_INT = 384
        B, S = (1, 1024)
        b, s, h = hidden_states.shape
        x = hidden_states.reshape(-1, h)
        logits = x @ gate_weight.T
        probs = jax.nn.softmax(logits.astype(jnp.float32), axis=-1).astype(logits.dtype)
        top_val, top_idx = lax.top_k(probs, TOP_K)
        top_val = top_val / jnp.clip(top_val.sum(-1, keepdims=True), 1e-12)
        sim = similarity.astype(jnp.float32)
        diag = jnp.arange(E)
        sim = sim.at[diag, diag].set(1.0)
        primary_mask = jnp.zeros((E,), bool).at[top_idx[:, :SEL_K].reshape(-1)].set(True)
        secondary_mask = jnp.zeros((E,), bool).at[top_idx[:, SEL_K:].reshape(-1)].set(True)
        cand = jnp.where(primary_mask[None, :], sim, -jnp.inf)
        best_primary = jnp.argmax(cand, axis=-1)
        best_sim = jnp.max(cand, axis=-1)
        replace = secondary_mask & ~primary_mask & (best_sim >= THRESH)
        mapping = jnp.where(replace, best_primary, jnp.arange(E))
        rerouted = mapping[top_idx]
        rerouted = rerouted.at[:, :SEL_K].set(top_idx[:, :SEL_K])
        flat_e = rerouted.reshape(-1)
        order = jnp.argsort(flat_e)
        tok = order // TOP_K
        xs = x[tok]
        group_sizes = jnp.zeros((E,), jnp.int32).at[flat_e].add(1)
        gu = lax.ragged_dot(xs, jnp.swapaxes(gate_up_proj, 1, 2), group_sizes)
        gate, up = jnp.split(gu, 2, axis=-1)
        hact = jax.nn.silu(gate) * up
        y = lax.ragged_dot(hact, jnp.swapaxes(down_proj, 1, 2), group_sizes)
        w = top_val.reshape(-1)[order]
        out = jnp.zeros_like(x).at[tok].add(y * w[:, None])
        return out.reshape(b, s, h)
    x = x + _L0_attn_ref(_layernorm(x, axis=-1), L0_attn_Wq, L0_attn_Wk, L0_attn_Wv, L0_attn_Wo)
    x = x + _L0_xattn_ref(_layernorm(x, axis=-1), ctx_1024, L0_xattn_Wq, L0_xattn_bq, L0_xattn_Wk, L0_xattn_bk)
    x = x + _L0_ffn_ref(_layernorm(x, axis=-1), L0_ffn_gate_weight, L0_ffn_gate_up_proj, L0_ffn_down_proj, L0_ffn_similarity)
    return x

_drawn_inputs = setup_inputs


def setup_inputs(seed=0):
    import zlib

    import numpy as np

    out = dict(_drawn_inputs(seed))
    spreads = {'L0_xattn_bq': (0.0, 0.1), 'L0_xattn_bk': (0.0, 0.1)}
    factors = {}
    for name, (base, spread) in spreads.items():
        noise = np.random.default_rng([zlib.crc32(name.encode()), seed]).standard_normal(out[name].shape)
        drawn = base * np.exp(spread * noise) if base else spread * noise
        out[name] = jnp.asarray(drawn.astype(out[name].dtype))
    for name, factor in factors.items():
        out[name] = (out[name] * factor).astype(out[name].dtype)
    return out
```

```python
from contextlib import ExitStack

import numpy as np
import concourse.bass as bass
from concourse import mybir

F32 = mybir.dt.float32
F32R = mybir.dt.float32r
BF16 = mybir.dt.bfloat16
I32 = mybir.dt.int32
U32 = mybir.dt.uint32
ALU = mybir.AluOpType
ACT = mybir.ActivationFunctionType
AX = mybir.AxisListType

P = 128
B, S, H = 4, 1024, 1024
NH, HD = 16, 64
HB = H // P
TB = S // P
NP = NH // 2
C, D = 512, 128
CB = C // P
E, TOPK, SELK, F = 64, 8, 4, 384
FB = F // P
BANK = 512
GQ = BANK // P
EPS = 1e-5
MASKED = -1e30


class Memory:

    def __init__(self, nc, scope):
        self.nc, self.scope = nc, scope

    def sb(self, name, shape, dt=F32):
        return self.scope.enter_context(self.nc.sbuf_tensor(name, shape, dt))

    def ps(self, name, shape, dt=F32):
        return self.scope.enter_context(self.nc.psum_tensor(name, shape, dt))

    def sem(self, name):
        return self.scope.enter_context(self.nc.semaphore(name))


def raw(ap):
    return ap.bitcast(F32)


def stand_alone(eng, passed):
    eng.sem_inc(passed, 1)


def constants(nc, m):
    ident = m.sb("ident", [P, P])
    ident16 = m.sb("ident16", [P, P], BF16)
    mask16 = m.sb("mask16", [P, P], BF16)
    half = m.sb("minus_half", [P, TB])
    made = m.sem("const_made")
    passed = m.sem("passed")
    with nc.Block() as block:
        @block.gpsimd
        def _(pool):
            pool.memset(ident[:, :], 0.0).then_inc(made, 1)
            pool.memset(ident16[:, :], 0.0).then_inc(made, 1)
            pool.memset(mask16[:, :], 0.0).then_inc(made, 1)
            pool.memset(half[:, :], -0.5).then_inc(made, 1)
            pool.wait_ge(made, 4)
            for t in (ident, ident16):
                pool.affine_select(out=t[:, :], in_=t[:, :], compare_op=ALU.not_equal, fill=1.0,
                                   base=0, pattern=[[-1, P]], channel_multiplier=1).then_inc(made, 1)
            pool.affine_select(out=mask16[:, :], in_=mask16[:, :], compare_op=ALU.is_ge, fill=MASKED,
                               base=0, pattern=[[-1, P]], channel_multiplier=1).then_inc(made, 1)
            pool.wait_ge(made, 7)
    return ident, ident16, mask16, half, passed


def self_attention(nc, const, x, wqkv, cos, sin, attn_out):
    ident, ident16, mask16, half, passed = const
    W = 3 * P
    UNITS = [(h, g) for h in range(2) for g in range(S // BANK)]
    KB = [GQ * (g + 1) for _, g in UNITS]
    NK = sum(KB)
    NQ = GQ * len(UNITS)
    PTS = 3
    with ExitStack() as scope:
        m = Memory(nc, scope)
        x_tile = m.sb("x_tile", [P, 2, H])
        stats = m.sb("ln1_stats", [P, TB, 2, 6])
        mean_var = m.sb("ln1_mean_var", [P, TB, 2])
        rstd = m.sb("ln1_rstd", [P, TB])
        xt_hi = m.sb("xt_hi", [P, HB, S], F32R)
        xt_lo = m.sb("xt_lo", [P, HB, S], F32R)
        w_raw = m.sb("w_raw", [P, HB, W])
        w_hi = m.sb("w_hi", [P, HB, W], F32R)
        w_lo = m.sb("w_lo", [P, HB, W], F32R)
        cos_sb = m.sb("cos_sb", [P, TB, 2, HD])
        sin_sb = m.sb("sin_sb", [P, TB, 2, HD])
        r_cos = m.sb("r_cos", [P, 4, HD])
        r_sin = m.sb("r_sin", [P, 4, HD])
        rotated = m.sb("rotated", [P, 2, 4, 2, HD])
        qk_hi = m.sb("qk_hi", [P, 4, S], F32R)
        q_lo = m.sb("q_lo", [P, 2, S], F32R)
        v_hi = m.sb("v_hi", [P, TB, 2, P], F32R)
        v_lo = m.sb("v_lo", [P, TB, 2, P], F32R)
        neg_max = m.sb("neg_max", [P, NQ])
        probs = [m.sb(f"probs{g}", [P, GQ, BANK * (g + 1)]) for g in range(S // BANK)]
        pt_hi = m.sb("pt_hi", [P, PTS, BANK], F32R)
        pt_lo = m.sb("pt_lo", [P, PTS, BANK], F32R)
        inv_sum = m.sb("inv_sum", [HD, BANK])
        out_t = m.sb("out_t", [P, 2, BANK])
        ps_s = m.ps("ps_s", [P, 2, 2 * BANK])
        ps_t = m.ps("ps_t", [P, 2, BANK])
        ps_o = m.ps("ps_o", [P, 2, BANK])

        x_in = [m.sem(f"x_in{i}") for i in range(2)]
        x_free = m.sem("x_free")
        w_in, w_free = m.sem("w_in"), m.sem("w_free")
        tab_in, fill_ok = m.sem("tab_in"), m.sem("fill_ok")
        ln_step, ln_eps, ln_rstd = m.sem("ln_step"), m.sem("ln_eps"), m.sem("ln_rstd")
        xn_ok, xt_ok, xt_hi_ok, xt_lo_ok = (m.sem(n) for n in ("xn_ok", "xt_ok", "xt_hi_ok", "xt_lo_ok"))
        w_hi_ok, w_lo_ok = m.sem("w_hi_ok"), m.sem("w_lo_ok")
        qkv_ok, qkv_read = m.sem("qkv_ok"), m.sem("qkv_read")
        v_hi_ok, rot_step, rot_ok = m.sem("v_hi_ok"), m.sem("rot_step"), m.sem("rot_ok")
        qkt_ok, qk_hi_ok, qk_lo_ok = m.sem("qkt_ok"), m.sem("qk_hi_ok"), m.sem("qk_lo_ok")
        s_ok, max_ok, exp_ok = m.sem("s_ok"), m.sem("max_ok"), m.sem("exp_ok")
        pt_ok, pt_hi_ok, pt_lo_ok, pv_ok = (m.sem(n) for n in ("pt_ok", "pt_hi_ok", "pt_lo_ok", "pv_ok"))
        inv_ok, o_ok, o_out = m.sem("inv_ok"), m.sem("o_ok"), [m.sem(f"o_out{i}") for i in range(2)]

        def steps(u):
            per = KB[u] // GQ
            return [(kb, (kb + 1) // per - 1 if (kb + 1) % per == 0 else None) for kb in range(KB[u])]

        def tiles_before(u):
            return sum(KB[:u])

        block = scope.enter_context(nc.Block())

        @block.sync
        def _(sp):
            sp.dma_start(cos_sb[:, :, :, :], cos.rearrange("(t p) a d -> p t a d", p=P)).then_inc(tab_in, 16)
            sp.dma_start(sin_sb[:, :, :, :], sin.rearrange("(t p) a d -> p t a d", p=P)).then_inc(tab_in, 16)
            sp.dma_start(w_raw[:, :, :], wqkv[0].rearrange("(k p) c -> p k c", p=P)).then_inc(w_in, 16)
            with sp.Fori(0, B) as b:
                for t in range(TB):
                    sp.wait_ge(x_free, b * TB + t + 1)
                    sp.dma_start(x_tile[:, t % 2, :], x[b, t * P:(t + 1) * P, :]).then_inc(x_in[t % 2], 16)
                with sp.Fori(1, NP) as pair:
                    sp.wait_ge(w_free, b * NP + pair)
                    sp.dma_start(w_raw[:, :, :], wqkv[pair].rearrange("(k p) c -> p k c", p=P)).then_inc(w_in, 16)
                sp.wait_ge(w_free, b * NP + NP)
                sp.dma_start(w_raw[:, :, :], wqkv[0].rearrange("(k p) c -> p k c", p=P)).then_inc(w_in, 16)
            sp.wait_ge(w_in, 16 * (B * NP + 1))

        @block.gpsimd
        def _(pool):
            pool.memset(raw(v_hi[:, :, :, HD:]), 1.0)
            pool.memset(raw(v_lo[:, :, :, HD:]), 0.0).then_inc(fill_ok, 1)
            with pool.Fori(0, B) as b:
                for t in range(TB):
                    pool.wait_ge(ln_step, (b * TB + t) * 3 + 3)
                    stand_alone(pool, passed)
                    pool.tensor_scalar(rstd[:, t:t + 1], mean_var[:, t, 1:2], EPS, 1.0, ALU.add, ALU.mult).then_inc(ln_eps, 1)
                    pool.wait_ge(ln_eps, b * TB + t + 1)
                    pool.tensor_tensor(rstd[:, t:t + 1], rstd[:, t:t + 1], half[:, 0:1], ALU.pow).then_inc(ln_rstd, 1)
                with pool.Fori(0, NP) as pair:
                    for u, (h, g) in enumerate(UNITS):
                        pool.wait_ge(o_ok, (b * NP + pair) * len(UNITS) + u + 1)
                        pool.dma_start(attn_out[b, pair, h * HD:(h + 1) * HD, g * BANK:(g + 1) * BANK],
                                       out_t[h * HD:(h + 1) * HD, u % 2, :]).then_inc(o_out[u % 2], 16)
            for i in range(2):
                pool.wait_ge(o_out[i], 16 * B * NP * len(UNITS) // 2)

        @block.tensor
        def _(pe):
            def split_product(out, a_hi, a_lo, w_hi, w_lo, first, last):
                pe.matmul(out, a_hi, w_hi, start=first, stop=False)
                pe.matmul(out, a_hi, w_lo, start=False, stop=False)
                return pe.matmul(out, a_lo, w_hi, start=False, stop=last)

            def scores(j, u, i):
                h, g = UNITS[u]
                n = GQ * u + i
                qb = GQ * g + i
                if n >= 2:
                    pe.wait_ge(exp_ok, j * NQ + n - 1)
                keys = P * (qb + 1)
                for c in range(0, keys, BANK):
                    w = max(min(BANK, keys - c), 2 * P)
                    out = ps_s[:, n % 2, c:c + w]
                    pe.matmul(out, qk_hi[:, h, qb * P:(qb + 1) * P], qk_hi[:, 2 + h, c:c + w],
                              start=True, stop=False, skip_group_check=True)
                    pe.matmul(out, q_lo[0:HD, h, qb * P:(qb + 1) * P], qk_hi[0:HD, 2 + h, c:c + w],
                              start=False, stop=True, skip_group_check=True)
                mm = pe.matmul(ps_s[:, n % 2, qb * P:(qb + 1) * P], ident16[:, :], mask16[:, :],
                               start=False, stop=True, skip_group_check=True)
                mm.then_inc(s_ok, 1)

            def turn_probs(j, u, kb):
                h, g = UNITS[u]
                n = tiles_before(u) + kb
                if n >= 2:
                    pe.wait_ge(pt_lo_ok, j * NK + n - 1)
                if kb == 0:
                    pe.wait_ge(exp_ok, j * NQ + GQ * (u + 1))
                for i in range(max(0, kb - GQ * g), GQ):
                    mm = pe.transpose(ps_t[:, n % 2, i * P:(i + 1) * P], probs[g][:, i, kb * P:(kb + 1) * P], ident[:, :])
                mm.then_inc(pt_ok, 1)

            def weigh_values(j, u, kb):
                h, g = UNITS[u]
                n = tiles_before(u) + kb
                pe.wait_ge(pt_lo_ok, j * NK + n + 1)
                if kb == 0 and u >= 2:
                    pe.wait_ge(o_ok, j * len(UNITS) + u - 1)
                if kb == 0 and u < 2:
                    pe.wait_ge(o_ok, j * len(UNITS))
                off = P * max(0, kb - GQ * g)
                out = ps_o[:, u % 2, off:]
                hi, lo = pt_hi[:, n % PTS, off:], pt_lo[:, n % PTS, off:]
                pe.matmul(out, v_hi[:, kb, h, :], hi, start=(kb == 0), stop=False, skip_group_check=True)
                pe.matmul(out, v_hi[:, kb, h, :], lo, start=False, stop=False, skip_group_check=True)
                pe.matmul(out, v_lo[:, kb, h, :], hi, start=False, stop=True,
                          skip_group_check=True).then_inc(pv_ok, 1)

            pe.wait_ge(fill_ok, 1)
            with pe.Fori(0, B) as b:
                pe.wait_ge(exp_ok, b * NP * NQ)
                for t in range(TB):
                    pe.wait_ge(xn_ok, b * TB + t + 1)
                    if t >= 2:
                        pe.wait_ge(xt_lo_ok, b * TB + t - 1)
                    for k in range(HB):
                        mm = pe.transpose(ps_s[:, t % 2, k * P:(k + 1) * P], x_tile[:, t % 2, k * P:(k + 1) * P], ident[:, :])
                    mm.then_inc(xt_ok, 1)
                pe.wait_ge(xt_lo_ok, b * TB + TB)
                stand_alone(pe, passed)
                with pe.Fori(0, NP) as pair:
                    j = b * NP + pair

                    def turn_qk(t):
                        pe.wait_ge(rot_ok, j * TB + t + 1)
                        if t >= 2:
                            pe.wait_ge(qk_lo_ok, j * TB + t - 1)
                        else:
                            pe.wait_ge(pt_lo_ok, j * NK)
                        for r in range(4):
                            mm = pe.transpose(ps_t[:, t % 2, r * P:(r + 1) * P],
                                              rotated[:, t % 2, r, :, :].rearrange("p a d -> p (a d)"), ident[:, :])
                        mm.then_inc(qkt_ok, 1)

                    pe.wait_ge(exp_ok, j * NQ)
                    for t in range(TB):
                        if t >= 2:
                            pe.wait_ge(qkv_read, j * TB + t - 1)
                        for k in range(HB):
                            if t == 0:
                                pe.wait_ge(w_lo_ok, j * HB + k + 1)
                            a = slice(t * P, (t + 1) * P)
                            mm = split_product(ps_s[:, t % 2, 0:W], xt_hi[:, k, a], xt_lo[:, k, a],
                                               w_hi[:, k, :], w_lo[:, k, :], k == 0, k == HB - 1)
                        mm.then_inc(qkv_ok, 1)
                        if t >= 1:
                            turn_qk(t - 1)
                    turn_qk(TB - 1)
                    pe.wait_ge(qkv_read, j * TB + TB)
                    pe.wait_ge(qk_lo_ok, j * TB + TB)
                    for i in range(GQ):
                        scores(j, 0, i)
                    for u in range(len(UNITS)):
                        for kb, after in steps(u):
                            turn_probs(j, u, kb)
                            if after is not None and u + 1 < len(UNITS):
                                scores(j, u + 1, after)
                            if kb > 0:
                                weigh_values(j, u, kb - 1)
                        weigh_values(j, u, KB[u] - 1)

        @block.scalar
        def _(act):
            with act.Fori(0, B) as b:
                act.wait_ge(qkv_ok, b * NP * TB)
                for t in range(TB):
                    act.wait_ge(xt_ok, b * TB + t + 1)
                    act.activation(xt_hi[:, :, t * P:(t + 1) * P],
                                   ps_s[:, t % 2, :].rearrange("p (k c) -> p k c", c=P), ACT.Copy).then_inc(xt_hi_ok, 1)
                with act.Fori(0, NP) as pair:
                    j = b * NP + pair
                    act.wait_ge(w_in, 16 * j + 16)
                    act.wait_ge(qkv_ok, j * TB)
                    for k in range(HB):
                        act.activation(w_hi[:, k, :], w_raw[:, k, :], ACT.Copy).then_inc(w_hi_ok, 1)
                    act.wait_ge(s_ok, j * NQ)
                    act.wait_ge(pv_ok, j * NK)

                    def split_qk(t):
                        act.wait_ge(qkt_ok, j * TB + t + 1)
                        act.activation(qk_hi[:, :, t * P:(t + 1) * P],
                                       ps_t[:, t % 2, :].rearrange("p (r c) -> p r c", c=P), ACT.Copy).then_inc(qk_hi_ok, 1)

                    for t in range(TB):
                        act.wait_ge(qkv_ok, j * TB + t + 1)
                        act.activation(v_hi[:, t, :, 0:HD],
                                       ps_s[:, t % 2, 2 * P:W].rearrange("p (h d) -> p h d", d=HD), ACT.Copy).then_inc(v_hi_ok, 1)
                        if t >= 1:
                            split_qk(t - 1)
                    split_qk(TB - 1)

                    def exps(u, i):
                        h, g = UNITS[u]
                        n = GQ * u + i
                        act.wait_ge(max_ok, j * NQ + n + 1)
                        if i == 0:
                            if u >= 2:
                                act.wait_ge(pt_ok, j * NK + tiles_before(u - 1))
                            else:
                                act.wait_ge(pt_ok, j * NK)
                        keys = P * (GQ * g + i + 1)
                        act.activation(probs[g][:, i, 0:keys], ps_s[:, n % 2, 0:keys], ACT.Exp,
                                       bias=neg_max[:, n:n + 1]).then_inc(exp_ok, 1)

                    def split_probs(u, kb):
                        h, g = UNITS[u]
                        n = tiles_before(u) + kb
                        act.wait_ge(pt_ok, j * NK + n + 1)
                        if n >= PTS:
                            act.wait_ge(pv_ok, j * NK + n - PTS + 1)
                        off = P * max(0, kb - GQ * g)
                        act.activation(pt_hi[:, n % PTS, off:], ps_t[:, n % 2, off:], ACT.Copy).then_inc(pt_hi_ok, 1)

                    for i in range(GQ):
                        exps(0, i)
                    for u in range(len(UNITS)):
                        for kb, after in steps(u):
                            split_probs(u, kb)
                            if after is not None and u + 1 < len(UNITS):
                                exps(u + 1, after)

        @block.vector
        def _(dve):
            dve.sem_inc(x_free, 2)
            dve.wait_ge(tab_in, 32)
            with dve.Fori(0, B) as b:
                def moments(t):
                    dve.wait_ge(x_in[t % 2], (b * (TB // 2) + t // 2) * 16 + 16)
                    for c in range(2):
                        dve.bn_stats(stats[:, t, c, :], x_tile[:, t % 2, c * BANK:(c + 1) * BANK]).then_inc(ln_step, 1)
                    dve.wait_ge(ln_step, (b * TB + t) * 3 + 2)
                    stand_alone(dve, passed)
                    dve.bn_aggr(mean_var[:, t, :], stats[:, t, :, :].rearrange("p a s -> p (a s)")).then_inc(ln_step, 1)

                def normalise(t):
                    dve.wait_ge(ln_rstd, b * TB + t + 1)
                    dve.tensor_scalar(x_tile[:, t % 2, :], x_tile[:, t % 2, :], mean_var[:, t, 0:1], rstd[:, t:t + 1],
                                      ALU.subtract, ALU.mult).then_inc(xn_ok, 1)

                def rest_of_x(t):
                    dve.wait_ge(xt_hi_ok, b * TB + t + 1)
                    dve.tensor_tensor(xt_lo[:, :, t * P:(t + 1) * P],
                                      ps_s[:, t % 2, :].rearrange("p (k c) -> p k c", c=P),
                                      raw(xt_hi[:, :, t * P:(t + 1) * P]), ALU.subtract).then_inc(xt_lo_ok, 1)
                    dve.sem_inc(x_free, 1)

                moments(0)
                for t in range(TB):
                    normalise(t)
                    if t >= 1:
                        rest_of_x(t - 1)
                    if t + 1 < TB:
                        moments(t + 1)
                rest_of_x(TB - 1)

                with dve.Fori(0, NP) as pair:
                    j = b * NP + pair
                    for k in range(HB):
                        dve.wait_ge(w_hi_ok, j * HB + k + 1)
                        ins = dve.tensor_tensor(w_lo[:, k, :], w_raw[:, k, :], raw(w_hi[:, k, :]), ALU.subtract)
                        ins.then_inc(w_lo_ok, 1)
                    dve.wait_ge(w_lo_ok, j * HB + HB)
                    dve.sem_inc(w_free, 1)

                    def rotate(t):
                        n = j * TB + t
                        dve.wait_ge(v_hi_ok, n + 1)
                        qk = ps_s[:, t % 2, 0:2 * P].rearrange("p (a h d) -> p a h d", a=2, d=HD)
                        c = r_cos[:, :, :].rearrange("p (a h) d -> p a h d", a=2)
                        s = r_sin[:, :, :].rearrange("p (a h) d -> p a h d", a=2)
                        half_d = HD // 2
                        cb = cos_sb[:, t, :, :].unsqueeze(2).broadcast_to([P, 2, 2, HD])
                        sb_ = sin_sb[:, t, :, :].unsqueeze(2).broadcast_to([P, 2, 2, HD])
                        dve.wait_ge(rot_ok, n)
                        dve.tensor_tensor(c, qk, cb, ALU.mult).then_inc(rot_step, 1)
                        dve.tensor_tensor(s[:, :, :, 0:half_d], qk[:, :, :, half_d:], sb_[:, :, :, 0:half_d], ALU.mult).then_inc(rot_step, 1)
                        dve.tensor_tensor(s[:, :, :, half_d:], qk[:, :, :, 0:half_d], sb_[:, :, :, half_d:], ALU.mult).then_inc(rot_step, 1)
                        dve.tensor_tensor(v_lo[:, t, :, 0:HD], ps_s[:, t % 2, 2 * P:W].rearrange("p (h d) -> p h d", d=HD),
                                          raw(v_hi[:, t, :, 0:HD]), ALU.subtract).then_inc(qkv_read, 1)
                        dve.wait_ge(rot_step, n * 3 + 3)
                        if t >= 2:
                            dve.wait_ge(qkt_ok, n - 1)
                        dve.tensor_tensor(rotated[:, t % 2, :, :, :],
                                          r_cos[:, :, :].unsqueeze(2).broadcast_to([P, 4, 2, HD]),
                                          r_sin[:, :, :].unsqueeze(2).broadcast_to([P, 4, 2, HD]), ALU.add).then_inc(rot_ok, 1)

                    def rest_of_qk(t):
                        dve.wait_ge(qk_hi_ok, j * TB + t + 1)
                        a = slice(t * P, (t + 1) * P)
                        both = ps_t[:, t % 2, :].rearrange("p (r c) -> p r c", c=P)
                        dve.tensor_tensor(q_lo[0:HD, :, a], both[0:HD, 0:2, :], raw(qk_hi[0:HD, 0:2, a]), ALU.subtract)
                        dve.tensor_tensor(qk_hi[HD:P, 2:4, a], both[HD:P, 2:4, :], raw(qk_hi[HD:P, 2:4, a]),
                                          ALU.subtract).then_inc(qk_lo_ok, 1)

                    for t in range(TB):
                        rotate(t)
                        if t >= 1:
                            rest_of_qk(t - 1)
                    rest_of_qk(TB - 1)

                    def maxima(u, i):
                        h, g = UNITS[u]
                        n = GQ * u + i
                        dve.wait_ge(s_ok, j * NQ + n + 1)
                        keys = P * (GQ * g + i + 1)
                        dve.tensor_reduce(neg_max[:, n:n + 1], ps_s[:, n % 2, 0:keys], AX.X, ALU.max, negate=True).then_inc(max_ok, 1)

                    def rest_of_probs(u, kb):
                        h, g = UNITS[u]
                        n = tiles_before(u) + kb
                        dve.wait_ge(pt_hi_ok, j * NK + n + 1)
                        off = P * max(0, kb - GQ * g)
                        dve.tensor_tensor(pt_lo[:, n % PTS, off:], ps_t[:, n % 2, off:], raw(pt_hi[:, n % PTS, off:]),
                                          ALU.subtract).then_inc(pt_lo_ok, 1)

                    def divide(u):
                        h, g = UNITS[u]
                        n = j * len(UNITS) + u
                        dve.wait_ge(pv_ok, j * NK + tiles_before(u + 1))
                        dve.reciprocal(inv_sum[:, :], ps_o[HD:P, u % 2, :]).then_inc(inv_ok, 1)
                        dve.wait_ge(inv_ok, n + 1)
                        if u >= 2:
                            dve.wait_ge(o_out[u % 2], (j * 2 + 1) * 16)
                        else:
                            dve.wait_ge(o_out[u % 2], j * 2 * 16)
                        dve.tensor_tensor(out_t[h * HD:(h + 1) * HD, u % 2, :], ps_o[0:HD, u % 2, :],
                                          inv_sum[:, :], ALU.mult).then_inc(o_ok, 1)

                    for i in range(GQ):
                        maxima(0, i)
                    for u in range(len(UNITS)):
                        for kb, after in steps(u):
                            rest_of_probs(u, kb)
                            if after is not None and u + 1 < len(UNITS):
                                maxima(u + 1, after)
                            if kb == 0 and u > 0:
                                divide(u - 1)
                    divide(len(UNITS) - 1)


def mix_features(nc, const, logits, x, attn_out, wo, ctx_t, xw, xbias, gate, rows, out):
    ident, ident16, mask16, half, passed = const
    HALVES = H // BANK
    with ExitStack() as scope:
        m = Memory(nc, scope)
        wo_hi = m.sb("wo_hi", [P, HB, H], F32R)
        wo_lo = m.sb("wo_lo", [P, HB, H], F32R)
        xw_hi = m.sb("xw_hi", [P, CB, 2 * D], F32R)
        xw_lo = m.sb("xw_lo", [P, CB, 2 * D], F32R)
        bias = m.sb("xattn_bias", [P, 2])
        gate_sb = m.sb("gate_sb", [P, HB, E])
        at_hi = m.sb("at_hi", [P, TB, S], F32R)
        at_lo = m.sb("at_lo", [P, TB, S], F32R)
        split = m.sb("split", [P, 4, H], F32R)
        qk = m.sb("xattn_qk", [P, 4, S], F32R)
        stage = m.sb("stage", [P, 2, H])
        work = m.sb("work", [P, 2, H])
        res = m.sb("residual", [P, 2, H])
        x3_t = m.sb("x3_t", [P, HB, P])
        small = m.sb("mix_small", [P, 8, 4])
        stats = m.sb("mix_stats", [P, 2, 2, 6])
        mean_var = m.sb("mix_mean_var", [P, 2, 2])
        rstd = m.sb("mix_rstd", [P, 2])
        ps_a = m.ps("ps_a", [P, H])
        ps_b = m.ps("ps_b", [P, H])
        ps_t2 = m.ps("ps_t2", [P, H])
        ps_r = m.ps("ps_r", [P, 2, BANK])
        ps_e = [ps_a, ps_b]

        zero_ok, zero_out = m.sem("zero_ok"), m.sem("zero_out")
        w_in = [m.sem(f"mix_w_in{i}") for i in range(2)]
        small_in = m.sem("mix_small_in")
        w_hi_ok, w_lo_ok = m.sem("mix_w_hi"), m.sem("mix_w_lo")
        ctx_in, ctx_hi, ctx_lo = m.sem("ctx_in"), m.sem("ctx_hi"), m.sem("ctx_lo")
        proj_ok, proj_hi, proj_lo = m.sem("proj_ok"), m.sem("proj_hi"), m.sem("proj_lo")
        e_ok, emax_ok, eexp_ok, einv_ok, enorm_ok = (m.sem(n) for n in ("e_ok", "emax_ok", "eexp_ok", "einv_ok", "enorm_ok"))
        et_ok, et_hi, et_lo = m.sem("et_ok"), m.sem("et_hi"), m.sem("et_lo")
        ot_in, res_in = [m.sem(f"ot_in{i}") for i in range(2)], [m.sem(f"res_in{i}") for i in range(2)]
        ot_hi, ot_lo = m.sem("ot_hi"), m.sem("ot_lo")
        wo_ok, x1_ok = m.sem("wo_ok"), m.sem("x1_ok")
        ln_step, ln_eps, ln_rstd, ln_ok = (m.sem(n) for n in ("mix_ln_step", "mix_ln_eps", "mix_ln_rstd", "mix_ln_ok"))
        t2_ok, t2_hi, t2_lo = m.sem("t2_ok"), m.sem("t2_hi"), m.sem("t2_lo")
        xm_ok, x2_ok, x2_out, x3_out = m.sem("xm_ok"), m.sem("x2_ok"), m.sem("x2_out"), m.sem("x3_out")
        t3_ok, t3_read, r_ok, r_read = m.sem("t3_ok"), m.sem("t3_read"), m.sem("r_ok"), m.sem("r_read")

        order = [(2, 0)]
        for i in range(TB):
            order += [(2, i + 1)] * (i + 1 < TB) + [(3, i)]
        LN = {what: n for n, what in enumerate(order)}

        block = scope.enter_context(nc.Block())

        @block.sync
        def _(sp):
            sp.wait_ge(zero_ok, 1)
            sp.dma_start(rows[0:P, 0:H], res[:, 0, :]).then_inc(zero_out, 16)
            sp.dma_start(rows[0:P, H:H + E], res[:, 0, 0:E]).then_inc(zero_out, 16)
            sp.dma_start(out[0:P, :], res[:, 0, :]).then_inc(zero_out, 16)
            sp.dma_start(bias[:, :], xbias).then_inc(small_in, 16)
            sp.dma_start(gate_sb[:, :, :], gate.rearrange("(k p) e -> p k e", p=P)).then_inc(small_in, 16)
            for k in range(HB + 1):
                if k >= 2:
                    sp.wait_ge(w_lo_ok, k - 1)
                if k < HB:
                    sp.dma_start(stage[:, k % 2, :], wo[k * P:(k + 1) * P, :]).then_inc(w_in[k % 2], 16)
                else:
                    sp.dma_start(stage[:, k % 2, :].rearrange("p (c d) -> p c d", d=2 * D),
                                 xw.rearrange("(c p) d -> p c d", p=P)).then_inc(w_in[k % 2], 16)
            sp.wait_ge(w_lo_ok, HB + 1)
            sp.wait_ge(zero_out, 48)
            with sp.Fori(0, B) as b:
                for n in range(2):
                    sp.wait_ge(ctx_lo, (b * 2 + n) * CB)
                    stand_alone(sp, passed)
                    if n == 0:
                        sp.wait_ge(ot_lo, b * TB)
                        stand_alone(sp, passed)
                    sp.dma_start(stage[:, :, :].rearrange("p a (c n) -> p (a c) n", n=BANK),
                                 ctx_t[b].rearrange("(c p) n -> p c n", p=P)[:, :, n * BANK:(n + 1) * BANK]).then_inc(ctx_in, 16)

                def load_attn(i):
                    if i >= 2:
                        sp.wait_ge(ot_lo, b * TB + i - 1)
                    sp.dma_start(stage[:, i % 2, :].rearrange("p (k c) -> p k c", c=P),
                                 attn_out[b].rearrange("k p c -> p k c")[:, :, i * P:(i + 1) * P]).then_inc(ot_in[i % 2], 16)

                def load_x(i):
                    sp.dma_start(res[:, i % 2, :], x[b, i * P:(i + 1) * P, :]).then_inc(res_in[i % 2], 16)

                load_x(0)
                load_x(1)
                sp.wait_ge(ctx_lo, (b * 2 + 2) * CB)
                stand_alone(sp, passed)
                load_attn(0)
                load_attn(1)
                for i in range(TB):
                    if i + 2 < TB:
                        load_attn(i + 2)
                    row = P + (b * TB + i) * P
                    sp.wait_ge(x2_ok, b * TB + i + 1)
                    sp.dma_start(out[bass.ds(row, P), :], res[:, i % 2, :]).then_inc(x2_out, 16)
                    sp.wait_ge(ln_ok, b * 2 * TB + LN[3, i] + 1)
                    sp.dma_start(rows[bass.ds(row, P), 0:H], work[:, 1, :]).then_inc(x3_out, 16)
                    sp.wait_ge(x2_out, (b * TB + i + 1) * 16)
                    stand_alone(sp, passed)
                    if i + 2 < TB:
                        load_x(i + 2)
            sp.wait_ge(x3_out, B * TB * 16)

        @block.gpsimd
        def _(pool):
            pool.memset(res[:, 0, :], 0.0).then_inc(zero_ok, 1)
            with pool.Fori(0, B) as b:
                for which, i in order:
                    n = b * 2 * TB + LN[which, i]
                    s = which - 2
                    pool.wait_ge(ln_step, n * 3 + 3)
                    stand_alone(pool, passed)
                    pool.tensor_scalar(rstd[:, s:s + 1], mean_var[:, s, 1:2], EPS, 1.0, ALU.add, ALU.mult).then_inc(ln_eps, 1)
                    pool.wait_ge(ln_eps, n + 1)
                    pool.tensor_tensor(rstd[:, s:s + 1], rstd[:, s:s + 1], half[:, 0:1], ALU.pow).then_inc(ln_rstd, 1)

        @block.tensor
        def _(pe):
            def split_product(out, a_hi, a_lo, w_hi, w_lo, first, last):
                pe.matmul(out, a_hi, w_hi, start=first, stop=False)
                pe.matmul(out, a_hi, w_lo, start=False, stop=False)
                return pe.matmul(out, a_lo, w_hi, start=False, stop=last)

            pe.wait_ge(w_lo_ok, HB + 1)
            pe.wait_ge(small_in, 32)
            with pe.Fori(0, B) as b:
                for n in range(2):
                    pe.wait_ge(ctx_lo, (b * 2 + n + 1) * CB)
                    for w in range(2):
                        pe.wait_ge(proj_lo, (b * 2 + n) * 2)
                        pe.wait_ge(r_read, b * TB)
                        hi = split[:, 0:2, :].rearrange("p a (c n) -> p (a c) n", n=BANK)
                        lo = split[:, 2:4, :].rearrange("p a (c n) -> p (a c) n", n=BANK)
                        for c in range(CB):
                            mm = split_product(ps_r[:, w, :], xw_hi[:, c, w * D:(w + 1) * D], xw_lo[:, c, w * D:(w + 1) * D],
                                               hi[:, c, :], lo[:, c, :], c == 0, c == CB - 1)
                        mm.then_inc(proj_ok, 1)

                def energies(i):
                    if i >= 2:
                        pe.wait_ge(eexp_ok, b * TB + i - 1)
                    a = slice(i * P, (i + 1) * P)
                    for c in range(HALVES):
                        n = slice(c * BANK, (c + 1) * BANK)
                        mm = split_product(ps_e[i % 2][:, n], qk[:, 0, a], qk[:, 1, a], qk[:, 2, n], qk[:, 3, n], True, True)
                    mm.then_inc(e_ok, 1)

                def turn_attention(i):
                    pe.wait_ge(enorm_ok, b * TB + i + 1)
                    pe.wait_ge(et_lo, b * TB + i)
                    pe.wait_ge(t3_read, b * TB)
                    for k in range(TB):
                        mm = pe.transpose(ps_t2[:, k * P:(k + 1) * P], work[:, i % 2, k * P:(k + 1) * P], ident[:, :])
                    mm.then_inc(et_ok, 1)

                pe.wait_ge(proj_lo, (b + 1) * 4)
                pe.wait_ge(x1_ok, b * TB)
                pe.wait_ge(x2_ok, b * TB)
                energies(0)
                for i in range(TB):
                    if i + 1 < TB:
                        energies(i + 1)
                    turn_attention(i)
                pe.wait_ge(et_lo, b * TB + TB)

                def project(i, c):
                    pe.wait_ge(ot_lo, b * TB + i + 1)
                    if c == 0:
                        pe.wait_ge(x1_ok, b * TB + i)
                    n = slice(c * BANK, (c + 1) * BANK)
                    for k in range(HB):
                        a = slice(k * P, (k + 1) * P)
                        mm = split_product(ps_a[:, n], split[:, 0, a], split[:, 1, a], wo_hi[:, k, n], wo_lo[:, k, n], k == 0, k == HB - 1)
                    if c == HALVES - 1:
                        mm.then_inc(wo_ok, 1)

                def turn(which, i):
                    g = b * TB + i
                    pe.wait_ge(ln_ok, b * 2 * TB + LN[which, i] + 1)
                    if which == 2:
                        if i >= 2:
                            pe.wait_ge(t3_read, g - 1)
                    else:
                        if i + 1 < TB:
                            pe.wait_ge(t2_lo, g + 2)
                        else:
                            pe.wait_ge(t3_read, g)
                    for k in range(HB):
                        mm = pe.transpose(ps_t2[:, k * P:(k + 1) * P], work[:, which - 2, k * P:(k + 1) * P], ident[:, :])
                    mm.then_inc(t2_ok if which == 2 else t3_ok, 1)

                def mix(i):
                    g = b * TB + i
                    pe.wait_ge(t2_lo, g + 1)
                    pe.wait_ge(x2_ok, g)
                    for c in range(HALVES):
                        n = slice(c * BANK, (c + 1) * BANK)
                        for k in range(TB):
                            a = slice(k * P, (k + 1) * P)
                            mm = split_product(ps_b[:, n], split[:, 2, a], split[:, 3, a], at_hi[:, k, n], at_lo[:, k, n], k == 0, k == TB - 1)
                    mm.then_inc(xm_ok, 1)

                def route_logits(i):
                    g = b * TB + i
                    pe.wait_ge(t3_read, g + 1)
                    pe.wait_ge(r_read, g)
                    for k in range(HB):
                        mm = pe.matmul(ps_r[:, 0, 0:E], x3_t[:, k, :], gate_sb[:, k, :], start=(k == 0), stop=(k == HB - 1))
                    mm.then_inc(r_ok, 1)

                project(0, 0)
                project(0, 1)
                for i in range(TB):
                    if i + 1 < TB:
                        project(i + 1, 0)
                    turn(2, i)
                    if i + 1 < TB:
                        project(i + 1, 1)
                    mix(i)
                    if i >= 1:
                        turn(3, i - 1)
                        route_logits(i - 1)
                turn(3, TB - 1)
                route_logits(TB - 1)

        @block.scalar
        def _(act):
            for k in range(HB + 1):
                act.wait_ge(w_in[k % 2], (k // 2) * 16 + 16)
                dst = wo_hi[:, k, :] if k < HB else xw_hi[:, :, :].rearrange("p c d -> p (c d)")
                act.activation(dst, stage[:, k % 2, :], ACT.Copy).then_inc(w_hi_ok, 1)
            act.wait_ge(small_in, 32)
            with act.Fori(0, B) as b:
                for n in range(2):
                    act.wait_ge(ctx_in, (b * 2 + n + 1) * 16)
                    act.wait_ge(proj_ok, (b * 2 + n) * 2)
                    if n == 0:
                        act.wait_ge(xm_ok, b * TB)
                    src = stage[:, :, :].rearrange("p a (c n) -> p (a c) n", n=BANK)
                    hi = split[:, 0:2, :].rearrange("p a (c n) -> p (a c) n", n=BANK)
                    for c in range(CB):
                        act.activation(hi[:, c, :], src[:, c, :], ACT.Copy).then_inc(ctx_hi, 1)
                    for w in range(2):
                        act.wait_ge(proj_ok, (b * 2 + n) * 2 + w + 1)
                        act.activation(qk[:, 2 * w, n * BANK:(n + 1) * BANK], ps_r[:, w, :], ACT.Identity,
                                       bias=bias[:, w:w + 1]).then_inc(proj_hi, 1)

                def exps(i):
                    act.wait_ge(emax_ok, b * TB + i + 1)
                    if i >= 2:
                        act.wait_ge(et_ok, b * TB + i - 1)
                    else:
                        act.wait_ge(t3_ok, b * TB)
                        act.wait_ge(x3_out, b * TB * 16)
                    act.activation(work[:, i % 2, :], ps_e[i % 2][:, :], ACT.Exp, bias=small[:, i, 0:1],
                                   accum_out=small[:, i, 1:2]).then_inc(eexp_ok, 1)

                def split_attention(i):
                    act.wait_ge(et_ok, b * TB + i + 1)
                    act.activation(at_hi[:, :, i * P:(i + 1) * P], ps_t2[:, :].rearrange("p (k c) -> p k c", c=P),
                                   ACT.Copy).then_inc(et_hi, 1)

                exps(0)
                for i in range(TB):
                    if i + 1 < TB:
                        exps(i + 1)
                    split_attention(i)

                def split_attn_out(i):
                    g = b * TB + i
                    act.wait_ge(ot_in[i % 2], (b * (TB // 2) + i // 2) * 16 + 16)
                    act.wait_ge(wo_ok, g)
                    if i == 0:
                        act.wait_ge(proj_ok, (b + 1) * 4)
                    act.activation(split[:, 0, :], stage[:, i % 2, :], ACT.Copy).then_inc(ot_hi, 1)

                def split_ln2(i):
                    g = b * TB + i
                    act.wait_ge(t2_ok, g + 1)
                    act.wait_ge(xm_ok, g)
                    act.activation(split[:, 2, :], ps_t2[:, :], ACT.Copy).then_inc(t2_hi, 1)

                def copy_ln3(i):
                    g = b * TB + i
                    act.wait_ge(t3_ok, g + 1)
                    act.wait_ge(r_ok, g)
                    act.activation(x3_t[:, :, :].rearrange("p k c -> p (k c)"), ps_t2[:, :], ACT.Copy).then_inc(t3_read, 1)

                def copy_logits(i):
                    g = b * TB + i
                    act.wait_ge(r_ok, g + 1)
                    act.activation(logits[:, bass.ds(g, 1), :].rearrange("p a e -> p (a e)"), ps_r[:, 0, 0:E], ACT.Copy).then_inc(r_read, 1)

                split_attn_out(0)
                split_attn_out(1)
                for i in range(TB):
                    split_ln2(i)
                    if i + 2 < TB:
                        split_attn_out(i + 2)
                    if i >= 1:
                        copy_ln3(i - 1)
                        copy_logits(i - 1)
                copy_ln3(TB - 1)
                copy_logits(TB - 1)

        @block.vector
        def _(dve):
            for k in range(HB + 1):
                dve.wait_ge(w_hi_ok, k + 1)
                dst, hi = (wo_lo[:, k, :], wo_hi[:, k, :]) if k < HB else (t[:, :, :].rearrange("p c d -> p (c d)") for t in (xw_lo, xw_hi))
                dve.tensor_tensor(dst, stage[:, k % 2, :], raw(hi), ALU.subtract).then_inc(w_lo_ok, 1)
            dve.wait_ge(small_in, 32)
            with dve.Fori(0, B) as b:
                for n in range(2):
                    src = stage[:, :, :].rearrange("p a (c n) -> p (a c) n", n=BANK)
                    hi = split[:, 0:2, :].rearrange("p a (c n) -> p (a c) n", n=BANK)
                    lo = split[:, 2:4, :].rearrange("p a (c n) -> p (a c) n", n=BANK)
                    for c in range(CB):
                        dve.wait_ge(ctx_hi, (b * 2 + n) * CB + c + 1)
                        dve.tensor_tensor(lo[:, c, :], src[:, c, :], raw(hi[:, c, :]), ALU.subtract).then_inc(ctx_lo, 1)
                    for w in range(2):
                        dve.wait_ge(proj_hi, (b * 2 + n) * 2 + w + 1)
                        a = slice(n * BANK, (n + 1) * BANK)
                        dve.scalar_tensor_tensor(out=qk[:, 2 * w + 1, a], in0=ps_r[:, w, :], scalar=bias[:, w:w + 1],
                                                 in1=raw(qk[:, 2 * w, a]), op0=ALU.add, op1=ALU.subtract).then_inc(proj_lo, 1)

                def maxima(i):
                    dve.wait_ge(e_ok, b * TB + i + 1)
                    dve.tensor_reduce(small[:, i, 0:1], ps_e[i % 2][:, :], AX.X, ALU.max, negate=True).then_inc(emax_ok, 1)

                def normalise_rows(i):
                    dve.wait_ge(eexp_ok, b * TB + i + 1)
                    dve.reciprocal(small[:, i, 2:3], small[:, i, 1:2]).then_inc(einv_ok, 1)
                    dve.wait_ge(einv_ok, b * TB + i + 1)
                    dve.tensor_scalar(work[:, i % 2, :], work[:, i % 2, :], small[:, i, 2:3], None, ALU.mult).then_inc(enorm_ok, 1)

                def rest_of_attention(i):
                    dve.wait_ge(et_hi, b * TB + i + 1)
                    a = slice(i * P, (i + 1) * P)
                    dve.tensor_tensor(at_lo[:, :, a], ps_t2[:, :].rearrange("p (k c) -> p k c", c=P), raw(at_hi[:, :, a]),
                                      ALU.subtract).then_inc(et_lo, 1)

                maxima(0)
                for i in range(TB):
                    if i + 1 < TB:
                        maxima(i + 1)
                    normalise_rows(i)
                    if i >= 1:
                        rest_of_attention(i - 1)
                rest_of_attention(TB - 1)

                def rest_of_attn_out(i):
                    dve.wait_ge(ot_hi, b * TB + i + 1)
                    dve.tensor_tensor(split[:, 1, :], stage[:, i % 2, :], raw(split[:, 0, :]), ALU.subtract).then_inc(ot_lo, 1)

                def layer_norm(which, i):
                    n = b * 2 * TB + LN[which, i]
                    s = which - 2
                    for c in range(HALVES):
                        dve.bn_stats(stats[:, s, c, :], res[:, i % 2, c * BANK:(c + 1) * BANK]).then_inc(ln_step, 1)
                    dve.wait_ge(ln_step, n * 3 + 2)
                    stand_alone(dve, passed)
                    dve.bn_aggr(mean_var[:, s, :], stats[:, s, :, :].rearrange("p a s -> p (a s)")).then_inc(ln_step, 1)
                    dve.wait_ge(ln_rstd, n + 1)
                    if which == 2 and i >= 1:
                        dve.wait_ge(t2_ok, b * TB + i)
                    if which == 3 and i >= 1:
                        dve.wait_ge(t3_ok, b * TB + i)
                        dve.wait_ge(x3_out, (b * TB + i) * 16)
                    dve.tensor_scalar(work[:, s, :], res[:, i % 2, :], mean_var[:, s, 0:1], rstd[:, s:s + 1],
                                      ALU.subtract, ALU.mult).then_inc(ln_ok, 1)

                def add_projection(i):
                    dve.wait_ge(wo_ok, b * TB + i + 1)
                    dve.wait_ge(res_in[i % 2], (b * (TB // 2) + i // 2) * 16 + 16)
                    dve.tensor_tensor(res[:, i % 2, :], ps_a[:, :], res[:, i % 2, :], ALU.add).then_inc(x1_ok, 1)
                    dve.wait_ge(x1_ok, b * TB + i + 1)
                    layer_norm(2, i)

                def rest_of_ln2(i):
                    dve.wait_ge(t2_hi, b * TB + i + 1)
                    dve.tensor_tensor(split[:, 3, :], ps_t2[:, :], raw(split[:, 2, :]), ALU.subtract).then_inc(t2_lo, 1)

                def add_mix(i):
                    dve.wait_ge(xm_ok, b * TB + i + 1)
                    dve.tensor_tensor(res[:, i % 2, :], ps_b[:, :], res[:, i % 2, :], ALU.add).then_inc(x2_ok, 1)
                    dve.wait_ge(x2_ok, b * TB + i + 1)
                    layer_norm(3, i)

                rest_of_attn_out(0)
                add_projection(0)
                rest_of_attn_out(1)
                for i in range(TB):
                    rest_of_ln2(i)
                    if i + 1 < TB:
                        add_projection(i + 1)
                    if i + 2 < TB:
                        rest_of_attn_out(i + 2)
                    add_mix(i)


def route(nc, const, logits, lo16, hi16, starts, similarity, rows):
    ident, passed = const[0], const[-1]
    N = B * TB
    G = BANK // P
    R = BANK // E
    with ExitStack() as scope:
        m = Memory(nc, scope)
        top = m.sb("top_values", [P, N, TOPK])
        top_i = m.sb("top_index", [P, N, TOPK], U32)
        top_f = m.sb("top_index_f", [P, N, TOPK])
        rest = m.sb("rest", [P, N, E])
        prob = m.sb("prob", [P, N, E])
        first = m.sb("first", [P, N, E])
        hit = m.sb("hit", [P, N, E])
        sums = m.sb("sums", [P, 4, N])
        iota_e = m.sb("iota_e", [P, E])
        place = m.sb("place", [E, 1])
        picked = m.sb("picked", [P, 2, E], BF16)
        ones16 = m.sb("ones16", [P, P], BF16)
        before16 = m.sb("before16", [P, P], BF16)
        sim = m.sb("sim_sb", [E, E])
        cand = m.sb("cand", [E, E])
        is_first = m.sb("is_first", [E, E], I32)
        best = m.sb("best", [E, TOPK])
        best_i = m.sb("best_i", [E, TOPK], U32)
        s1 = m.sb("route_small", [E, 8])
        remap = m.sb("remap", [E, E])
        weight_t = m.sb("weight_t", [E, 2, BANK])
        weight = m.sb("weight", [P, N, E])
        routed16 = m.sb("routed16", [P, N, E], BF16)
        so_far16 = m.sb("so_far16", [P, N + 1, E], BF16)
        rank = m.sb("rank", [P, E, N], I32)
        part = m.sb("part", [P, E, N], I32)
        count = m.sb("count", [P, E], I32)
        blocks = m.sb("blocks", [P, E])
        ends = m.sb("ends", [P, E])
        zeros = m.sb("zeros", [P, E])
        ps_n = m.ps("ps_n", [P, BANK])
        ps_w = m.ps("ps_w", [P, 2, BANK])
        ps_x = m.ps("ps_x", [P, 2, BANK])
        ps_k = m.ps("ps_k", [P, 2, BANK])

        made, sim_in, sim_ok = m.sem("route_made"), m.sem("sim_in"), m.sem("sim_ok")
        step = m.sem("route_step")
        z_ok, exp_ok, picked_ok, votes_ok = (m.sem(n) for n in ("z_ok", "p_exp_ok", "picked_ok", "votes_ok"))
        remap_ok, wt_ok, wt_read, w2_ok, w2_read = (m.sem(n) for n in ("remap_ok", "wt_ok", "wt_read", "w2_ok", "w2_read"))
        w_out, routed_ok, rank_ok, rank_read = (m.sem(n) for n in ("w_out", "routed_ok", "rank_ok", "rank_read"))
        block = scope.enter_context(nc.Block())

        @block.gpsimd
        def _(pool):
            pool.iota(iota_e[:, :], [[1, E]], base=0, channel_multiplier=0, allow_small_or_imprecise_dtypes=True).then_inc(made, 1)
            pool.iota(place[:, :], [[1, 1]], base=0, channel_multiplier=1, allow_small_or_imprecise_dtypes=True).then_inc(made, 1)
            pool.memset(ones16[:, :], 1.0).then_inc(made, 1)
            pool.memset(before16[:, :], 1.0).then_inc(made, 1)
            pool.memset(cand[:, :], -3e38).then_inc(made, 1)
            pool.memset(so_far16[:, 0, :], 0.0).then_inc(made, 1)
            pool.memset(zeros[:, :], 0.0).then_inc(made, 1)
            pool.memset(starts[:, 0:1], 0).then_inc(made, 1)
            pool.memset(lo16[:, E:, :], 0.0).then_inc(made, 1)
            pool.memset(hi16[:, E:, :], 0.0).then_inc(made, 1)
            pool.wait_ge(made, 10)
            pool.affine_select(out=before16[:, :], in_=before16[:, :], compare_op=ALU.is_gt, fill=0.0,
                               base=0, pattern=[[1, P]], channel_multiplier=-1).then_inc(made, 1)
            pool.wait_ge(sim_in, 16)
            pool.affine_select(out=sim[:, :], in_=sim[:, :], compare_op=ALU.not_equal, fill=1.0,
                               base=0, pattern=[[-1, E]], channel_multiplier=1).then_inc(sim_ok, 1)

        @block.sync
        def _(sp):
            sp.dma_start(sim[:, :], similarity).then_inc(sim_in, 16)
            sp.wait_ge(w2_read, N // G)
            sp.dma_start(rows[P:P + N * P, H:H + E].rearrange("(n p) e -> p n e", p=P), weight[:, :, :]).then_inc(w_out, 16)
            sp.wait_ge(w_out, 16)

        @block.scalar
        def _(act):
            act.wait_ge(z_ok, 1)
            act.activation(prob[:, :, :], prob[:, :, :], ACT.Exp).then_inc(exp_ok, 1)
            for g in range(N // G):
                act.wait_ge(wt_ok, g + 1)
                if g >= 2:
                    act.wait_ge(w2_ok, g - 1)
                act.activation(weight_t[:, g % 2, :], ps_w[0:E, g % 2, :], ACT.Copy).then_inc(wt_read, 1)

        @block.tensor
        def _(pe):
            pe.wait_ge(made, 11)
            pe.wait_ge(picked_ok, 1)
            pe.matmul(ps_n[0:E, 0:E], ones16[:, 0:E], picked[:, 0, :], start=True, stop=True)
            pe.matmul(ps_n[0:E, E:E + 1], picked[:, 0, :], ones16[:, 0:1], start=True, stop=True)
            pe.matmul(ps_n[0:E, E + 1:E + 2], picked[:, 1, :], ones16[:, 0:1], start=True, stop=True).then_inc(votes_ok, 1)
            pe.wait_ge(remap_ok, 1)

            def remapped(g):
                pe.wait_ge(wt_read, g + 1)
                if g >= 2:
                    pe.wait_ge(w2_read, g - 1)
                for i in range(G):
                    mm = pe.matmul(ps_x[:, g % 2, i * E:(i + 1) * E], weight_t[:, g % 2, i * P:(i + 1) * P], remap[:, :],
                                   start=True, stop=True)
                mm.then_inc(w2_ok, 1)

            for g in range(N // G):
                if g >= 2:
                    pe.wait_ge(wt_read, g - 1)
                for i in range(G):
                    mm = pe.transpose(ps_w[0:E, g % 2, i * P:(i + 1) * P], prob[:, g * G + i, :], ident[:, :])
                mm.then_inc(wt_ok, 1)
                if g >= 1:
                    remapped(g - 1)
            remapped(N // G - 1)
            pe.wait_ge(routed_ok, 1)
            for r in range(N // R):
                if r >= 2:
                    pe.wait_ge(rank_read, r - 1)
                a = slice(r * R, (r + 1) * R)
                pe.matmul(ps_k[:, r % 2, :], before16[:, :], routed16[:, a, :].rearrange("p n e -> p (n e)"), start=True, stop=False)
                pe.matmul(ps_k[:, r % 2, :], ones16[:, :], so_far16[:, a, :].rearrange("p n e -> p (n e)"),
                          start=False, stop=True).then_inc(rank_ok, 1)
            pe.matmul(ps_n[:, 0:E], ones16[:, :], so_far16[:, N, :], start=True, stop=True).then_inc(rank_ok, 1)

        @block.vector
        def _(dve):
            done = [0]

            def after(ins):
                done[0] += 1
                ins.then_inc(step, 1)
                dve.wait_ge(step, done[0])

            def each(ap, n):
                return ap.unsqueeze(2).broadcast_to([P, N, n])

            for n in range(N):
                ins = dve.max(top[:, n, :], logits[:, n, :])
            after(ins)
            dve.tensor_tensor(prob[:, :, :], logits[:, :, :], each(top[:, :, 0], E), ALU.subtract).then_inc(z_ok, 1)
            for n in range(N):
                dve.max_index(top_i[:, n, :], top[:, n, :], logits[:, n, :])
                ins = dve.match_replace(rest[:, n, :], top[:, n, :], logits[:, n, :], -3e38)
            after(ins)
            dve.tensor_copy(top_f[:, :, :], top_i[:, :, :])
            after(dve.tensor_tensor(rest[:, :, :], rest[:, :, :], logits[:, :, :], ALU.not_equal))
            dve.wait_ge(exp_ok, 1)
            after(dve.tensor_reduce(sums[:, 0, :], prob[:, :, :], AX.X, ALU.add))
            after(dve.reciprocal(sums[:, 1, :], sums[:, 0, :]))
            after(dve.tensor_tensor(prob[:, :, :], prob[:, :, :], each(sums[:, 1, :], E), ALU.mult))
            after(dve.tensor_tensor(prob[:, :, :], prob[:, :, :], rest[:, :, :], ALU.mult))
            after(dve.tensor_reduce(sums[:, 2, :], prob[:, :, :], AX.X, ALU.add))
            after(dve.tensor_scalar(sums[:, 2, :], sums[:, 2, :], 1e-12, None, ALU.max))
            after(dve.reciprocal(sums[:, 3, :], sums[:, 2, :]))
            after(dve.tensor_tensor(prob[:, :, :], prob[:, :, :], each(sums[:, 3, :], E), ALU.mult))
            dve.wait_ge(made, 11)
            experts = iota_e[:, :].unsqueeze(1).broadcast_to([P, N, E])
            after(dve.tensor_tensor(first[:, :, :], experts, each(top_f[:, :, 0], E), ALU.is_equal))
            for k in range(1, SELK):
                after(dve.tensor_tensor(hit[:, :, :], experts, each(top_f[:, :, k], E), ALU.is_equal))
                after(dve.tensor_tensor(first[:, :, :], first[:, :, :], hit[:, :, :], ALU.add))
            after(dve.tensor_tensor(hit[:, :, :], rest[:, :, :], first[:, :, :], ALU.subtract))
            with nc.allow_low_precision(reason="counts up to 32 are exact in bfloat16"):
                dve.tensor_reduce(picked[:, 0, :], first[:, :, :].rearrange("p n e -> p e n"), AX.X, ALU.add)
                dve.tensor_reduce(picked[:, 1, :], hit[:, :, :].rearrange("p n e -> p e n"), AX.X, ALU.add).then_inc(picked_ok, 1)
            dve.wait_ge(votes_ok, 1)
            dve.wait_ge(sim_ok, 1)
            after(dve.tensor_scalar(is_first[:, :], ps_n[0:E, 0:E], 0.5, None, ALU.is_ge))
            after(dve.copy_predicated(cand[:, :], is_first[:, :], sim[:, :]))
            after(dve.max(best[:, :], cand[:, :]))
            after(dve.max_index(best_i[:, :], best[:, :], cand[:, :]))
            dve.tensor_copy(s1[:, 0:1], best_i[:, 0:1])
            dve.tensor_scalar(s1[:, 1:2], ps_n[0:E, E:E + 1], 0.5, None, ALU.is_lt)
            dve.tensor_scalar(s1[:, 2:3], ps_n[0:E, E + 1:E + 2], 0.5, None, ALU.is_ge)
            after(dve.tensor_scalar(s1[:, 3:4], best[:, 0:1], 0.5, None, ALU.is_ge))
            dve.tensor_tensor(s1[:, 4:5], s1[:, 0:1], place[:, :], ALU.subtract)
            after(dve.tensor_tensor(s1[:, 5:6], s1[:, 1:2], s1[:, 2:3], ALU.mult))
            after(dve.tensor_tensor(s1[:, 5:6], s1[:, 5:6], s1[:, 3:4], ALU.mult))
            after(dve.tensor_tensor(s1[:, 4:5], s1[:, 4:5], s1[:, 5:6], ALU.mult))
            after(dve.tensor_tensor(s1[:, 6:7], s1[:, 4:5], place[:, :], ALU.add))
            dve.tensor_scalar(remap[:, :], iota_e[0:E, :], s1[:, 6:7], None, ALU.is_equal).then_inc(remap_ok, 1)
            for g in range(N // G):
                dve.wait_ge(w2_ok, g + 1)
                dve.tensor_copy(weight[:, g * G:(g + 1) * G, :],
                                ps_x[:, g % 2, 0:G * E].rearrange("p (n e) -> p n e", e=E)).then_inc(w2_read, 1)
            dve.wait_ge(w2_read, N // G)
            after(dve.tensor_scalar(routed16[:, :, :], weight[:, :, :], 0.0, None, ALU.is_gt))
            for n in range(N):
                ins = dve.tensor_tensor(so_far16[:, n + 1, :], so_far16[:, n, :], routed16[:, n, :], ALU.add)
                if n < N - 1:
                    after(ins)
            ins.then_inc(routed_ok, 1)
            for r in range(N // R):
                dve.wait_ge(rank_ok, r + 1)
                dve.tensor_copy(rank[:, :, r * R:(r + 1) * R],
                                ps_k[:, r % 2, :].rearrange("p (n e) -> p e n", e=E)).then_inc(rank_read, 1)
            dve.wait_ge(rank_ok, N // R + 1)
            after(dve.tensor_copy(count[:, :], ps_n[:, 0:E]))
            dve.wait_ge(rank_read, N // R)
            after(dve.tensor_scalar(part[:, :, :], rank[:, :, :], 7, None, ALU.arith_shift_right))
            dve.tensor_copy(hi16[:, 0:E, :], part[:, :, :])
            after(dve.tensor_scalar(count[:, :], count[:, :], P - 1, None, ALU.add))
            after(dve.tensor_scalar(part[:, :, :], rank[:, :, :], P - 1, None, ALU.bitwise_and))
            dve.scalar_tensor_tensor(out=lo16[:, 0:E, :], in0=part[:, :, :], scalar=1.0,
                                     in1=routed16[:, :, :].rearrange("p n e -> p e n"), op0=ALU.add, op1=ALU.mult)
            after(dve.tensor_scalar(count[:, :], count[:, :], 7, None, ALU.arith_shift_right))
            after(dve.tensor_scalar(blocks[:, :], count[:, :], 1.0, None, ALU.max))
            after(dve.tensor_tensor_scan(ends[:, :], zeros[:, :], blocks[:, :], 0.0, ALU.add, ALU.add))
            dve.tensor_copy(starts[:, 1:E + 1], ends[:, :])
            after(dve.tensor_copy(starts[:, E + 1:], ends[:, E - 1:E].broadcast_to([P, AHEAD])))


AHEAD = 3


def experts(nc, const, lo16, hi16, starts, w_gu, w_down, rows, out):
    ident, passed = const[0], const[-1]
    N = B * TB
    W = 2 * P
    PIECES = [("gu", f, q) for f in range(FB) for q in range(4)] + [("dn", f, q) for f in range(FB) for q in range(2)]
    NPC = len(PIECES)
    CHUNKS = 2 * FB
    with ExitStack() as scope:
        m = Memory(nc, scope)
        gu_raw = m.sb("gu_raw", [P, FB, HB * W])
        dn_raw = m.sb("dn_raw", [P, FB, H])
        gu_hi = m.sb("gu_hi", [P, FB, HB * W], F32R)
        gu_lo = m.sb("gu_lo", [P, FB, HB * W], F32R)
        dn_hi = m.sb("dn_hi", [P, FB, H], F32R)
        dn_lo = m.sb("dn_lo", [P, FB, H], F32R)
        x_rows = m.sb("x_rows", [P, H + E])
        xe_hi = m.sb("xe_hi", [P, H], F32R)
        xe_lo = m.sb("xe_lo", [P, H], F32R)
        silu = m.sb("silu", [P, FB, P])
        act_h = m.sb("act_h", [P, FB, P])
        ht_hi = m.sb("ht_hi", [P, FB, P], F32R)
        ht_lo = m.sb("ht_lo", [P, FB, P], F32R)
        y_out = m.sb("y_out", [P, H])
        w_next = m.sb("w_next", [P, E])
        w_now = m.sb("w_now", [P, 1])
        gather_i = m.sb("gather_i", [P, 1], I32)
        scatter_i = m.sb("scatter_i", [P, 1], I32)
        table = m.sb("table", [P, 1 + N * TOPK + E + N], I32)
        own = m.sb("own", [P, 1])
        iota_lo = m.sb("iota_lo", [P, P], BF16)
        iota_hi = m.sb("iota_hi", [P, N], BF16)
        row_base = m.sb("row_base", [P, N, N], BF16)
        at_lo = m.sb("at_lo16", [P, N, P], BF16)
        at_hi = m.sb("at_hi16", [P, N, 2, N], BF16)
        found = m.sb("found", [P, 2, N])
        ps_gu = m.ps("ps_gu", [P, 2, BANK])
        ps_x1 = m.ps("ps_xe", [P, H])
        ps_y = m.ps("ps_y", [P, H])
        ps_h = m.ps("ps_h", [P, BANK])
        ps_l = m.ps("ps_l", [P, BANK])

        raw_in = [m.sem(f"raw_in{c}") for c in range(CHUNKS)]
        hi_ok, lo_ok = m.sem("we_hi_ok"), m.sem("we_lo_ok")
        set_up = m.sem("set_up")
        mask_ok, list_a, list_ps, list_id, found_ok, list_ok = (
            m.sem(n) for n in ("mask_ok", "list_a", "list_ps", "list_id", "found_ok", "list_ok"))
        gidx_ok, rows_in, xe_ps, xe_hi_ok, xe_lo_ok, wn_ok = (m.sem(n) for n in ("gidx_ok", "rows_in", "xe_ps", "xe_hi_ok", "xe_lo_ok", "wn_ok"))
        gu_ok, silu_ok, h_ok, h_ps, ht_hi_ok, ht_lo_ok = (m.sem(n) for n in ("gu_ok", "silu_ok", "h_ok", "h_ps", "ht_hi_ok", "ht_lo_ok"))
        dn_ok, sidx_ok, y_ok, y_sent = (m.sem(n) for n in ("dn_ok", "sidx_ok", "y_ok", "y_sent"))
        wnow_ok = m.sem("wnow_ok")

        def start_of(eng, e):
            return eng.value_load(starts[0:1, bass.ds(e, 1)], min_val=0, max_val=N * TOPK + E)

        def for_blocks(eng, body):
            with eng.Fori(0, E) as e:
                g0 = start_of(eng, e)
                g1 = start_of(eng, e + 1)
                body(e, g0, True)
                with eng.If(g1 - g0 > 1):
                    with eng.Fori(g0 + 1, g1) as g:
                        body(e, g, False)

        block = scope.enter_context(nc.Block())

        @block.sync
        def _(sp):
            def load(e, c):
                if c < FB:
                    sp.dma_start(gu_raw[:, c, :].rearrange("p (k c) -> p k c", c=W),
                                 w_gu[e, c].rearrange("(k p) c -> p k c", p=P)).then_inc(raw_in[c], 16)
                else:
                    sp.dma_start(dn_raw[:, c - FB, :], w_down[e, (c - FB) * P:(c - FB + 1) * P, :]).then_inc(raw_in[c], 16)

            for c in range(CHUNKS):
                load(0, c)
            with sp.Fori(1, E) as e:
                for c in range(CHUNKS):
                    split = 4 * (c + 1) if c < FB else 4 * FB + 2 * (c - FB + 1)
                    sp.wait_ge(lo_ok, (e - 1) * NPC + split)
                    load(e, c)

        @block.gpsimd
        def _(pool):
            pool.iota(own[:, :], [[1, 1]], base=0, channel_multiplier=1, allow_small_or_imprecise_dtypes=True).then_inc(set_up, 1)
            pool.iota(iota_lo[:, :], [[1, P]], base=1, channel_multiplier=0, allow_small_or_imprecise_dtypes=True).then_inc(set_up, 1)
            pool.iota(iota_hi[:, :], [[1, N]], base=0, channel_multiplier=0, allow_small_or_imprecise_dtypes=True).then_inc(set_up, 1)
            pool.iota(row_base[:, :, :], [[P, N], [0, N]], base=P, channel_multiplier=0, allow_small_or_imprecise_dtypes=True).then_inc(set_up, 1)
            pool.iota(table[:, :], [[0, table.shape[1]]], base=0, channel_multiplier=1).then_inc(set_up, 1)
            pool.iota(scatter_i[:, :], [[0, 1]], base=0, channel_multiplier=1).then_inc(set_up, 1)

            def gather(n):
                pool.wait_ge(gidx_ok, n + 1)
                if not (isinstance(n, int) and n == 0):
                    pool.wait_ge(wn_ok, n)
                stand_alone(pool, passed)
                pool.indirect_dma_start(x_rows[:, :], None, rows, bass.IndirectOffsetOnAxis(ap=gather_i[:, 0:1], axis=0)).then_inc(rows_in, 16)

            gather(0)
            gather(1)

            def body(e, g, first):
                pool.wait_ge(y_ok, g + 1)
                pool.wait_ge(sidx_ok, g + 1)
                stand_alone(pool, passed)
                pool.indirect_dma_start(out, bass.IndirectOffsetOnAxis(ap=scatter_i[:, 0:1], axis=0), y_out[:, :], None,
                                        compute_op=ALU.add).then_inc(y_sent, 16)
                gather(g + 2)

            for_blocks(pool, body)
            total = start_of(pool, E)
            pool.wait_ge(y_ok, total + 1)
            pool.wait_ge(sidx_ok, total + 1)
            stand_alone(pool, passed)
            pool.indirect_dma_start(out, bass.IndirectOffsetOnAxis(ap=scatter_i[:, 0:1], axis=0), y_out[:, :], None,
                                    compute_op=ALU.add).then_inc(y_sent, 16)
            pool.wait_ge(y_sent, (total + 1) * 16)
            pool.wait_ge(rows_in, (total + 2) * 16)

        @block.tensor
        def _(pe):
            def split_product(out, a_hi, a_lo, w_hi, w_lo, first, last):
                pe.matmul(out, a_hi, w_hi, start=first, stop=False)
                pe.matmul(out, a_hi, w_lo, start=False, stop=False)
                return pe.matmul(out, a_lo, w_hi, start=False, stop=last)

            def find_rows(n):
                pe.wait_ge(list_a, n + 1)
                pe.wait_ge(list_id, n)
                for i in range(N):
                    mm = pe.matmul(ps_l[:, 0:2 * N], at_lo[:, i, :], at_hi[:, i, :, :].rearrange("p a h -> p (a h)"),
                                   start=(i == 0), stop=(i == N - 1))
                mm.then_inc(list_ps, 1)

            def turn_rows(n):
                pe.wait_ge(rows_in, (n + 1) * 16)
                pe.wait_ge(xe_lo_ok, n * 2)
                for k in range(HB):
                    mm = pe.transpose(ps_x1[:, k * P:(k + 1) * P], x_rows[:, k * P:(k + 1) * P], ident[:, :])
                mm.then_inc(xe_ps, 1)

            for n in range(AHEAD):
                find_rows(n)
            turn_rows(0)
            pe.wait_ge(set_up, 8)
            for k in range(HB):
                mm = pe.transpose(ps_y[:, k * P:(k + 1) * P], y_out[:, k * P:(k + 1) * P], ident[:, :])
            mm.then_inc(dn_ok, 1)

            def body(e, g, first):
                def first_layer(f):
                    pe.wait_ge(xe_lo_ok, g * 2 + 2)
                    if f == 2:
                        pe.wait_ge(h_ok, g * FB + 1)
                    else:
                        pe.wait_ge(h_ok, g * FB)
                    gw = slice(0, W)
                    for k in range(HB):
                        if first and k % 2 == 0:
                            pe.wait_ge(lo_ok, e * NPC + 4 * f + k // 2 + 1)
                        a = slice(k * P, (k + 1) * P)
                        c = slice(k * W, (k + 1) * W)
                        mm = split_product(ps_gu[:, f % 2, gw], xe_hi[:, a], xe_lo[:, a], gu_hi[:, f, c], gu_lo[:, f, c], k == 0, k == HB - 1)
                    mm.then_inc(gu_ok, 1)

                def turn_h(f):
                    pe.wait_ge(h_ok, g * FB + f + 1)
                    pe.wait_ge(ht_lo_ok, g * FB + f)
                    pe.transpose(ps_h[:, f * P:(f + 1) * P], act_h[:, f, :], ident[:, :]).then_inc(h_ps, 1)

                def second_layer(f):
                    pe.wait_ge(ht_lo_ok, g * FB + f + 1)
                    if f == 0:
                        pe.wait_ge(y_ok, g + 1)
                    for c in range(H // BANK):
                        if first:
                            pe.wait_ge(lo_ok, e * NPC + 4 * FB + 2 * f + c + 1)
                        n = slice(c * BANK, (c + 1) * BANK)
                        mm = split_product(ps_y[:, n], ht_hi[:, f, :], ht_lo[:, f, :], dn_hi[:, f, n], dn_lo[:, f, n], f == 0, f == FB - 1)
                    if f == FB - 1:
                        mm.then_inc(dn_ok, 1)

                first_layer(0)
                first_layer(1)
                if first:
                    find_rows(e + AHEAD)
                turn_h(0)
                first_layer(2)
                turn_h(1)
                turn_rows(g + 1)
                turn_h(2)
                second_layer(0)
                second_layer(1)
                second_layer(2)

            for_blocks(pe, body)

        @block.scalar
        def _(act):
            def split_rows(n):
                act.wait_ge(xe_ps, n + 1)
                act.wait_ge(gu_ok, n * FB)
                for c in range(2):
                    a = slice(c * BANK, (c + 1) * BANK)
                    act.activation(xe_hi[:, a], ps_x1[:, a], ACT.Copy).then_inc(xe_hi_ok, 1)

            split_rows(0)

            def finish(n):
                act.wait_ge(dn_ok, n + 1)
                act.wait_ge(sidx_ok, n + 1)
                act.wait_ge(y_sent, n * 16)
                act.activation(y_out[:, :], ps_y[:, :], ACT.Copy, scale=w_now[:, 0:1]).then_inc(y_ok, 1)

            def body(e, g, first):
                def split(kind, f):
                    c = f if kind == "gu" else FB + f
                    act.wait_ge(raw_in[c], e * 16 + 16)
                    if kind == "gu":
                        act.wait_ge(gu_ok, g * FB)
                        for q in range(4):
                            a = slice(q * 2 * W, (q + 1) * 2 * W)
                            act.activation(gu_hi[:, f, a], gu_raw[:, f, a], ACT.Copy).then_inc(hi_ok, 1)
                    else:
                        act.wait_ge(dn_ok, g + 1)
                        for q in range(2):
                            a = slice(q * BANK, (q + 1) * BANK)
                            act.activation(dn_hi[:, f, a], dn_raw[:, f, a], ACT.Copy).then_inc(hi_ok, 1)

                def silu_of(f):
                    act.wait_ge(gu_ok, g * FB + f + 1)
                    act.wait_ge(h_ok, g * FB)
                    act.activation(silu[:, f, :], ps_gu[:, f % 2, 0:P], ACT.Silu).then_inc(silu_ok, 1)

                def split_h(f):
                    act.wait_ge(h_ps, g * FB + f + 1)
                    act.wait_ge(dn_ok, g + 1)
                    act.activation(ht_hi[:, f, :], ps_h[:, f * P:(f + 1) * P], ACT.Copy).then_inc(ht_hi_ok, 1)

                if first:
                    split("gu", 0)
                finish(g)
                if first:
                    split("gu", 1)
                silu_of(0)
                if first:
                    split("gu", 2)
                silu_of(1)
                split_h(0)
                if first:
                    split("dn", 0)
                silu_of(2)
                split_h(1)
                if first:
                    split("dn", 1)
                split_h(2)
                if first:
                    split("dn", 2)
                split_rows(g + 1)

            for_blocks(act, body)
            finish(start_of(act, E))

        @block.vector
        def _(dve):
            dve.memset(y_out[:, :], 0.0).then_inc(set_up, 1)
            dve.memset(w_next[:, :], 0.0).then_inc(set_up, 1)
            dve.memset(w_now[:, :], 0.0).then_inc(sidx_ok, 1)
            dve.wait_ge(set_up, 8)

            def make_list(n):
                dve.wait_ge(list_ps, n)
                lo = lo16[:, bass.ds(n, 1), :].rearrange("p a n -> p (a n)").unsqueeze(2)
                hi = hi16[:, bass.ds(n, 1), :].rearrange("p a n -> p (a n)").unsqueeze(2)
                dve.tensor_tensor(at_hi[:, :, 1, :], iota_hi[:, :].unsqueeze(1).broadcast_to([P, N, N]),
                                  hi.broadcast_to([P, N, N]), ALU.is_equal).then_inc(mask_ok, 1)
                dve.tensor_tensor(at_lo[:, :, :], iota_lo[:, :].unsqueeze(1).broadcast_to([P, N, P]),
                                  lo.broadcast_to([P, N, P]), ALU.is_equal)
                dve.wait_ge(mask_ok, n * 2 + 1)
                dve.tensor_scalar(at_hi[:, :, 0, :], at_hi[:, :, 1, :], own[:, 0:1], None, ALU.mult).then_inc(mask_ok, 1)
                dve.wait_ge(mask_ok, n * 2 + 2)
                dve.tensor_tensor(at_hi[:, :, 1, :], at_hi[:, :, 1, :], row_base[:, :, :], ALU.mult).then_inc(list_a, 1)

            def finish_list(n):
                dve.wait_ge(list_ps, n + 1)
                dve.tensor_reduce(found[:, 0, :], ps_l[:, 0:2 * N].rearrange("p (a h) -> p h a", a=2), AX.X, ALU.add).then_inc(list_id, 1)
                dve.wait_ge(list_id, n + 1)
                dve.tensor_scalar(found[:, 1, :], found[:, 0, :], 0.0, own[:, 0:1], ALU.is_equal, ALU.mult).then_inc(found_ok, 1)
                dve.wait_ge(found_ok, n + 1)
                at = start_of(dve, n)
                dve.tensor_tensor(table[:, bass.ds(at + 1, N)], found[:, 0, :], found[:, 1, :], ALU.add).then_inc(list_ok, 1)
                dve.wait_ge(list_ok, n + 1)

            def gather_index(n):
                if not (isinstance(n, int) and n == 0):
                    dve.wait_ge(rows_in, n * 16)
                dve.tensor_copy(gather_i[:, :], table[:, bass.ds(n + 1, 1)]).then_inc(gidx_ok, 1)

            def rest_of_rows(n):
                for c in range(2):
                    dve.wait_ge(xe_hi_ok, n * 2 + c + 1)
                    a = slice(c * BANK, (c + 1) * BANK)
                    dve.tensor_tensor(xe_lo[:, a], ps_x1[:, a], raw(xe_hi[:, a]), ALU.subtract).then_inc(xe_lo_ok, 1)

            def keep_weights(n):
                dve.wait_ge(xe_ps, n + 1)
                dve.tensor_copy(w_next[:, :], x_rows[:, H:H + E]).then_inc(wn_ok, 1)

            for n in range(AHEAD):
                make_list(n)
                finish_list(n)
            make_list(AHEAD)
            gather_index(0)
            keep_weights(0)
            gather_index(1)
            rest_of_rows(0)

            def body(e, g, first):
                def rest_of(kind, f):
                    n = 4 if kind == "gu" else 2
                    for q in range(n):
                        at = 4 * f + q if kind == "gu" else 4 * FB + 2 * f + q
                        dve.wait_ge(hi_ok, e * NPC + at + 1)
                        a = slice(q * BANK, (q + 1) * BANK)
                        lo, r, hi = ((gu_lo, gu_raw, gu_hi) if kind == "gu" else (dn_lo, dn_raw, dn_hi))
                        dve.tensor_tensor(lo[:, f, a], r[:, f, a], raw(hi[:, f, a]), ALU.subtract).then_inc(lo_ok, 1)

                def multiply(f):
                    dve.wait_ge(silu_ok, g * FB + f + 1)
                    dve.wait_ge(h_ps, g * FB)
                    dve.tensor_tensor(act_h[:, f, :], ps_gu[:, f % 2, P:W], silu[:, f, :], ALU.mult).then_inc(h_ok, 1)

                def rest_of_h(f):
                    dve.wait_ge(ht_hi_ok, g * FB + f + 1)
                    dve.tensor_tensor(ht_lo[:, f, :], ps_h[:, f * P:(f + 1) * P], raw(ht_hi[:, f, :]), ALU.subtract).then_inc(ht_lo_ok, 1)

                if first:
                    rest_of("gu", 0)
                if first:
                    rest_of("gu", 1)
                multiply(0)
                if first:
                    rest_of("gu", 2)
                multiply(1)
                rest_of_h(0)
                if first:
                    rest_of("dn", 0)
                multiply(2)
                rest_of_h(1)
                if first:
                    rest_of("dn", 1)
                rest_of_h(2)
                if first:
                    rest_of("dn", 2)
                dve.wait_ge(y_ok, g + 1)
                dve.wait_ge(wn_ok, g + 1)
                stand_alone(dve, passed)
                dve.tensor_copy(w_now[:, :], w_next[:, bass.ds(e, 1)]).then_inc(wnow_ok, 1)
                dve.wait_ge(wnow_ok, g + 1)
                keep_weights(g + 1)
                gather_index(g + 2)
                rest_of_rows(g + 1)
                dve.wait_ge(y_sent, (g + 1) * 16)
                dve.tensor_copy(scatter_i[:, :], table[:, bass.ds(g + 1, 1)]).then_inc(sidx_ok, 1)
                if first:
                    finish_list(e + AHEAD)
                    make_list(e + AHEAD + 1)

            for_blocks(dve, body)


def rope_tables():
    inv = 1.0 / 10000.0 ** (np.arange(0, HD, 2, dtype=np.float32) / HD)
    freqs = np.einsum("i,j->ij", np.arange(S, dtype=np.float32), inv)
    emb = np.concatenate((freqs, freqs), axis=-1)
    c, s = np.cos(emb).astype(np.float32), np.sin(emb).astype(np.float32)
    s[:, :HD // 2] *= -1
    scale = np.float32(HD ** -0.5)
    return (np.ascontiguousarray(np.stack([c * scale, c], 1)), np.ascontiguousarray(np.stack([s * scale, s], 1)))


def host_layout(i):
    i = {n: np.asarray(a) for n, a in i.items()}
    qkv = np.stack([i[f"L0_attn_W{n}"].T.reshape(H, NP, P) for n in "qkv"], 2)
    cos, sin = rope_tables()
    tidy = np.ascontiguousarray
    return {
        "x": i["x"],
        "wqkv": tidy(qkv.transpose(1, 0, 2, 3).reshape(NP, H, 3 * P)),
        "cos": cos, "sin": sin,
        "wo": tidy(i["L0_attn_Wo"].T),
        "ctx_t": tidy(i["ctx_1024"].transpose(0, 2, 1)),
        "xw": tidy(np.concatenate([i["L0_xattn_Wq"].T, i["L0_xattn_Wk"].T], 1)),
        "xbias": tidy(np.stack([i["L0_xattn_bq"], i["L0_xattn_bk"]], 1)),
        "gate": tidy(i["L0_ffn_gate_weight"].T),
        "similarity": i["L0_ffn_similarity"],
        "w_gu": tidy(i["L0_ffn_gate_up_proj"].reshape(E, 2, FB, P, H).transpose(0, 2, 4, 1, 3).reshape(E, FB, H, 2 * P)),
        "w_down": tidy(i["L0_ffn_down_proj"].transpose(0, 2, 1)),
    }


def build(nc, x, wqkv, cos, sin, wo, ctx_t, xw, xbias, gate, similarity, w_gu, w_down, out):
    attn_out = nc.dram_tensor("attn_out", (B, NP, P, S), F32, kind="Internal").ap()
    rows = nc.dram_tensor("rows", (P + B * S, H + E), F32, kind="Internal").ap()
    with ExitStack() as scope:
        m = Memory(nc, scope)
        const = constants(nc, m)
        self_attention(nc, const, x, wqkv, cos, sin, attn_out)
        logits = m.sb("logits", [P, B * TB, E])
        mix_features(nc, const, logits, x, attn_out, wo, ctx_t, xw, xbias, gate, rows, out)
        lo16 = m.sb("lo16", [P, E + AHEAD + 1, B * TB], BF16)
        hi16 = m.sb("hi16", [P, E + AHEAD + 1, B * TB], BF16)
        starts = m.sb("starts", [P, E + 1 + AHEAD], I32)
        route(nc, const, logits, lo16, hi16, starts, similarity, rows)
        experts(nc, const, lo16, hi16, starts, w_gu, w_down, rows, out)


def kernel(**inputs):
    import concourse.bacc as bacc
    from concourse.bass_utils import run_bass_kernel_spmd

    nc = bacc.Bacc("TRN2", target_bir_lowering=False, num_devices=1)
    arrays = host_layout(inputs)
    args = {n: nc.dram_tensor(n, a.shape, mybir.dt.from_np(a.dtype), kind="ExternalInput").ap() for n, a in arrays.items()}
    out = nc.dram_tensor("out", (P + B * S, H), F32, kind="ExternalOutput").ap()
    build(nc, **args, out=out)
    r = run_bass_kernel_spmd(nc, [arrays], core_ids=[0])
    return r.results[0]["out"][P:].reshape(B, S, H)
```

```python
from contextlib import ExitStack

import numpy as np
import concourse.bass as bass
from concourse import mybir

F32 = mybir.dt.float32
F32R = mybir.dt.float32r
BF16 = mybir.dt.bfloat16
I32 = mybir.dt.int32
U32 = mybir.dt.uint32
ALU = mybir.AluOpType
ACT = mybir.ActivationFunctionType
AX = mybir.AxisListType

P = 128
B, S, H = 4, 1024, 1024
NH, HD = 16, 64
HB = H // P
TB = S // P
NP = NH // 2
C, D = 512, 128
CB = C // P
E, TOPK, SELK, F = 64, 8, 4, 384
FB = F // P
BANK = 512
GQ = BANK // P
EPS = 1e-5
MASKED = -1e30


class Memory:

    def __init__(self, nc, scope):
        self.nc, self.scope = nc, scope

    def sb(self, name, shape, dt=F32):
        return self.scope.enter_context(self.nc.sbuf_tensor(name, shape, dt))

    def ps(self, name, shape, dt=F32):
        return self.scope.enter_context(self.nc.psum_tensor(name, shape, dt))

    def sem(self, name):
        return self.scope.enter_context(self.nc.semaphore(name))


def raw(ap):
    return ap.bitcast(F32)


def stand_alone(eng, passed):
    eng.sem_inc(passed, 1)


def constants(nc, m):
    ident = m.sb("ident", [P, P])
    ident16 = m.sb("ident16", [P, P], BF16)
    mask16 = m.sb("mask16", [P, P], BF16)
    half = m.sb("minus_half", [P, TB])
    made = m.sem("const_made")
    passed = m.sem("passed")
    with nc.Block() as block:
        @block.gpsimd
        def _(pool):
            pool.memset(ident[:, :], 0.0).then_inc(made, 1)
            pool.memset(ident16[:, :], 0.0).then_inc(made, 1)
            pool.memset(mask16[:, :], 0.0).then_inc(made, 1)
            pool.memset(half[:, :], -0.5).then_inc(made, 1)
            pool.wait_ge(made, 4)
            for t in (ident, ident16):
                pool.affine_select(out=t[:, :], in_=t[:, :], compare_op=ALU.not_equal, fill=1.0,
                                   base=0, pattern=[[-1, P]], channel_multiplier=1).then_inc(made, 1)
            pool.affine_select(out=mask16[:, :], in_=mask16[:, :], compare_op=ALU.is_ge, fill=MASKED,
                               base=0, pattern=[[-1, P]], channel_multiplier=1).then_inc(made, 1)
            pool.wait_ge(made, 7)
    return ident, ident16, mask16, half, passed


def self_attention(nc, const, x, wqkv, cos, sin, attn_out):
    ident, ident16, mask16, half, passed = const
    W = 3 * P
    UNITS = [(h, g) for h in range(2) for g in range(S // BANK)]
    NU = len(UNITS)
    KB = [GQ * (g + 1) for _, g in UNITS]
    STEPS = [(u, kb) for u in range(NU) for kb in range(KB[u])]
    NS = len(STEPS)
    PER = NS // TB
    NQ = GQ * NU
    PARTS = [range(i * 3 * HB // PER, (i + 1) * 3 * HB // PER) for i in range(PER)]
    SLOTS = 4
    W_OF_STEP = {NS - 2: (2, (0, 1)), NS - 1: (2, (2, 3)), 0: (1, (4, 5)), 1: (1, (6, 7))}
    XS = GQ
    NT = NS + TB

    def steps_from(u):
        return sum(KB[:u])

    def next_queries(s, last):
        u, kb = STEPS[s]
        if KB[u] == GQ:
            then = [(u + 1, kb + 1)] if kb + 1 < GQ else []
        else:
            then = [(u + 1, kb // 2)] if kb % 2 == 0 else [(u + 2, 0)] if kb == KB[u] - 1 else []
        return [(unit // NU, unit % NU, i) for unit, i in then if unit < NU or not last]

    def tile_order(last):
        order = []
        for s in range(NS):
            order.append(("probs", s))
            if s % PER == 1 and (s < PER or not last):
                order.append(("qk", s // PER))
        return {key: i for i, key in enumerate(order)}

    with ExitStack() as scope:
        m = Memory(nc, scope)
        stats = m.sb("ln1_stats", [P, TB, 2, 6])
        mean_var = m.sb("ln1_mean_var", [P, TB, 2])
        rstd = m.sb("ln1_rstd", [P, TB])
        xt_hi = m.sb("xt_hi", [P, HB, S], F32R)
        xt_lo = m.sb("xt_lo", [P, HB, S], F32R)
        w_raw = m.sb("w_raw", [P, SLOTS, W])
        w_hi = m.sb("w_hi", [P, HB, W], F32R)
        w_lo = m.sb("w_lo", [P, HB, W], F32R)
        cos_sb = m.sb("cos_sb", [P, TB, 2, HD // 2])
        sin_sb = m.sb("sin_sb", [P, TB, 2, HD])
        r_cos = m.sb("r_cos", [P, 4, HD])
        r_sin = m.sb("r_sin", [P, 4, HD])
        rotated = m.sb("rotated", [P, 4, 2, HD])
        qk_hi = [m.sb(f"qk_hi{i}", [P, 4, S], F32R) for i in range(2)]
        q_lo = [m.sb(f"q_lo{i}", [P, 2, S], F32R) for i in range(2)]
        v = [m.sb(f"v{i}", [P, TB, 2, 2, HD], F32R) for i in range(2)]
        neg_max = m.sb("neg_max", [P, NQ])
        row_sum = m.sb("row_sum", [P, NQ])
        inv_sum = m.sb("inv_sum", [P, NQ])
        probs = [m.sb(f"probs{g}", [P, GQ, BANK * (g + 1)]) for g in range(S // BANK)]
        x_tile = probs[1]
        pt_hi = m.sb("pt_hi", [P, 2, BANK], F32R)
        pt_lo = m.sb("pt_lo", [P, 2, BANK], F32R)
        out_t = m.sb("out_t", [P, 2, BANK])
        ps_s = m.ps("ps_s", [P, 2, 2 * BANK])
        ps_t = m.ps("ps_t", [P, 2, BANK])
        ps_o = m.ps("ps_o", [P, BANK])
        ps_qkv = m.ps("ps_qkv", [P, BANK])

        x_in = [m.sem(f"x_in{i}") for i in range(XS)]
        w_in = [m.sem(f"w_in{i}") for i in range(SLOTS)]
        tab_in = m.sem("tab_in")
        ln_step, ln_eps, ln_rstd = m.sem("ln_step"), m.sem("ln_eps"), m.sem("ln_rstd")
        xn_ok, xt_ok, xt_hi_ok, xt_lo_ok = (m.sem(n) for n in ("xn_ok", "xt_ok", "xt_hi_ok", "xt_lo_ok"))
        w_hi_ok, w_lo_ok, w_early = m.sem("w_hi_ok"), m.sem("w_lo_ok"), m.sem("w_early")
        qkv_ok, qkv_read = m.sem("qkv_ok"), m.sem("qkv_read")
        v_hi_ok, rot_step, rot_ok = m.sem("v_hi_ok"), m.sem("rot_step"), m.sem("rot_ok")
        tile_ok, tile_hi_ok, tile_lo_ok = m.sem("tile_ok"), m.sem("tile_hi_ok"), m.sem("tile_lo_ok")
        s_ok, max_ok, exp_ok = m.sem("s_ok"), m.sem("max_ok"), m.sem("exp_ok")
        inv_ok, norm_ok, pv_ok = m.sem("inv_ok"), m.sem("norm_ok"), m.sem("pv_ok")
        o_half, o_ok, o_out = m.sem("o_half"), m.sem("o_ok"), [m.sem(f"o_out{i}") for i in range(2)]

        def first_tile(j):
            return j * NT + TB - 1

        ROUNDS = TB + 3
        FIRST_SCORES = {TB + 1: (0, 1), TB + 2: (2, 3, 4)}

        def for_pairs(eng, prologue, attention, drain):
            with eng.Fori(0, B) as b:
                j = b * NP
                prologue(b, j)
                attention(j, 0, True, False)
                with eng.Fori(0, (NP - 2) // 2) as two:
                    attention(j + two * 2 + 1, 1, False, False)
                    attention(j + two * 2 + 2, 0, False, False)
                attention(j + (NP - 1), 1, False, True)
                drain(j + (NP - 1))

        block = scope.enter_context(nc.Block())

        @block.sync
        def _(sp):
            def load_w(pair, k):
                sp.dma_start(w_raw[:, k % SLOTS, :], wqkv[pair, k * P:(k + 1) * P, :]).then_inc(w_in[k % SLOTS], 16)

            def first_w(j, pair):
                for k in range(SLOTS):
                    sp.wait_ge(w_lo_ok, (j - 1) * HB + k + SLOTS + 1)
                    load_w(pair, k)

            def rest_of_w(j, pair):
                for k in range(SLOTS, HB):
                    sp.wait_ge(w_lo_ok, j * HB + k - SLOTS + 1)
                    load_w(pair, k)

            sp.dma_start(cos_sb[:, :, :, :], cos.rearrange("(t p) a d -> p t a d", p=P)).then_inc(tab_in, 16)
            sp.dma_start(sin_sb[:, :, :, :], sin.rearrange("(t p) a d -> p t a d", p=P)).then_inc(tab_in, 16)
            for k in range(SLOTS):
                load_w(0, k)
            with sp.Fori(0, B) as b:
                for t in range(TB):
                    if t < XS:
                        sp.wait_ge(tile_ok, b * NP * NT)
                    else:
                        sp.wait_ge(xt_ok, b * TB + t - XS + 1)
                    sp.dma_start(x_tile[:, t % XS, :], x[b, t * P:(t + 1) * P, :]).then_inc(x_in[t % XS], 16)
                    if t == XS - 1:
                        rest_of_w(b * NP, 0)
                with sp.Fori(1, NP) as pair:
                    first_w(b * NP + pair, pair)
                    rest_of_w(b * NP + pair, pair)
                first_w(b * NP + NP, 0)
            for k in range(SLOTS):
                sp.wait_ge(w_in[k], 16 * (2 * B * NP + 1))

        @block.gpsimd
        def _(pool):
            def rest_of_w(j, k):
                pool.wait_ge(w_hi_ok, j * HB + k + 1)
                pool.tensor_tensor(w_lo[:, k, :], w_raw[:, k % SLOTS, :], raw(w_hi[:, k, :]), ALU.subtract).then_inc(w_lo_ok, 1)

            def find_rstd(b, t):
                pool.wait_ge(ln_step, (b * TB + t) * 3 + 3)
                stand_alone(pool, passed)
                pool.tensor_scalar(rstd[:, t:t + 1], mean_var[:, t, 1:2], EPS, 1.0, ALU.add, ALU.mult).then_inc(ln_eps, 1)
                pool.wait_ge(ln_eps, b * TB + t + 1)
                pool.tensor_tensor(rstd[:, t:t + 1], rstd[:, t:t + 1], half[:, 0:1], ALU.pow).then_inc(ln_rstd, 1)

            def prologue(b, j):
                find_rstd(b, 0)
                for t in range(1, TB):
                    find_rstd(b, t)
                    if SLOTS + 2 * t <= HB:
                        rest_of_w(j, SLOTS + 2 * t - 2)
                        rest_of_w(j, SLOTS + 2 * t - 1)
                for k in range(SLOTS):
                    rest_of_w(j + 1, k)

            def store(b, pair, u):
                h, g = UNITS[u]
                pool.wait_ge(o_ok, (b * NP + pair) * NU + u + 1)
                pool.dma_start(attn_out[b, pair, h * HD:(h + 1) * HD, g * BANK:(g + 1) * BANK],
                               out_t[h * HD:(h + 1) * HD, u % 2, :]).then_inc(o_out[u % 2], 16)

            for k in range(SLOTS):
                rest_of_w(0, k)
            with pool.Fori(0, B) as b:
                prologue(b, b * NP)
                for k in range(SLOTS, HB):
                    rest_of_w(b * NP + 1, k)
                for u in range(NU - 1):
                    store(b, 0, u)
                for k in range(SLOTS):
                    rest_of_w(b * NP + 2, k)
                with pool.Fori(1, NP - 1) as pair:
                    for k in range(SLOTS, HB):
                        rest_of_w(b * NP + pair + 1, k)
                    store(b, pair - 1, NU - 1)
                    for u in range(NU - 1):
                        store(b, pair, u)
                    for k in range(SLOTS):
                        rest_of_w(b * NP + pair + 2, k)
                store(b, NP - 2, NU - 1)
                for u in range(NU):
                    store(b, NP - 1, u)
            for i in range(2):
                pool.wait_ge(o_out[i], 16 * B * NP * NU // 2)

        @block.tensor
        def _(pe):
            def turn_x(b, t):
                pe.wait_ge(xn_ok, b * TB + t + 1)
                if t >= 2:
                    pe.wait_ge(xt_lo_ok, b * TB + t - 1)
                for k in range(HB):
                    mm = pe.transpose(ps_s[:, t % 2, k * P:(k + 1) * P], x_tile[:, t % XS, k * P:(k + 1) * P], ident[:, :])
                mm.then_inc(xt_ok, 1)

            def qkv(j, t, part, out):
                for n in part:
                    k, term = divmod(n, 3)
                    if t == 0 and term == 0:
                        pe.wait_ge(w_lo_ok, j * HB + k + 1)
                    a = slice(t * P, (t + 1) * P)
                    xs, ws = ((xt_hi, w_hi), (xt_hi, w_lo), (xt_lo, w_hi))[term]
                    mm = pe.matmul(out, xs[:, k, a], ws[:, k, :], start=(n == 0), stop=(n == 3 * HB - 1))
                    if t == TB - 1 and n == 3 * SLOTS - 1:
                        mm.then_inc(w_early, 1)
                if part[-1] == 3 * HB - 1:
                    mm.then_inc(qkv_ok, 1)

            def turn_qk(j, t, start, at):
                pe.wait_ge(rot_ok, j * TB + t + 1)
                pe.wait_ge(tile_lo_ok, start + (at - 1 if at >= 2 else 0))
                for r in range(4):
                    mm = pe.transpose(ps_t[:, at % 2, r * P:(r + 1) * P], rotated[:, r, :, :].rearrange("p a d -> p (a d)"), ident[:, :])
                mm.then_inc(tile_ok, 1)

            def scores(j, slot, u, i):
                h, g = UNITS[u]
                n = GQ * u + i
                qb = GQ * g + i
                keys = P * (qb + 1)
                for c in range(0, keys, BANK):
                    w = max(min(BANK, keys - c), 2 * P)
                    out = ps_s[:, n % 2, c:c + w]
                    pe.matmul(out, qk_hi[slot][:, h, qb * P:(qb + 1) * P], qk_hi[slot][:, 2 + h, c:c + w],
                              start=True, stop=False, skip_group_check=True)
                    pe.matmul(out, q_lo[slot][:, h, qb * P:(qb + 1) * P], qk_hi[slot][:, 2 + h, c:c + w],
                              start=False, stop=True, skip_group_check=True)
                mm = pe.matmul(ps_s[:, n % 2, qb * P:(qb + 1) * P], ident16[:, :], mask16[:, :],
                               start=False, stop=True, skip_group_check=True)
                mm.then_inc(s_ok, 1)

            def prologue(b, j):
                pe.wait_ge(exp_ok, j * NQ)
                pe.wait_ge(qkv_read, j * TB)
                pe.wait_ge(o_ok, j * NU)
                for i in range(ROUNDS):
                    if i < TB:
                        turn_x(b, i)
                    if i >= 4:
                        turn_qk(j, i - 4, j * NT, i - 4)
                    t = i - 2
                    if 0 <= t < TB:
                        pe.wait_ge(xt_lo_ok, b * TB + t + 1)
                        stand_alone(pe, passed)
                        if t >= 2:
                            pe.wait_ge(qkv_read, j * TB + t - 1)
                        qkv(j, t, range(3 * HB), (ps_qkv if t % 2 else ps_o)[:, 0:W])
                    for n in FIRST_SCORES.get(i, ()):
                        pe.wait_ge(tile_lo_ok, j * NT + n + 1 + (n % GQ == 0))
                        if n >= 2:
                            pe.wait_ge(exp_ok, j * NQ + n - 1)
                        scores(j, 0, n // GQ, n % GQ)

            def weigh_values(j, slot, s, tile):
                u, kb = STEPS[s]
                h, g = UNITS[u]
                pe.wait_ge(tile_lo_ok, tile)
                if kb == 0:
                    pe.wait_ge(o_ok, j * NU + u)
                off = P * max(0, kb - GQ * g)
                both = v[slot][:, kb, h, :, :].rearrange("p a d -> p (a d)")
                pe.matmul(ps_o[:, off:], both, pt_hi[:, s % 2, off:], start=(kb == 0), stop=False, skip_group_check=True)
                pe.matmul(ps_o[:, off:], both, pt_lo[:, s % 2, off:], start=False, stop=True,
                          skip_group_check=True).then_inc(pv_ok, 1)

            def attention(j, slot, first, last):
                tiles = tile_order(last)
                for s, (u, kb) in enumerate(STEPS):
                    h, g = UNITS[u]
                    group, place = divmod(s, PER)
                    if kb == 0:
                        pe.wait_ge(norm_ok, j * NQ + GQ * (u + 1))
                    at = tiles["probs", s]
                    pe.wait_ge(tile_lo_ok, first_tile(j) + (at - 1))
                    for i in range(max(0, kb - GQ * g), GQ):
                        mm = pe.transpose(ps_t[:, (TB - 1 + at) % 2, i * P:(i + 1) * P], probs[g][:, i, kb * P:(kb + 1) * P], ident[:, :])
                    mm.then_inc(tile_ok, 1)
                    for ahead, unit, i in next_queries(s, last):
                        if unit == 1 and not ahead:
                            pe.wait_ge(tile_lo_ok, first_tile(j) + (tiles["qk", 0] + 1 if i == GQ - 1 else 0))
                        elif unit == 1:
                            pe.wait_ge(tile_lo_ok, first_tile(j) + tiles["qk", GQ + 1] + 1)
                        elif unit == 0 and i == 0:
                            pe.wait_ge(tile_lo_ok, first_tile(j) + tiles["qk", GQ] + 1)
                        pe.wait_ge(exp_ok, (j + ahead) * NQ + GQ * unit + i - 1)
                        scores(j + ahead, (slot + ahead) % 2, unit, i)
                    if 0 < s and place < PER - 1:
                        weigh_values(j, slot, s - 1, first_tile(j) + tiles["probs", s - 1] + 1)
                    elif s == 0 and not first:
                        weigh_values(j - 1, 1 - slot, NS - 1, first_tile(j))
                    if place == 1 and group == 0:
                        turn_qk(j, TB - 1, j * NT, TB - 1 + tiles["qk", 0])
                    elif place == 1 and not last:
                        turn_qk(j + 1, group - 1, j * NT, TB - 1 + tiles["qk", group])
                    if not last:
                        if place == 0:
                            pe.wait_ge(qkv_read, j * TB + TB + group)
                        qkv(j + 1, group, PARTS[place], ps_qkv[:, 0:W])
                    if place == PER - 1:
                        weigh_values(j, slot, s - 1, first_tile(j) + tiles["probs", s - 1] + 1)

            def drain(j):
                weigh_values(j, 1, NS - 1, (j + 1) * NT)

            for_pairs(pe, prologue, attention, drain)

        @block.scalar
        def _(act):
            def split_w(j, k):
                act.wait_ge(w_in[k % SLOTS], 16 * (j * 2 + k // SLOTS + 1))
                act.activation(w_hi[:, k, :], w_raw[:, k % SLOTS, :], ACT.Copy).then_inc(w_hi_ok, 1)

            def split_x(b, t):
                act.wait_ge(xt_ok, b * TB + t + 1)
                act.activation(xt_hi[:, :, t * P:(t + 1) * P],
                               ps_s[:, t % 2, :].rearrange("p (k c) -> p k c", c=P), ACT.Copy).then_inc(xt_hi_ok, 1)

            def split_v(j, slot, t, bank):
                act.wait_ge(qkv_ok, j * TB + t + 1)
                act.activation(v[slot][:, t, :, 0, :], bank[:, 2 * P:W].rearrange("p (h d) -> p h d", d=HD), ACT.Copy).then_inc(v_hi_ok, 1)

            def split_qk(slot, t, start, at):
                act.wait_ge(tile_ok, start + (at + 1))
                act.activation(qk_hi[slot][:, :, t * P:(t + 1) * P],
                               ps_t[:, at % 2, :].rearrange("p (r c) -> p r c", c=P), ACT.Copy).then_inc(tile_hi_ok, 1)

            def exps(j, u, i):
                h, g = UNITS[u]
                n = GQ * u + i
                act.wait_ge(max_ok, j * NQ + n + 1)
                keys = P * (GQ * g + i + 1)
                act.activation(probs[g][:, i, 0:keys], ps_s[:, n % 2, 0:keys], ACT.Exp,
                               bias=neg_max[:, n:n + 1], accum_out=row_sum[:, n:n + 1]).then_inc(exp_ok, 1)

            def normalise(j, u, i):
                h, g = UNITS[u]
                n = GQ * u + i
                keys = P * (GQ * g + i + 1)
                act.wait_ge(inv_ok, j * NQ + n + 1)
                act.activation(probs[g][:, i, 0:keys], probs[g][:, i, 0:keys], ACT.Copy, scale=inv_sum[:, n:n + 1]).then_inc(norm_ok, 1)

            def lo_summand(j, u):
                h, g = UNITS[u]
                act.wait_ge(pv_ok, j * NS + steps_from(u + 1))
                act.wait_ge(o_out[u % 2], (j * 2 + u // 2) * 16)
                act.activation(out_t[(1 - h) * HD:(2 - h) * HD, u % 2, :], ps_o[HD:P, :], ACT.Copy).then_inc(o_half, 1)

            def early_weights(j):
                act.wait_ge(w_early, j)
                for k in range(SLOTS):
                    split_w(j, k)

            def prologue(b, j):
                act.wait_ge(qkv_ok, j * TB)
                act.wait_ge(s_ok, j * NQ)
                act.wait_ge(pv_ok, j * NS)
                for i in range(ROUNDS):
                    for k in range(SLOTS + 2 * i, min(SLOTS + 2 * i + 2, HB)):
                        split_w(j, k)
                    if i < TB:
                        split_x(b, i)
                    if i >= 4:
                        split_qk(0, i - 4, j * NT, i - 4)
                    t = i - 2
                    if 0 <= t < TB:
                        split_v(j, 0, t, ps_qkv if t % 2 else ps_o)
                    for n in FIRST_SCORES.get(i, ()):
                        exps(j, n // GQ, n % GQ)
                        if n >= 1:
                            normalise(j, 0, n - 1)
                early_weights(j + 1)
                normalise(j, 1, 0)

            def attention(j, slot, first, last):
                tiles = tile_order(last)
                fresh = [] if first else [(j, 1, 0)]
                for s, (u, kb) in enumerate(STEPS):
                    h, g = UNITS[u]
                    group, place = divmod(s, PER)
                    at = tiles["probs", s]
                    act.wait_ge(tile_ok, first_tile(j) + (at + 1))
                    if s > 0:
                        act.wait_ge(pv_ok, j * NS + s - 1)
                    elif not first:
                        act.wait_ge(pv_ok, j * NS - 1)
                    off = P * max(0, kb - GQ * g)
                    act.activation(pt_hi[:, s % 2, off:], ps_t[:, (TB - 1 + at) % 2, off:], ACT.Copy).then_inc(tile_hi_ok, 1)
                    for args in fresh:
                        normalise(*args)
                    fresh = []
                    if kb == 0 and u > 0:
                        lo_summand(j, u - 1)
                    elif s == 0 and not first:
                        lo_summand(j - 1, NU - 1)
                    if place == PER - 1 and not last:
                        if group == 0:
                            act.wait_ge(pv_ok, j * NS)
                        split_v(j + 1, 1 - slot, group, ps_qkv)
                    if place == 1 and group == 0:
                        split_qk(slot, TB - 1, j * NT, TB - 1 + tiles["qk", 0])
                    elif place == 1 and not last:
                        if group == 1:
                            act.wait_ge(s_ok, j * NQ)
                        split_qk(1 - slot, group - 1, j * NT, TB - 1 + tiles["qk", group])
                    if s in W_OF_STEP and not last:
                        ahead, blocks = W_OF_STEP[s]
                        if ahead == 2:
                            act.wait_ge(w_early, j + 2)
                        else:
                            act.wait_ge(qkv_ok, j * TB + TB)
                        for k in blocks:
                            split_w(j + ahead, k)
                    for ahead, unit, i in next_queries(s, last):
                        exps(j + ahead, unit, i)
                        fresh.append((j + ahead, unit, i))

            def drain(j):
                lo_summand(j, NU - 1)

            for k in range(SLOTS):
                split_w(0, k)
            for_pairs(act, prologue, attention, drain)

        @block.vector
        def _(dve):
            dve.wait_ge(tab_in, 32)

            def moments(b, t):
                dve.wait_ge(x_in[t % XS], (b * (TB // XS) + t // XS) * 16 + 16)
                for c in range(2):
                    dve.bn_stats(stats[:, t, c, :], x_tile[:, t % XS, c * BANK:(c + 1) * BANK]).then_inc(ln_step, 1)
                dve.wait_ge(ln_step, (b * TB + t) * 3 + 2)
                stand_alone(dve, passed)
                dve.bn_aggr(mean_var[:, t, :], stats[:, t, :, :].rearrange("p a s -> p (a s)")).then_inc(ln_step, 1)

            def ln1(b, t):
                dve.wait_ge(ln_rstd, b * TB + t + 1)
                dve.tensor_scalar(x_tile[:, t % XS, :], x_tile[:, t % XS, :], mean_var[:, t, 0:1], rstd[:, t:t + 1],
                                  ALU.subtract, ALU.mult).then_inc(xn_ok, 1)

            def rest_of_x(b, t):
                dve.wait_ge(xt_hi_ok, b * TB + t + 1)
                dve.tensor_tensor(xt_lo[:, :, t * P:(t + 1) * P],
                                  ps_s[:, t % 2, :].rearrange("p (k c) -> p k c", c=P),
                                  raw(xt_hi[:, :, t * P:(t + 1) * P]), ALU.subtract).then_inc(xt_lo_ok, 1)

            def rotate(j, slot, t, bank, turned):
                n = j * TB + t
                dve.wait_ge(v_hi_ok, n + 1)
                half_d = HD // 2
                qk = bank[:, 0:2 * P].rearrange("p (a h d) -> p a h d", a=2, d=HD)
                s = r_sin[:, :, :].rearrange("p (a h) d -> p a h d", a=2)
                sb_ = sin_sb[:, t, :, :].unsqueeze(2).broadcast_to([P, 2, 2, HD])
                dve.wait_ge(rot_ok, n)
                dve.tensor_tensor(r_cos[:, :, :].rearrange("p (a h) (c d) -> p a (h c) d", a=2, c=2),
                                  bank[:, 0:2 * P].rearrange("p (a h d) -> p a h d", a=2, d=half_d),
                                  cos_sb[:, t, :, :].unsqueeze(2).broadcast_to([P, 2, 4, half_d]), ALU.mult).then_inc(rot_step, 1)
                dve.tensor_tensor(s[:, :, :, 0:half_d], qk[:, :, :, half_d:], sb_[:, :, :, 0:half_d], ALU.mult).then_inc(rot_step, 1)
                dve.tensor_tensor(s[:, :, :, half_d:], qk[:, :, :, 0:half_d], sb_[:, :, :, half_d:], ALU.mult).then_inc(rot_step, 1)
                dve.tensor_tensor(v[slot][:, t, :, 1, :], bank[:, 2 * P:W].rearrange("p (h d) -> p h d", d=HD),
                                  raw(v[slot][:, t, :, 0, :]), ALU.subtract).then_inc(qkv_read, 1)
                dve.wait_ge(rot_step, n * 3 + 3)
                dve.wait_ge(tile_ok, turned)
                dve.tensor_tensor(rotated[:, :, :, :],
                                  r_cos[:, :, :].unsqueeze(2).broadcast_to([P, 4, 2, HD]),
                                  r_sin[:, :, :].unsqueeze(2).broadcast_to([P, 4, 2, HD]), ALU.add).then_inc(rot_ok, 1)

            def rest_of_qk(slot, t, start, at):
                dve.wait_ge(tile_hi_ok, start + (at + 1))
                a = slice(t * P, (t + 1) * P)
                both = ps_t[:, at % 2, :].rearrange("p (r c) -> p r c", c=P)
                dve.tensor_tensor(q_lo[slot][:, :, a], both[:, 0:2, :], raw(qk_hi[slot][:, 0:2, a]), ALU.subtract)
                dve.tensor_tensor(qk_hi[slot][HD:P, 2:4, a], both[HD:P, 2:4, :], raw(qk_hi[slot][HD:P, 2:4, a]),
                                  ALU.subtract).then_inc(tile_lo_ok, 1)

            def maxima(j, u, i):
                h, g = UNITS[u]
                n = GQ * u + i
                dve.wait_ge(s_ok, j * NQ + n + 1)
                keys = P * (GQ * g + i + 1)
                dve.tensor_reduce(neg_max[:, n:n + 1], ps_s[:, n % 2, 0:keys], AX.X, ALU.max, negate=True).then_inc(max_ok, 1)

            def invert(j, u, i):
                n = GQ * u + i
                dve.wait_ge(exp_ok, j * NQ + n + 1)
                stand_alone(dve, passed)
                dve.reciprocal(inv_sum[:, n:n + 1], row_sum[:, n:n + 1]).then_inc(inv_ok, 1)

            def add_parts(j, u):
                h, g = UNITS[u]
                dve.wait_ge(o_half, j * NU + u + 1)
                dve.tensor_tensor(out_t[h * HD:(h + 1) * HD, u % 2, :], ps_o[0:HD, :],
                                  out_t[(1 - h) * HD:(2 - h) * HD, u % 2, :], ALU.add).then_inc(o_ok, 1)

            def prologue(b, j):
                moments(b, 0)
                for i in range(ROUNDS):
                    if i + 1 < TB:
                        moments(b, i + 1)
                    if i < TB:
                        ln1(b, i)
                    if 1 <= i <= TB:
                        rest_of_x(b, i - 1)
                    if i >= 4:
                        rest_of_qk(0, i - 4, j * NT, i - 4)
                    t = i - 3
                    if t >= 0:
                        rotate(j, 0, t, ps_qkv if t % 2 else ps_o, j * NT + t)
                    for n in FIRST_SCORES.get(i, ()):
                        maxima(j, n // GQ, n % GQ)
                        if n >= 1:
                            invert(j, 0, n - 1)
                invert(j, 1, 0)

            def attention(j, slot, first, last):
                tiles = tile_order(last)
                fresh = [] if first else [(j, 1, 0)]
                for s, (u, kb) in enumerate(STEPS):
                    h, g = UNITS[u]
                    group, place = divmod(s, PER)
                    for args in fresh:
                        invert(*args)
                    fresh = []
                    at = tiles["probs", s]
                    dve.wait_ge(tile_hi_ok, first_tile(j) + (at + 1))
                    off = P * max(0, kb - GQ * g)
                    dve.tensor_tensor(pt_lo[:, s % 2, off:], ps_t[:, (TB - 1 + at) % 2, off:], raw(pt_hi[:, s % 2, off:]),
                                      ALU.subtract).then_inc(tile_lo_ok, 1)
                    for ahead, unit, i in next_queries(s, last):
                        maxima(j + ahead, unit, i)
                        fresh.append((j + ahead, unit, i))
                    if kb == 0 and u > 0:
                        add_parts(j, u - 1)
                    elif s == 0 and not first:
                        add_parts(j - 1, NU - 1)
                    if place == PER - 1 and not last:
                        rotate(j + 1, 1 - slot, group, ps_qkv, first_tile(j) + tiles["qk", group] + 1)
                    if place == 1 and group == 0:
                        rest_of_qk(slot, TB - 1, j * NT, TB - 1 + tiles["qk", 0])
                    elif place == 1 and not last:
                        rest_of_qk(1 - slot, group - 1, j * NT, TB - 1 + tiles["qk", group])

            def drain(j):
                add_parts(j, NU - 1)

            for_pairs(dve, prologue, attention, drain)


def mix_features(nc, const, logits, x, attn_out, wo, ctx_t, xw, xbias, gate, rows, out):
    ident, ident16, mask16, half, passed = const
    HALVES = H // BANK
    with ExitStack() as scope:
        m = Memory(nc, scope)
        wo_hi = m.sb("wo_hi", [P, HB, H], F32R)
        wo_lo = m.sb("wo_lo", [P, HB, H], F32R)
        xw_hi = m.sb("xw_hi", [P, CB, 2 * D], F32R)
        xw_lo = m.sb("xw_lo", [P, CB, 2 * D], F32R)
        bias = m.sb("xattn_bias", [P, 2])
        gate_sb = m.sb("gate_sb", [P, HB, E])
        at_hi = m.sb("at_hi", [P, TB, S], F32R)
        at_lo = m.sb("at_lo", [P, TB, S], F32R)
        split = m.sb("split", [P, 4, H], F32R)
        qk = m.sb("xattn_qk", [P, 4, S], F32R)
        stage = m.sb("stage", [P, 2, H])
        work = m.sb("work", [P, 2, H])
        ctx_hi_sb, ctx_lo_sb = at_hi[:, 0:CB, :], at_lo[:, 0:CB, :]
        ctx_raw = [t[:, :, :].rearrange("p a (c n) -> p (a c) n", n=BANK) for t in (stage, work)]
        res = m.sb("residual", [P, 2, H])
        x3_t = m.sb("x3_t", [P, HB, P])
        small = m.sb("mix_small", [P, 8, 4])
        stats = m.sb("mix_stats", [P, 2, 2, 6])
        mean_var = m.sb("mix_mean_var", [P, 2, 2])
        rstd = m.sb("mix_rstd", [P, 2])
        ps_a = m.ps("ps_a", [P, H])
        ps_b = m.ps("ps_b", [P, H])
        ps_t2 = m.ps("ps_t2", [P, H])
        ps_r = m.ps("ps_r", [P, 2, BANK])
        ps_e = [ps_a, ps_b]
        ps_et = [ps_t2[:, :], ps_r[:, :, :].rearrange("p a n -> p (a n)")]

        zero_ok, zero_out = m.sem("zero_ok"), m.sem("zero_out")
        w_in = [m.sem(f"mix_w_in{i}") for i in range(4)]
        small_in = m.sem("mix_small_in")
        w_hi_ok, w_lo_ok = m.sem("mix_w_hi"), m.sem("mix_w_lo")
        ctx_in, ctx_hi, ctx_lo = [m.sem(f"ctx_in{n}") for n in range(2)], m.sem("ctx_hi"), m.sem("ctx_lo")
        proj_ok, proj_hi, proj_lo = m.sem("proj_ok"), m.sem("proj_hi"), m.sem("proj_lo")
        e_ok, emax_ok, eexp_ok, einv_ok, enorm_ok = (m.sem(n) for n in ("e_ok", "emax_ok", "eexp_ok", "einv_ok", "enorm_ok"))
        et_ok, et_hi, et_lo = m.sem("et_ok"), m.sem("et_hi"), m.sem("et_lo")
        ot_in, res_in = [m.sem(f"ot_in{i}") for i in range(2)], [m.sem(f"res_in{i}") for i in range(2)]
        ot_hi, ot_lo = m.sem("ot_hi"), m.sem("ot_lo")
        wo_ok, x1_ok = m.sem("wo_ok"), m.sem("x1_ok")
        ln_step, ln_eps, ln_rstd, ln_ok = (m.sem(n) for n in ("mix_ln_step", "mix_ln_eps", "mix_ln_rstd", "mix_ln_ok"))
        t2_ok, t2_hi, t2_lo = m.sem("t2_ok"), m.sem("t2_hi"), m.sem("t2_lo")
        xm_ok, x2_ok, x2_out, x3_out = m.sem("xm_ok"), m.sem("x2_ok"), m.sem("x2_out"), m.sem("x3_out")
        t3_ok, t3_read, r_ok, r_read = m.sem("t3_ok"), m.sem("t3_read"), m.sem("r_ok"), m.sem("r_read")

        order = [(2, 0)]
        for i in range(TB):
            order += [(2, i + 1)] * (i + 1 < TB) + [(3, i)]
        LN = {what: n for n, what in enumerate(order)}

        def raw_weights(k):
            return (stage, work)[k % 4 // 2][:, k % 2, :]

        block = scope.enter_context(nc.Block())

        @block.sync
        def _(sp):
            sp.wait_ge(zero_ok, 1)
            sp.dma_start(rows[0:P, 0:H], res[:, 0, :]).then_inc(zero_out, 16)
            sp.dma_start(rows[0:P, H:H + E], res[:, 0, 0:E]).then_inc(zero_out, 16)
            sp.dma_start(out[0:P, :], res[:, 0, :]).then_inc(zero_out, 16)
            sp.dma_start(bias[:, :], xbias).then_inc(small_in, 16)
            sp.dma_start(gate_sb[:, :, :], gate.rearrange("(k p) e -> p k e", p=P)).then_inc(small_in, 16)
            for k in range(HB + 1):
                if k >= 4:
                    sp.wait_ge(w_lo_ok, k - 3)
                if k == 0:
                    sp.dma_start(raw_weights(k).rearrange("p (c d) -> p c d", d=2 * D),
                                 xw.rearrange("(c p) d -> p c d", p=P)).then_inc(w_in[k % 4], 16)
                else:
                    sp.dma_start(raw_weights(k), wo[(k - 1) * P:k * P, :]).then_inc(w_in[k % 4], 16)
            sp.wait_ge(w_lo_ok, HB + 1)
            sp.wait_ge(zero_out, 48)
            with sp.Fori(0, B) as b:
                for n in range(2):
                    if n == 0:
                        sp.wait_ge(ot_lo, b * TB)
                    else:
                        sp.wait_ge(t3_ok, b * TB)
                        stand_alone(sp, passed)
                        sp.wait_ge(x3_out, b * TB * 16)
                    stand_alone(sp, passed)
                    sp.dma_start(ctx_raw[n], ctx_t[b].rearrange("(c p) n -> p c n", p=P)[:, :, n * BANK:(n + 1) * BANK]).then_inc(ctx_in[n], 16)

                def load_attn(i):
                    if i >= 2:
                        sp.wait_ge(ot_lo, b * TB + i - 1)
                    sp.dma_start(stage[:, i % 2, :].rearrange("p (k c) -> p k c", c=P),
                                 attn_out[b].rearrange("k p c -> p k c")[:, :, i * P:(i + 1) * P]).then_inc(ot_in[i % 2], 16)

                def load_x(i):
                    sp.dma_start(res[:, i % 2, :], x[b, i * P:(i + 1) * P, :]).then_inc(res_in[i % 2], 16)

                load_x(0)
                load_x(1)
                sp.wait_ge(ctx_lo, (b * 2 + 1) * CB)
                stand_alone(sp, passed)
                load_attn(0)
                load_attn(1)
                for i in range(TB):
                    if i + 2 < TB:
                        load_attn(i + 2)
                    row = P + (b * TB + i) * P
                    sp.wait_ge(x2_ok, b * TB + i + 1)
                    sp.dma_start(out[bass.ds(row, P), :], res[:, i % 2, :]).then_inc(x2_out, 16)
                    sp.wait_ge(ln_ok, b * 2 * TB + LN[3, i] + 1)
                    sp.dma_start(rows[bass.ds(row, P), 0:H], work[:, 1, :]).then_inc(x3_out, 16)
                    sp.wait_ge(x2_out, (b * TB + i + 1) * 16)
                    stand_alone(sp, passed)
                    if i + 2 < TB:
                        load_x(i + 2)
            sp.wait_ge(x3_out, B * TB * 16)

        @block.gpsimd
        def _(pool):
            pool.memset(res[:, 0, :], 0.0).then_inc(zero_ok, 1)
            with pool.Fori(0, B) as b:
                for which, i in order:
                    n = b * 2 * TB + LN[which, i]
                    s = which - 2
                    pool.wait_ge(ln_step, n * 3 + 3)
                    stand_alone(pool, passed)
                    pool.tensor_scalar(rstd[:, s:s + 1], mean_var[:, s, 1:2], EPS, 1.0, ALU.add, ALU.mult).then_inc(ln_eps, 1)
                    pool.wait_ge(ln_eps, n + 1)
                    pool.tensor_tensor(rstd[:, s:s + 1], rstd[:, s:s + 1], half[:, 0:1], ALU.pow).then_inc(ln_rstd, 1)

        @block.tensor
        def _(pe):
            def split_product(out, a_hi, a_lo, w_hi, w_lo, first, last):
                pe.matmul(out, a_hi, w_hi, start=first, stop=False)
                pe.matmul(out, a_hi, w_lo, start=False, stop=False)
                return pe.matmul(out, a_lo, w_hi, start=False, stop=last)

            pe.wait_ge(w_lo_ok, HB + 1)
            pe.wait_ge(small_in, 32)
            with pe.Fori(0, B) as b:
                for n in range(2):
                    pe.wait_ge(ctx_lo, (b * 2 + n + 1) * CB)
                    for w in range(2):
                        pe.wait_ge(proj_lo, (b * 2 + n) * 2)
                        pe.wait_ge(r_read, b * TB)
                        pe.wait_ge(et_lo, b * TB)
                        half_n = slice(n * BANK, (n + 1) * BANK)
                        for c in range(CB):
                            mm = split_product(ps_r[:, w, :], xw_hi[:, c, w * D:(w + 1) * D], xw_lo[:, c, w * D:(w + 1) * D],
                                               ctx_hi_sb[:, c, half_n], ctx_lo_sb[:, c, half_n], c == 0, c == CB - 1)
                        mm.then_inc(proj_ok, 1)

                def energies(i):
                    if i >= 2:
                        pe.wait_ge(eexp_ok, b * TB + i - 1)
                    a = slice(i * P, (i + 1) * P)
                    for c in range(HALVES):
                        n = slice(c * BANK, (c + 1) * BANK)
                        mm = split_product(ps_e[i % 2][:, n], qk[:, 0, a], qk[:, 1, a], qk[:, 2, n], qk[:, 3, n], True, True)
                    mm.then_inc(e_ok, 1)

                def turn_attention(i):
                    pe.wait_ge(enorm_ok, b * TB + i + 1)
                    if i >= 2:
                        pe.wait_ge(et_lo, b * TB + i - 1)
                    else:
                        pe.wait_ge(t3_read, b * TB)
                    for k in range(TB):
                        mm = pe.transpose(ps_et[i % 2][:, k * P:(k + 1) * P], work[:, i % 2, k * P:(k + 1) * P], ident[:, :])
                    mm.then_inc(et_ok, 1)

                pe.wait_ge(proj_lo, (b + 1) * 4)
                pe.wait_ge(x1_ok, b * TB)
                pe.wait_ge(x2_ok, b * TB)
                def project(i, c):
                    pe.wait_ge(ot_lo, b * TB + i + 1)
                    if c == 0:
                        pe.wait_ge(x1_ok, b * TB + i)
                    n = slice(c * BANK, (c + 1) * BANK)
                    for k in range(HB):
                        a = slice(k * P, (k + 1) * P)
                        mm = split_product(ps_a[:, n], split[:, 0, a], split[:, 1, a], wo_hi[:, k, n], wo_lo[:, k, n], k == 0, k == HB - 1)
                    if c == HALVES - 1:
                        mm.then_inc(wo_ok, 1)

                def turn(which, i):
                    g = b * TB + i
                    pe.wait_ge(ln_ok, b * 2 * TB + LN[which, i] + 1)
                    if which == 2:
                        if i >= 2:
                            pe.wait_ge(t3_read, g - 1)
                        elif i == 0:
                            pe.wait_ge(et_lo, b * TB + TB)
                    else:
                        if i + 1 < TB:
                            pe.wait_ge(t2_lo, g + 2)
                        else:
                            pe.wait_ge(t3_read, g)
                    for k in range(HB):
                        mm = pe.transpose(ps_t2[:, k * P:(k + 1) * P], work[:, which - 2, k * P:(k + 1) * P], ident[:, :])
                    mm.then_inc(t2_ok if which == 2 else t3_ok, 1)

                def mix(i):
                    g = b * TB + i
                    pe.wait_ge(t2_lo, g + 1)
                    pe.wait_ge(x2_ok, g)
                    for c in range(HALVES):
                        n = slice(c * BANK, (c + 1) * BANK)
                        for k in range(TB):
                            a = slice(k * P, (k + 1) * P)
                            mm = split_product(ps_b[:, n], split[:, 2, a], split[:, 3, a], at_hi[:, k, n], at_lo[:, k, n], k == 0, k == TB - 1)
                    mm.then_inc(xm_ok, 1)

                def route_logits(i):
                    g = b * TB + i
                    pe.wait_ge(t3_read, g + 1)
                    pe.wait_ge(r_read, g)
                    for k in range(HB):
                        mm = pe.matmul(ps_r[:, 0, 0:E], x3_t[:, k, :], gate_sb[:, k, :], start=(k == 0), stop=(k == HB - 1))
                    mm.then_inc(r_ok, 1)

                energies(0)
                for i in range(TB):
                    if i + 1 < TB:
                        energies(i + 1)
                    else:
                        project(0, 0)
                        project(0, 1)
                    turn_attention(i)
                for i in range(TB):
                    if i + 1 < TB:
                        project(i + 1, 0)
                    turn(2, i)
                    if i + 1 < TB:
                        project(i + 1, 1)
                    if i >= 1:
                        turn(3, i - 1)
                    mix(i)
                    if i >= 1:
                        route_logits(i - 1)
                turn(3, TB - 1)
                route_logits(TB - 1)

        @block.scalar
        def _(act):
            for k in range(HB + 1):
                act.wait_ge(w_in[k % 4], (k // 4) * 16 + 16)
                dst = wo_hi[:, k - 1, :] if k else xw_hi[:, :, :].rearrange("p c d -> p (c d)")
                act.activation(dst, raw_weights(k), ACT.Copy).then_inc(w_hi_ok, 1)
            act.wait_ge(small_in, 32)
            with act.Fori(0, B) as b:
                for n in range(2):
                    act.wait_ge(ctx_in[n], b * 16 + 16)
                    if n == 0:
                        act.wait_ge(xm_ok, b * TB)
                    for c in range(CB):
                        act.activation(ctx_hi_sb[:, c, n * BANK:(n + 1) * BANK], ctx_raw[n][:, c, :], ACT.Copy).then_inc(ctx_hi, 1)
                for n in range(2):
                    for w in range(2):
                        act.wait_ge(proj_ok, (b * 2 + n) * 2 + w + 1)
                        act.activation(qk[:, 2 * w, n * BANK:(n + 1) * BANK], ps_r[:, w, :], ACT.Identity,
                                       bias=bias[:, w:w + 1]).then_inc(proj_hi, 1)

                def exps(i):
                    act.wait_ge(emax_ok, b * TB + i + 1)
                    if i >= 2:
                        act.wait_ge(et_ok, b * TB + i - 1)
                    else:
                        act.wait_ge(ctx_lo, (b + 1) * 2 * CB)
                    act.activation(work[:, i % 2, :], ps_e[i % 2][:, :], ACT.Exp, bias=small[:, i, 0:1],
                                   accum_out=small[:, i, 1:2]).then_inc(eexp_ok, 1)

                def split_attention(i):
                    act.wait_ge(et_ok, b * TB + i + 1)
                    act.activation(at_hi[:, :, i * P:(i + 1) * P], ps_et[i % 2].rearrange("p (k c) -> p k c", c=P),
                                   ACT.Copy).then_inc(et_hi, 1)

                def split_attn_out(i):
                    g = b * TB + i
                    act.wait_ge(ot_in[i % 2], (b * (TB // 2) + i // 2) * 16 + 16)
                    act.wait_ge(wo_ok, g)
                    act.activation(split[:, 0, :], stage[:, i % 2, :], ACT.Copy).then_inc(ot_hi, 1)

                exps(0)
                for i in range(TB):
                    if i + 1 < TB:
                        exps(i + 1)
                    else:
                        split_attn_out(1)
                    split_attention(i)
                    if i == 0:
                        split_attn_out(0)

                def split_ln2(i):
                    g = b * TB + i
                    act.wait_ge(t2_ok, g + 1)
                    act.wait_ge(xm_ok, g)
                    act.activation(split[:, 2, :], ps_t2[:, :], ACT.Copy).then_inc(t2_hi, 1)

                def copy_ln3(i):
                    g = b * TB + i
                    act.wait_ge(t3_ok, g + 1)
                    act.wait_ge(r_ok, g)
                    act.activation(x3_t[:, :, :].rearrange("p k c -> p (k c)"), ps_t2[:, :], ACT.Copy).then_inc(t3_read, 1)

                def copy_logits(i):
                    g = b * TB + i
                    act.wait_ge(r_ok, g + 1)
                    act.activation(logits[:, bass.ds(g, 1), :].rearrange("p a e -> p (a e)"), ps_r[:, 0, 0:E], ACT.Copy).then_inc(r_read, 1)

                for i in range(TB):
                    split_ln2(i)
                    if i + 2 < TB:
                        split_attn_out(i + 2)
                    if i >= 1:
                        copy_ln3(i - 1)
                        copy_logits(i - 1)
                copy_ln3(TB - 1)
                copy_logits(TB - 1)

        @block.vector
        def _(dve):
            for k in range(HB + 1):
                dve.wait_ge(w_hi_ok, k + 1)
                dst, hi = (wo_lo[:, k - 1, :], wo_hi[:, k - 1, :]) if k else (t[:, :, :].rearrange("p c d -> p (c d)") for t in (xw_lo, xw_hi))
                dve.tensor_tensor(dst, raw_weights(k), raw(hi), ALU.subtract).then_inc(w_lo_ok, 1)
            dve.wait_ge(small_in, 32)
            with dve.Fori(0, B) as b:
                for n in range(2):
                    for c in range(CB):
                        dve.wait_ge(ctx_hi, (b * 2 + n) * CB + c + 1)
                        a = slice(n * BANK, (n + 1) * BANK)
                        dve.tensor_tensor(ctx_lo_sb[:, c, a], ctx_raw[n][:, c, :], raw(ctx_hi_sb[:, c, a]), ALU.subtract).then_inc(ctx_lo, 1)
                for n in range(2):
                    for w in range(2):
                        dve.wait_ge(proj_hi, (b * 2 + n) * 2 + w + 1)
                        a = slice(n * BANK, (n + 1) * BANK)
                        dve.scalar_tensor_tensor(out=qk[:, 2 * w + 1, a], in0=ps_r[:, w, :], scalar=bias[:, w:w + 1],
                                                 in1=raw(qk[:, 2 * w, a]), op0=ALU.add, op1=ALU.subtract).then_inc(proj_lo, 1)

                def maxima(i):
                    dve.wait_ge(e_ok, b * TB + i + 1)
                    dve.tensor_reduce(small[:, i, 0:1], ps_e[i % 2][:, :], AX.X, ALU.max, negate=True).then_inc(emax_ok, 1)

                def normalise_rows(i):
                    dve.wait_ge(eexp_ok, b * TB + i + 1)
                    dve.reciprocal(small[:, i, 2:3], small[:, i, 1:2]).then_inc(einv_ok, 1)
                    dve.wait_ge(einv_ok, b * TB + i + 1)
                    dve.tensor_scalar(work[:, i % 2, :], work[:, i % 2, :], small[:, i, 2:3], None, ALU.mult).then_inc(enorm_ok, 1)

                def rest_of_attention(i):
                    dve.wait_ge(et_hi, b * TB + i + 1)
                    a = slice(i * P, (i + 1) * P)
                    dve.tensor_tensor(at_lo[:, :, a], ps_et[i % 2].rearrange("p (k c) -> p k c", c=P), raw(at_hi[:, :, a]),
                                      ALU.subtract).then_inc(et_lo, 1)

                def rest_of_attn_out(i):
                    dve.wait_ge(ot_hi, b * TB + i + 1)
                    dve.tensor_tensor(split[:, 1, :], stage[:, i % 2, :], raw(split[:, 0, :]), ALU.subtract).then_inc(ot_lo, 1)

                def layer_norm(which, i):
                    n = b * 2 * TB + LN[which, i]
                    s = which - 2
                    for c in range(HALVES):
                        dve.bn_stats(stats[:, s, c, :], res[:, i % 2, c * BANK:(c + 1) * BANK]).then_inc(ln_step, 1)
                    dve.wait_ge(ln_step, n * 3 + 2)
                    stand_alone(dve, passed)
                    dve.bn_aggr(mean_var[:, s, :], stats[:, s, :, :].rearrange("p a s -> p (a s)")).then_inc(ln_step, 1)
                    dve.wait_ge(ln_rstd, n + 1)
                    if which == 2 and i >= 1:
                        dve.wait_ge(t2_ok, b * TB + i)
                    if which == 3 and i >= 1:
                        dve.wait_ge(t3_ok, b * TB + i)
                        dve.wait_ge(x3_out, (b * TB + i) * 16)
                    dve.tensor_scalar(work[:, s, :], res[:, i % 2, :], mean_var[:, s, 0:1], rstd[:, s:s + 1],
                                      ALU.subtract, ALU.mult).then_inc(ln_ok, 1)

                def add_projection(i, between=None):
                    dve.wait_ge(wo_ok, b * TB + i + 1)
                    dve.wait_ge(res_in[i % 2], (b * (TB // 2) + i // 2) * 16 + 16)
                    dve.tensor_tensor(res[:, i % 2, :], ps_a[:, :], res[:, i % 2, :], ALU.add).then_inc(x1_ok, 1)
                    dve.wait_ge(x1_ok, b * TB + i + 1)
                    if between:
                        between(i + 1)
                    layer_norm(2, i)

                def rest_of_ln2(i):
                    dve.wait_ge(t2_hi, b * TB + i + 1)
                    dve.tensor_tensor(split[:, 3, :], ps_t2[:, :], raw(split[:, 2, :]), ALU.subtract).then_inc(t2_lo, 1)

                def add_mix(i):
                    dve.wait_ge(xm_ok, b * TB + i + 1)
                    dve.tensor_tensor(res[:, i % 2, :], ps_b[:, :], res[:, i % 2, :], ALU.add).then_inc(x2_ok, 1)
                    dve.wait_ge(x2_ok, b * TB + i + 1)
                    layer_norm(3, i)

                maxima(0)
                for i in range(TB):
                    if i + 1 < TB:
                        maxima(i + 1)
                    normalise_rows(i)
                    if i >= 1:
                        rest_of_attention(i - 1)
                    if i == 1:
                        rest_of_attn_out(0)
                add_projection(0, rest_of_attn_out)
                rest_of_attention(TB - 1)
                for i in range(TB):
                    rest_of_ln2(i)
                    if i + 1 < TB:
                        add_projection(i + 1)
                    if i + 2 < TB:
                        rest_of_attn_out(i + 2)
                    add_mix(i)


def route(nc, const, logits, lo16, hi16, starts, similarity, rows):
    ident, passed = const[0], const[-1]
    N = B * TB
    G = BANK // P
    R = BANK // E
    with ExitStack() as scope:
        m = Memory(nc, scope)
        top = m.sb("top_values", [P, N, TOPK])
        top_i = m.sb("top_index", [P, N, TOPK], U32)
        top_f = m.sb("top_index_f", [P, N, TOPK])
        rest = m.sb("rest", [P, N, E])
        prob = m.sb("prob", [P, N, E])
        first = m.sb("first", [P, N, E])
        hit = m.sb("hit", [P, N, E])
        sums = m.sb("sums", [P, 4, N])
        iota_e = m.sb("iota_e", [P, E])
        place = m.sb("place", [E, 1])
        picked = m.sb("picked", [P, 2, E], BF16)
        ones16 = m.sb("ones16", [P, P], BF16)
        before16 = m.sb("before16", [P, P], BF16)
        sim = m.sb("sim_sb", [E, E])
        cand = m.sb("cand", [E, E])
        is_first = m.sb("is_first", [E, E], I32)
        best = m.sb("best", [E, TOPK])
        best_i = m.sb("best_i", [E, TOPK], U32)
        s1 = m.sb("route_small", [E, 8])
        remap = m.sb("remap", [E, E])
        weight_t = m.sb("weight_t", [E, 2, BANK])
        weight = m.sb("weight", [P, N, E])
        routed16 = m.sb("routed16", [P, N, E], BF16)
        so_far16 = m.sb("so_far16", [P, N + 1, E], BF16)
        rank = m.sb("rank", [P, E, N], I32)
        part = m.sb("part", [P, E, N], I32)
        count = m.sb("count", [P, E], I32)
        blocks = m.sb("blocks", [P, E])
        ends = m.sb("ends", [P, E])
        zeros = m.sb("zeros", [P, E])
        ps_n = m.ps("ps_n", [P, BANK])
        ps_w = m.ps("ps_w", [P, 2, BANK])
        ps_x = m.ps("ps_x", [P, 2, BANK])
        ps_k = m.ps("ps_k", [P, 2, BANK])

        made, sim_in, sim_ok = m.sem("route_made"), m.sem("sim_in"), m.sem("sim_ok")
        step = m.sem("route_step")
        z_ok, exp_ok, picked_ok, votes_ok = (m.sem(n) for n in ("z_ok", "p_exp_ok", "picked_ok", "votes_ok"))
        remap_ok, wt_ok, wt_read, w2_ok, w2_read = (m.sem(n) for n in ("remap_ok", "wt_ok", "wt_read", "w2_ok", "w2_read"))
        w_out, routed_ok, rank_ok, rank_read = (m.sem(n) for n in ("w_out", "routed_ok", "rank_ok", "rank_read"))
        block = scope.enter_context(nc.Block())

        @block.gpsimd
        def _(pool):
            pool.iota(iota_e[:, :], [[1, E]], base=0, channel_multiplier=0, allow_small_or_imprecise_dtypes=True).then_inc(made, 1)
            pool.iota(place[:, :], [[1, 1]], base=0, channel_multiplier=1, allow_small_or_imprecise_dtypes=True).then_inc(made, 1)
            pool.memset(ones16[:, :], 1.0).then_inc(made, 1)
            pool.memset(before16[:, :], 1.0).then_inc(made, 1)
            pool.memset(cand[:, :], -3e38).then_inc(made, 1)
            pool.memset(so_far16[:, 0, :], 0.0).then_inc(made, 1)
            pool.memset(zeros[:, :], 0.0).then_inc(made, 1)
            pool.memset(starts[:, 0:1], 0).then_inc(made, 1)
            pool.memset(lo16[:, E:, :], 0.0).then_inc(made, 1)
            pool.memset(hi16[:, E:, :], 0.0).then_inc(made, 1)
            pool.wait_ge(made, 10)
            pool.affine_select(out=before16[:, :], in_=before16[:, :], compare_op=ALU.is_gt, fill=0.0,
                               base=0, pattern=[[1, P]], channel_multiplier=-1).then_inc(made, 1)
            pool.wait_ge(sim_in, 16)
            pool.affine_select(out=sim[:, :], in_=sim[:, :], compare_op=ALU.not_equal, fill=1.0,
                               base=0, pattern=[[-1, E]], channel_multiplier=1).then_inc(sim_ok, 1)

        @block.sync
        def _(sp):
            sp.dma_start(sim[:, :], similarity).then_inc(sim_in, 16)
            sp.wait_ge(w2_read, N // G)
            sp.dma_start(rows[P:P + N * P, H:H + E].rearrange("(n p) e -> p n e", p=P), weight[:, :, :]).then_inc(w_out, 16)
            sp.wait_ge(w_out, 16)

        @block.scalar
        def _(act):
            act.wait_ge(z_ok, 1)
            act.activation(prob[:, :, :], prob[:, :, :], ACT.Exp).then_inc(exp_ok, 1)
            for g in range(N // G):
                act.wait_ge(wt_ok, g + 1)
                if g >= 2:
                    act.wait_ge(w2_ok, g - 1)
                act.activation(weight_t[:, g % 2, :], ps_w[0:E, g % 2, :], ACT.Copy).then_inc(wt_read, 1)

        @block.tensor
        def _(pe):
            pe.wait_ge(made, 11)
            pe.wait_ge(picked_ok, 1)
            pe.matmul(ps_n[0:E, 0:E], ones16[:, 0:E], picked[:, 0, :], start=True, stop=True)
            pe.matmul(ps_n[0:E, E:E + 1], picked[:, 0, :], ones16[:, 0:1], start=True, stop=True)
            pe.matmul(ps_n[0:E, E + 1:E + 2], picked[:, 1, :], ones16[:, 0:1], start=True, stop=True).then_inc(votes_ok, 1)
            pe.wait_ge(remap_ok, 1)

            def remapped(g):
                pe.wait_ge(wt_read, g + 1)
                if g >= 2:
                    pe.wait_ge(w2_read, g - 1)
                for i in range(G):
                    mm = pe.matmul(ps_x[:, g % 2, i * E:(i + 1) * E], weight_t[:, g % 2, i * P:(i + 1) * P], remap[:, :],
                                   start=True, stop=True)
                mm.then_inc(w2_ok, 1)

            for g in range(N // G):
                if g >= 2:
                    pe.wait_ge(wt_read, g - 1)
                for i in range(G):
                    mm = pe.transpose(ps_w[0:E, g % 2, i * P:(i + 1) * P], prob[:, g * G + i, :], ident[:, :])
                mm.then_inc(wt_ok, 1)
                if g >= 1:
                    remapped(g - 1)
            remapped(N // G - 1)
            pe.wait_ge(routed_ok, 1)
            for r in range(N // R):
                if r >= 2:
                    pe.wait_ge(rank_read, r - 1)
                a = slice(r * R, (r + 1) * R)
                pe.matmul(ps_k[:, r % 2, :], before16[:, :], routed16[:, a, :].rearrange("p n e -> p (n e)"), start=True, stop=False)
                pe.matmul(ps_k[:, r % 2, :], ones16[:, :], so_far16[:, a, :].rearrange("p n e -> p (n e)"),
                          start=False, stop=True).then_inc(rank_ok, 1)
            pe.matmul(ps_n[:, 0:E], ones16[:, :], so_far16[:, N, :], start=True, stop=True).then_inc(rank_ok, 1)

        @block.vector
        def _(dve):
            done = [0]

            def after(ins):
                done[0] += 1
                ins.then_inc(step, 1)
                dve.wait_ge(step, done[0])

            def each(ap, n):
                return ap.unsqueeze(2).broadcast_to([P, N, n])

            for n in range(N):
                ins = dve.max(top[:, n, :], logits[:, n, :])
            after(ins)
            dve.tensor_tensor(prob[:, :, :], logits[:, :, :], each(top[:, :, 0], E), ALU.subtract).then_inc(z_ok, 1)
            for n in range(N):
                dve.max_index(top_i[:, n, :], top[:, n, :], logits[:, n, :])
                ins = dve.match_replace(rest[:, n, :], top[:, n, :], logits[:, n, :], -3e38)
            after(ins)
            dve.tensor_copy(top_f[:, :, :], top_i[:, :, :])
            after(dve.tensor_tensor(rest[:, :, :], rest[:, :, :], logits[:, :, :], ALU.not_equal))
            dve.wait_ge(exp_ok, 1)
            after(dve.tensor_reduce(sums[:, 0, :], prob[:, :, :], AX.X, ALU.add))
            after(dve.reciprocal(sums[:, 1, :], sums[:, 0, :]))
            after(dve.tensor_tensor(prob[:, :, :], prob[:, :, :], each(sums[:, 1, :], E), ALU.mult))
            after(dve.tensor_tensor(prob[:, :, :], prob[:, :, :], rest[:, :, :], ALU.mult))
            after(dve.tensor_reduce(sums[:, 2, :], prob[:, :, :], AX.X, ALU.add))
            after(dve.tensor_scalar(sums[:, 2, :], sums[:, 2, :], 1e-12, None, ALU.max))
            after(dve.reciprocal(sums[:, 3, :], sums[:, 2, :]))
            after(dve.tensor_tensor(prob[:, :, :], prob[:, :, :], each(sums[:, 3, :], E), ALU.mult))
            dve.wait_ge(made, 11)
            experts = iota_e[:, :].unsqueeze(1).broadcast_to([P, N, E])
            after(dve.tensor_tensor(first[:, :, :], experts, each(top_f[:, :, 0], E), ALU.is_equal))
            for k in range(1, SELK):
                after(dve.tensor_tensor(hit[:, :, :], experts, each(top_f[:, :, k], E), ALU.is_equal))
                after(dve.tensor_tensor(first[:, :, :], first[:, :, :], hit[:, :, :], ALU.add))
            after(dve.tensor_tensor(hit[:, :, :], rest[:, :, :], first[:, :, :], ALU.subtract))
            with nc.allow_low_precision(reason="counts up to 32 are exact in bfloat16"):
                dve.tensor_reduce(picked[:, 0, :], first[:, :, :].rearrange("p n e -> p e n"), AX.X, ALU.add)
                dve.tensor_reduce(picked[:, 1, :], hit[:, :, :].rearrange("p n e -> p e n"), AX.X, ALU.add).then_inc(picked_ok, 1)
            dve.wait_ge(votes_ok, 1)
            dve.wait_ge(sim_ok, 1)
            after(dve.tensor_scalar(is_first[:, :], ps_n[0:E, 0:E], 0.5, None, ALU.is_ge))
            after(dve.copy_predicated(cand[:, :], is_first[:, :], sim[:, :]))
            after(dve.max(best[:, :], cand[:, :]))
            after(dve.max_index(best_i[:, :], best[:, :], cand[:, :]))
            dve.tensor_copy(s1[:, 0:1], best_i[:, 0:1])
            dve.tensor_scalar(s1[:, 1:2], ps_n[0:E, E:E + 1], 0.5, None, ALU.is_lt)
            dve.tensor_scalar(s1[:, 2:3], ps_n[0:E, E + 1:E + 2], 0.5, None, ALU.is_ge)
            after(dve.tensor_scalar(s1[:, 3:4], best[:, 0:1], 0.5, None, ALU.is_ge))
            dve.tensor_tensor(s1[:, 4:5], s1[:, 0:1], place[:, :], ALU.subtract)
            after(dve.tensor_tensor(s1[:, 5:6], s1[:, 1:2], s1[:, 2:3], ALU.mult))
            after(dve.tensor_tensor(s1[:, 5:6], s1[:, 5:6], s1[:, 3:4], ALU.mult))
            after(dve.tensor_tensor(s1[:, 4:5], s1[:, 4:5], s1[:, 5:6], ALU.mult))
            after(dve.tensor_tensor(s1[:, 6:7], s1[:, 4:5], place[:, :], ALU.add))
            dve.tensor_scalar(remap[:, :], iota_e[0:E, :], s1[:, 6:7], None, ALU.is_equal).then_inc(remap_ok, 1)
            for g in range(N // G):
                dve.wait_ge(w2_ok, g + 1)
                dve.tensor_copy(weight[:, g * G:(g + 1) * G, :],
                                ps_x[:, g % 2, 0:G * E].rearrange("p (n e) -> p n e", e=E)).then_inc(w2_read, 1)
            dve.wait_ge(w2_read, N // G)
            after(dve.tensor_scalar(routed16[:, :, :], weight[:, :, :], 0.0, None, ALU.is_gt))
            for n in range(N):
                ins = dve.tensor_tensor(so_far16[:, n + 1, :], so_far16[:, n, :], routed16[:, n, :], ALU.add)
                if n < N - 1:
                    after(ins)
            ins.then_inc(routed_ok, 1)
            for r in range(N // R):
                dve.wait_ge(rank_ok, r + 1)
                dve.tensor_copy(rank[:, :, r * R:(r + 1) * R],
                                ps_k[:, r % 2, :].rearrange("p (n e) -> p e n", e=E)).then_inc(rank_read, 1)
            dve.wait_ge(rank_ok, N // R + 1)
            after(dve.tensor_copy(count[:, :], ps_n[:, 0:E]))
            dve.wait_ge(rank_read, N // R)
            after(dve.tensor_scalar(part[:, :, :], rank[:, :, :], 7, None, ALU.arith_shift_right))
            dve.tensor_copy(hi16[:, 0:E, :], part[:, :, :])
            after(dve.tensor_scalar(count[:, :], count[:, :], P - 1, None, ALU.add))
            after(dve.tensor_scalar(part[:, :, :], rank[:, :, :], P - 1, None, ALU.bitwise_and))
            dve.scalar_tensor_tensor(out=lo16[:, 0:E, :], in0=part[:, :, :], scalar=1.0,
                                     in1=routed16[:, :, :].rearrange("p n e -> p e n"), op0=ALU.add, op1=ALU.mult)
            after(dve.tensor_scalar(count[:, :], count[:, :], 7, None, ALU.arith_shift_right))
            after(dve.tensor_scalar(blocks[:, :], count[:, :], 1.0, None, ALU.max))
            after(dve.tensor_tensor_scan(ends[:, :], zeros[:, :], blocks[:, :], 0.0, ALU.add, ALU.add))
            dve.tensor_copy(starts[:, 1:E + 1], ends[:, :])
            after(dve.tensor_copy(starts[:, E + 1:], ends[:, E - 1:E].broadcast_to([P, AHEAD])))


AHEAD = 3


def experts(nc, const, lo16, hi16, starts, w_gu, w_down, rows, out):
    ident, passed = const[0], const[-1]
    N = B * TB
    W = 2 * P
    NGU, NDN = 4 * FB, 2 * FB
    OWN, POOL_DN = 1, 2 * (FB - 1)
    NHI, NLO = NGU + NDN - OWN, NGU + NDN - POOL_DN
    CHUNKS = 2 * FB
    with ExitStack() as scope:
        m = Memory(nc, scope)
        gu_raw = m.sb("gu_raw", [P, FB, HB * W])
        dn_raw = m.sb("dn_raw", [P, FB, H])
        gu_hi = m.sb("gu_hi", [P, FB, HB * W], F32R)
        gu_lo = m.sb("gu_lo", [P, FB, HB * W], F32R)
        dn_hi = m.sb("dn_hi", [P, FB, H], F32R)
        dn_lo = m.sb("dn_lo", [P, FB, H], F32R)
        x_rows = m.sb("x_rows", [P, H + E])
        xe_hi = m.sb("xe_hi", [P, H], F32R)
        xe_lo = m.sb("xe_lo", [P, H], F32R)
        silu = m.sb("silu", [P, FB, P])
        act_h = m.sb("act_h", [P, FB, P])
        ht_hi = m.sb("ht_hi", [P, FB, P], F32R)
        ht_lo = m.sb("ht_lo", [P, FB, P], F32R)
        y_out = m.sb("y_out", [P, H])
        w_next = m.sb("w_next", [P, E])
        w_now = m.sb("w_now", [P, 1])
        warm = m.sb("warm", [P, 1])
        gather_i = m.sb("gather_i", [P, 1], I32)
        scatter_i = m.sb("scatter_i", [P, 1], I32)
        table = m.sb("table", [P, 1 + N * TOPK + E + N], I32)
        own = m.sb("own", [P, 1])
        iota_lo = m.sb("iota_lo", [P, P], BF16)
        iota_hi = m.sb("iota_hi", [P, N], BF16)
        row_base = m.sb("row_base", [P, N, N], BF16)
        at_lo = m.sb("at_lo16", [P, N, P], BF16)
        at_hi = m.sb("at_hi16", [P, N, 2, N], BF16)
        found = m.sb("found", [P, 2, N])
        ps_gu = m.ps("ps_gu", [P, 2, BANK])
        ps_x1 = m.ps("ps_xe", [P, H])
        ps_y = m.ps("ps_y", [P, H])
        ps_h = m.ps("ps_h", [P, BANK])
        ps_l = m.ps("ps_l", [P, BANK])

        raw_in = [m.sem(f"raw_in{c}") for c in range(CHUNKS)]
        hi_ok, lo_ok, dn_lo_ok = m.sem("we_hi_ok"), m.sem("we_lo_ok"), m.sem("we_dn_lo_ok")
        own_hi = m.sem("we_own_hi")
        set_up = m.sem("set_up")
        mask_ok, list_a, list_ps, list_id, found_ok, list_ok = (
            m.sem(n) for n in ("mask_ok", "list_a", "list_ps", "list_id", "found_ok", "list_ok"))
        gidx_ok, rows_in, xe_ps, xe_hi_ok, xe_lo_ok, wn_ok = (m.sem(n) for n in ("gidx_ok", "rows_in", "xe_ps", "xe_hi_ok", "xe_lo_ok", "wn_ok"))
        gu_ok, silu_ok, h_ok, h_ps, ht_hi_ok, ht_lo_ok = (m.sem(n) for n in ("gu_ok", "silu_ok", "h_ok", "h_ps", "ht_hi_ok", "ht_lo_ok"))
        dn_ok, sidx_ok, y_ok, y_sent = (m.sem(n) for n in ("dn_ok", "sidx_ok", "y_ok", "y_sent"))
        wnow_ok = m.sem("wnow_ok")

        def start_of(eng, e):
            return eng.value_load(starts[0:1, bass.ds(e, 1)], min_val=0, max_val=N * TOPK + E)

        def for_blocks(eng, body):
            with eng.Fori(0, E) as e:
                g0 = start_of(eng, e)
                g1 = start_of(eng, e + 1)
                body(e, g0, True)
                with eng.If(g1 - g0 > 1):
                    with eng.Fori(g0 + 1, g1) as g:
                        body(e, g, False)

        block = scope.enter_context(nc.Block())

        @block.sync
        def _(sp):
            def load(e, c):
                if c < FB:
                    sp.dma_start(gu_raw[:, c, :].rearrange("p (k c) -> p k c", c=W),
                                 w_gu[e, c].rearrange("(k p) c -> p k c", p=P)).then_inc(raw_in[c], 16)
                else:
                    sp.dma_start(dn_raw[:, c - FB, :], w_down[e, (c - FB) * P:(c - FB + 1) * P, :]).then_inc(raw_in[c], 16)

            for c in range(CHUNKS):
                load(0, c)
            with sp.Fori(1, E) as e:
                for c in range(CHUNKS):
                    if c < FB:
                        sp.wait_ge(lo_ok, (e - 1) * NLO + 4 * (c + 1))
                    elif c < CHUNKS - 1:
                        sp.wait_ge(dn_lo_ok, (e - 1) * POOL_DN + 2 * (c - FB + 1))
                    else:
                        sp.wait_ge(lo_ok, e * NLO)
                    load(e, c)

        @block.gpsimd
        def _(pool):
            pool.iota(own[:, :], [[1, 1]], base=0, channel_multiplier=1, allow_small_or_imprecise_dtypes=True).then_inc(set_up, 1)
            pool.iota(iota_lo[:, :], [[1, P]], base=1, channel_multiplier=0, allow_small_or_imprecise_dtypes=True).then_inc(set_up, 1)
            pool.iota(iota_hi[:, :], [[1, N]], base=0, channel_multiplier=0, allow_small_or_imprecise_dtypes=True).then_inc(set_up, 1)
            pool.iota(row_base[:, :, :], [[P, N], [0, N]], base=P, channel_multiplier=0, allow_small_or_imprecise_dtypes=True).then_inc(set_up, 1)
            pool.iota(table[:, :], [[0, table.shape[1]]], base=0, channel_multiplier=1).then_inc(set_up, 1)
            pool.iota(scatter_i[:, :], [[0, 1]], base=0, channel_multiplier=1).then_inc(set_up, 1)

            def gather(n):
                pool.wait_ge(gidx_ok, n + 1)
                if not (isinstance(n, int) and n == 0):
                    pool.wait_ge(wn_ok, n)
                stand_alone(pool, passed)
                pool.indirect_dma_start(x_rows[:, :], None, rows, bass.IndirectOffsetOnAxis(ap=gather_i[:, 0:1], axis=0)).then_inc(rows_in, 16)

            gather(0)
            gather(1)

            def body(e, g, first):
                pool.wait_ge(y_ok, g + 1)
                pool.wait_ge(sidx_ok, g + 1)
                stand_alone(pool, passed)
                pool.indirect_dma_start(out, bass.IndirectOffsetOnAxis(ap=scatter_i[:, 0:1], axis=0), y_out[:, :], None,
                                        compute_op=ALU.add).then_inc(y_sent, 16)
                if first:
                    for n in range(POOL_DN):
                        pool.wait_ge(hi_ok, e * NHI + NGU - OWN + n + 1)
                        f, a = n // 2, slice(n % 2 * BANK, (n % 2 + 1) * BANK)
                        pool.tensor_tensor(dn_lo[:, f, a], dn_raw[:, f, a], raw(dn_hi[:, f, a]), ALU.subtract).then_inc(dn_lo_ok, 1)
                gather(g + 2)

            for_blocks(pool, body)
            total = start_of(pool, E)
            pool.wait_ge(y_ok, total + 1)
            pool.wait_ge(sidx_ok, total + 1)
            stand_alone(pool, passed)
            pool.indirect_dma_start(out, bass.IndirectOffsetOnAxis(ap=scatter_i[:, 0:1], axis=0), y_out[:, :], None,
                                    compute_op=ALU.add).then_inc(y_sent, 16)
            pool.wait_ge(y_sent, (total + 1) * 16)
            pool.wait_ge(rows_in, (total + 2) * 16)

        @block.tensor
        def _(pe):
            def split_product(out, a_hi, a_lo, w_hi, w_lo, first, last):
                pe.matmul(out, a_hi, w_hi, start=first, stop=False)
                pe.matmul(out, a_hi, w_lo, start=False, stop=False)
                return pe.matmul(out, a_lo, w_hi, start=False, stop=last)

            def find_rows(n):
                pe.wait_ge(list_a, n + 1)
                pe.wait_ge(list_id, n)
                for i in range(N):
                    mm = pe.matmul(ps_l[:, 0:2 * N], at_lo[:, i, :], at_hi[:, i, :, :].rearrange("p a h -> p (a h)"),
                                   start=(i == 0), stop=(i == N - 1))
                mm.then_inc(list_ps, 1)

            def turn_rows(n):
                pe.wait_ge(rows_in, (n + 1) * 16)
                pe.wait_ge(xe_lo_ok, n * 2)
                for k in range(HB):
                    mm = pe.transpose(ps_x1[:, k * P:(k + 1) * P], x_rows[:, k * P:(k + 1) * P], ident[:, :])
                mm.then_inc(xe_ps, 1)

            find_rows(0)
            turn_rows(0)
            for n in range(1, AHEAD):
                find_rows(n)
            pe.wait_ge(set_up, 9)
            for k in range(HB):
                mm = pe.transpose(ps_y[:, k * P:(k + 1) * P], y_out[:, k * P:(k + 1) * P], ident[:, :])
            mm.then_inc(dn_ok, 1)

            def body(e, g, first):
                def first_layer(f):
                    pe.wait_ge(xe_lo_ok, g * 2 + 2)
                    if f == 2:
                        pe.wait_ge(h_ok, g * FB + 1)
                    else:
                        pe.wait_ge(h_ok, g * FB)
                    gw = slice(0, W)
                    for k in range(HB):
                        if first and k % 2 == 0:
                            pe.wait_ge(lo_ok, e * NLO + 4 * f + k // 2 + 1)
                        a = slice(k * P, (k + 1) * P)
                        c = slice(k * W, (k + 1) * W)
                        mm = split_product(ps_gu[:, f % 2, gw], xe_hi[:, a], xe_lo[:, a], gu_hi[:, f, c], gu_lo[:, f, c], k == 0, k == HB - 1)
                    mm.then_inc(gu_ok, 1)

                def turn_h(f):
                    pe.wait_ge(h_ok, g * FB + f + 1)
                    pe.wait_ge(ht_lo_ok, g * FB + f)
                    pe.transpose(ps_h[:, f * P:(f + 1) * P], act_h[:, f, :], ident[:, :]).then_inc(h_ps, 1)

                def second_layer(f):
                    pe.wait_ge(ht_lo_ok, g * FB + f + 1)
                    if f == 0:
                        pe.wait_ge(y_ok, g + 1)
                    for c in range(H // BANK):
                        if first:
                            if 2 * f < POOL_DN:
                                pe.wait_ge(dn_lo_ok, e * POOL_DN + 2 * f + c + 1)
                            else:
                                pe.wait_ge(lo_ok, e * NLO + NGU + 2 * f - POOL_DN + c + 1)
                        n = slice(c * BANK, (c + 1) * BANK)
                        mm = split_product(ps_y[:, n], ht_hi[:, f, :], ht_lo[:, f, :], dn_hi[:, f, n], dn_lo[:, f, n], f == 0, f == FB - 1)
                    if f == FB - 1:
                        mm.then_inc(dn_ok, 1)

                first_layer(0)
                first_layer(1)
                if first:
                    find_rows(e + AHEAD)
                turn_h(0)
                first_layer(2)
                turn_h(1)
                turn_rows(g + 1)
                turn_h(2)
                second_layer(0)
                second_layer(1)
                second_layer(2)

            for_blocks(pe, body)

        @block.scalar
        def _(act):
            def split_rows(n):
                act.wait_ge(xe_ps, n + 1)
                act.wait_ge(gu_ok, n * FB)
                for c in range(2):
                    a = slice(c * BANK, (c + 1) * BANK)
                    act.activation(xe_hi[:, a], ps_x1[:, a], ACT.Copy).then_inc(xe_hi_ok, 1)

            act.wait_ge(set_up, 9)
            split_rows(0)

            def finish(n):
                act.wait_ge(dn_ok, n + 1)
                act.wait_ge(sidx_ok, n + 1)
                act.wait_ge(y_sent, n * 16)
                act.activation(y_out[:, :], ps_y[:, :], ACT.Copy, scale=w_now[:, 0:1]).then_inc(y_ok, 1)

            def body(e, g, first):
                def split(kind, f):
                    c = f if kind == "gu" else FB + f
                    act.wait_ge(raw_in[c], e * 16 + 16)
                    if kind == "gu":
                        act.wait_ge(gu_ok, g * FB)
                        for q in range(OWN if f == 0 else 0, 4):
                            a = slice(q * 2 * W, (q + 1) * 2 * W)
                            act.activation(gu_hi[:, f, a], gu_raw[:, f, a], ACT.Copy).then_inc(hi_ok, 1)
                    else:
                        act.wait_ge(dn_ok, g + 1)
                        for q in range(2):
                            a = slice(q * BANK, (q + 1) * BANK)
                            act.activation(dn_hi[:, f, a], dn_raw[:, f, a], ACT.Copy).then_inc(hi_ok, 1)

                def silu_of(f):
                    act.wait_ge(gu_ok, g * FB + f + 1)
                    act.wait_ge(h_ok, g * FB)
                    act.activation(silu[:, f, :], ps_gu[:, f % 2, 0:P], ACT.Silu).then_inc(silu_ok, 1)

                def split_h(f):
                    act.wait_ge(h_ps, g * FB + f + 1)
                    act.wait_ge(dn_ok, g + 1)
                    act.activation(ht_hi[:, f, :], ps_h[:, f * P:(f + 1) * P], ACT.Copy).then_inc(ht_hi_ok, 1)

                if first:
                    act.activation(warm[:, :], warm[:, :], ACT.Silu)
                    split("gu", 0)
                    split("gu", 1)
                finish(g)
                silu_of(0)
                if first:
                    split("gu", 2)
                silu_of(1)
                split_h(0)
                if first:
                    split("dn", 0)
                silu_of(2)
                split_h(1)
                if first:
                    split("dn", 1)
                split_h(2)
                if first:
                    split("dn", 2)
                split_rows(g + 1)

            for_blocks(act, body)
            finish(start_of(act, E))

        @block.vector
        def _(dve):
            dve.memset(y_out[:, :], 0.0).then_inc(set_up, 1)
            dve.memset(w_next[:, :], 0.0).then_inc(set_up, 1)
            dve.memset(warm[:, :], 0.0).then_inc(set_up, 1)
            dve.memset(w_now[:, :], 0.0).then_inc(sidx_ok, 1)
            dve.wait_ge(set_up, 9)

            LIST_PARTS = 4

            def start_list(n):
                dve.wait_ge(list_ps, n)
                hi = hi16[:, bass.ds(n, 1), :].rearrange("p a n -> p (a n)").unsqueeze(2)
                dve.tensor_tensor(at_hi[:, :, 1, :], iota_hi[:, :].unsqueeze(1).broadcast_to([P, N, N]),
                                  hi.broadcast_to([P, N, N]), ALU.is_equal).then_inc(mask_ok, 1)

            def list_part(n, part):
                a, w = part * N // LIST_PARTS, N // LIST_PARTS
                lo = lo16[:, bass.ds(n, 1), a:a + w].rearrange("p a n -> p (a n)").unsqueeze(2)
                dve.tensor_tensor(at_lo[:, a:a + w, :], iota_lo[:, :].unsqueeze(1).broadcast_to([P, w, P]),
                                  lo.broadcast_to([P, w, P]), ALU.is_equal)

            def end_list(n):
                dve.wait_ge(mask_ok, n * 2 + 1)
                dve.tensor_scalar(at_hi[:, :, 0, :], at_hi[:, :, 1, :], own[:, 0:1], None, ALU.mult).then_inc(mask_ok, 1)
                dve.wait_ge(mask_ok, n * 2 + 2)
                dve.tensor_tensor(at_hi[:, :, 1, :], at_hi[:, :, 1, :], row_base[:, :, :], ALU.mult).then_inc(list_a, 1)

            def make_list(n):
                start_list(n)
                for part in range(LIST_PARTS):
                    list_part(n, part)
                end_list(n)

            def finish_list(n):
                dve.wait_ge(list_ps, n + 1)
                dve.tensor_reduce(found[:, 0, :], ps_l[:, 0:2 * N].rearrange("p (a h) -> p h a", a=2), AX.X, ALU.add).then_inc(list_id, 1)
                dve.wait_ge(list_id, n + 1)
                dve.tensor_scalar(found[:, 1, :], found[:, 0, :], 0.0, own[:, 0:1], ALU.is_equal, ALU.mult).then_inc(found_ok, 1)
                dve.wait_ge(found_ok, n + 1)
                at = start_of(dve, n)
                dve.tensor_tensor(table[:, bass.ds(at + 1, N)], found[:, 0, :], found[:, 1, :], ALU.add).then_inc(list_ok, 1)
                dve.wait_ge(list_ok, n + 1)

            def gather_index(n):
                if not (isinstance(n, int) and n == 0):
                    dve.wait_ge(rows_in, n * 16)
                dve.tensor_copy(gather_i[:, :], table[:, bass.ds(n + 1, 1)]).then_inc(gidx_ok, 1)

            def rest_of_rows(n):
                for c in range(2):
                    dve.wait_ge(xe_hi_ok, n * 2 + c + 1)
                    a = slice(c * BANK, (c + 1) * BANK)
                    dve.tensor_tensor(xe_lo[:, a], ps_x1[:, a], raw(xe_hi[:, a]), ALU.subtract).then_inc(xe_lo_ok, 1)

            def keep_weights(n):
                dve.wait_ge(xe_ps, n + 1)
                dve.tensor_copy(w_next[:, :], x_rows[:, H:H + E]).then_inc(wn_ok, 1)

            make_list(0)
            finish_list(0)
            gather_index(0)
            make_list(1)
            keep_weights(0)
            finish_list(1)
            gather_index(1)
            rest_of_rows(0)
            for n in range(2, AHEAD):
                make_list(n)
                finish_list(n)
            make_list(AHEAD)

            def body(e, g, first):
                def rest_of(f):
                    for q in range(4):
                        a = slice(q * BANK, (q + 1) * BANK)
                        if 4 * f + q < OWN:
                            dve.wait_ge(raw_in[0], e * 16 + 16)
                            dve.wait_ge(gu_ok, g * FB)
                            dve.tensor_copy(gu_hi[:, f, a], gu_raw[:, f, a]).then_inc(own_hi, 1)
                            dve.wait_ge(own_hi, e * OWN + q + 1)
                        else:
                            dve.wait_ge(hi_ok, e * NHI + 4 * f + q - OWN + 1)
                        dve.tensor_tensor(gu_lo[:, f, a], gu_raw[:, f, a], raw(gu_hi[:, f, a]), ALU.subtract).then_inc(lo_ok, 1)

                def rest_of_dn(n):
                    dve.wait_ge(hi_ok, e * NHI + NGU - OWN + n + 1)
                    f, a = n // 2, slice(n % 2 * BANK, (n % 2 + 1) * BANK)
                    dve.tensor_tensor(dn_lo[:, f, a], dn_raw[:, f, a], raw(dn_hi[:, f, a]), ALU.subtract).then_inc(lo_ok, 1)

                def multiply(f):
                    dve.wait_ge(silu_ok, g * FB + f + 1)
                    dve.wait_ge(h_ps, g * FB)
                    dve.tensor_tensor(act_h[:, f, :], ps_gu[:, f % 2, P:W], silu[:, f, :], ALU.mult).then_inc(h_ok, 1)

                def rest_of_h(f):
                    dve.wait_ge(ht_hi_ok, g * FB + f + 1)
                    dve.tensor_tensor(ht_lo[:, f, :], ps_h[:, f * P:(f + 1) * P], raw(ht_hi[:, f, :]), ALU.subtract).then_inc(ht_lo_ok, 1)

                after = e + AHEAD + 1
                if first:
                    rest_of(0)
                    rest_of(1)
                multiply(0)
                if first:
                    rest_of(2)
                multiply(1)
                rest_of_h(0)
                if first:
                    start_list(after)
                    list_part(after, 0)
                multiply(2)
                rest_of_h(1)
                if first:
                    list_part(after, 1)
                rest_of_h(2)
                if first:
                    for n in range(POOL_DN, NDN):
                        rest_of_dn(n)
                dve.wait_ge(y_ok, g + 1)
                dve.wait_ge(wn_ok, g + 1)
                stand_alone(dve, passed)
                dve.tensor_copy(w_now[:, :], w_next[:, bass.ds(e, 1)]).then_inc(wnow_ok, 1)
                dve.wait_ge(wnow_ok, g + 1)
                keep_weights(g + 1)
                gather_index(g + 2)
                rest_of_rows(g + 1)
                dve.wait_ge(y_sent, (g + 1) * 16)
                dve.tensor_copy(scatter_i[:, :], table[:, bass.ds(g + 1, 1)]).then_inc(sidx_ok, 1)
                if first:
                    finish_list(e + AHEAD)
                    for part in range(2, LIST_PARTS):
                        list_part(after, part)
                    end_list(after)

            for_blocks(dve, body)


def rope_tables():
    inv = 1.0 / 10000.0 ** (np.arange(0, HD, 2, dtype=np.float32) / HD)
    freqs = np.einsum("i,j->ij", np.arange(S, dtype=np.float32), inv)
    emb = np.concatenate((freqs, freqs), axis=-1)
    c, s = np.cos(emb).astype(np.float32), np.sin(emb).astype(np.float32)
    s[:, :HD // 2] *= -1
    scale = np.float32(HD ** -0.5)
    c = c[:, :HD // 2]
    return (np.ascontiguousarray(np.stack([c * scale, c], 1)), np.ascontiguousarray(np.stack([s * scale, s], 1)))


def host_layout(i):
    i = {n: np.asarray(a) for n, a in i.items()}
    qkv = np.stack([i[f"L0_attn_W{n}"].T.reshape(H, NP, P) for n in "qkv"], 2)
    cos, sin = rope_tables()
    tidy = np.ascontiguousarray
    return {
        "x": i["x"],
        "wqkv": tidy(qkv.transpose(1, 0, 2, 3).reshape(NP, H, 3 * P)),
        "cos": cos, "sin": sin,
        "wo": tidy(i["L0_attn_Wo"].T),
        "ctx_t": tidy(i["ctx_1024"].transpose(0, 2, 1)),
        "xw": tidy(np.concatenate([i["L0_xattn_Wq"].T, i["L0_xattn_Wk"].T], 1)),
        "xbias": tidy(np.stack([i["L0_xattn_bq"], i["L0_xattn_bk"]], 1)),
        "gate": tidy(i["L0_ffn_gate_weight"].T),
        "similarity": i["L0_ffn_similarity"],
        "w_gu": tidy(i["L0_ffn_gate_up_proj"].reshape(E, 2, FB, P, H).transpose(0, 2, 4, 1, 3).reshape(E, FB, H, 2 * P)),
        "w_down": tidy(i["L0_ffn_down_proj"].transpose(0, 2, 1)),
    }


def build(nc, x, wqkv, cos, sin, wo, ctx_t, xw, xbias, gate, similarity, w_gu, w_down, out):
    attn_out = nc.dram_tensor("attn_out", (B, NP, P, S), F32, kind="Internal").ap()
    rows = nc.dram_tensor("rows", (P + B * S, H + E), F32, kind="Internal").ap()
    with ExitStack() as scope:
        m = Memory(nc, scope)
        const = constants(nc, m)
        self_attention(nc, const, x, wqkv, cos, sin, attn_out)
        logits = m.sb("logits", [P, B * TB, E])
        mix_features(nc, const, logits, x, attn_out, wo, ctx_t, xw, xbias, gate, rows, out)
        lo16 = m.sb("lo16", [P, E + AHEAD + 1, B * TB], BF16)
        hi16 = m.sb("hi16", [P, E + AHEAD + 1, B * TB], BF16)
        starts = m.sb("starts", [P, E + 1 + AHEAD], I32)
        route(nc, const, logits, lo16, hi16, starts, similarity, rows)
        experts(nc, const, lo16, hi16, starts, w_gu, w_down, rows, out)


def kernel(**inputs):
    import concourse.bacc as bacc
    from concourse.bass_utils import run_bass_kernel_spmd

    nc = bacc.Bacc("TRN2", target_bir_lowering=False, num_devices=1)
    arrays = host_layout(inputs)
    args = {n: nc.dram_tensor(n, a.shape, mybir.dt.from_np(a.dtype), kind="ExternalInput").ap() for n, a in arrays.items()}
    out = nc.dram_tensor("out", (P + B * S, H), F32, kind="ExternalOutput").ap()
    build(nc, **args, out=out)
    r = run_bass_kernel_spmd(nc, [arrays], core_ids=[0])
    return r.results[0]["out"][P:].reshape(B, S, H)
```

```python
from contextlib import ExitStack

import numpy as np
import concourse.bass as bass
from concourse import mybir

F32 = mybir.dt.float32
F32R = mybir.dt.float32r
BF16 = mybir.dt.bfloat16
I32 = mybir.dt.int32
U32 = mybir.dt.uint32
ALU = mybir.AluOpType
ACT = mybir.ActivationFunctionType
AX = mybir.AxisListType

P = 128
B, S, H = 4, 1024, 1024
NH, HD = 16, 64
HB = H // P
TB = S // P
NP = NH // 2
C, D = 512, 128
CB = C // P
E, TOPK, SELK, F = 64, 8, 4, 384
FB = F // P
BANK = 512
GQ = BANK // P
EPS = 1e-5
MASKED = -1e30
START = 1
LOADED = 16


class Memory:

    def __init__(self, nc, scope):
        self.nc, self.scope, self.sems = nc, scope, []

    def sb(self, name, shape, dt=F32):
        return self.scope.enter_context(self.nc.sbuf_tensor(name, shape, dt))

    def ps(self, name, shape, dt=F32):
        return self.scope.enter_context(self.nc.psum_tensor(name, shape, dt))

    def sem(self, name):
        self.sems.append(self.dma_sem(name))
        return self.sems[-1]

    def dma_sem(self, name):
        return self.scope.enter_context(self.nc.semaphore(name))

    def start_counts(self):
        with self.nc.Block() as block:
            @block.gpsimd
            def _(pool):
                for sem in self.sems:
                    pool.sem_inc(sem, START)


def raw(ap):
    return ap.bitcast(F32)


def stand_alone(eng, passed):
    eng.sem_inc(passed, 1)


def constants(nc, m):
    ident = m.sb("ident", [P, P])
    ident16 = m.sb("ident16", [P, P], BF16)
    mask16 = m.sb("mask16", [P, P], BF16)
    half = m.sb("minus_half", [P, TB])
    made = m.sem("const_made")
    passed = m.sem("passed")
    with nc.Block() as block:
        @block.gpsimd
        def _(pool):
            pool.memset(ident[:, :], 0.0).then_inc(made, 1)
            pool.memset(ident16[:, :], 0.0).then_inc(made, 1)
            pool.memset(mask16[:, :], 0.0).then_inc(made, 1)
            pool.memset(half[:, :], -0.5).then_inc(made, 1)
            pool.wait_ge(made, 4)
            for t in (ident, ident16):
                pool.affine_select(out=t[:, :], in_=t[:, :], compare_op=ALU.not_equal, fill=1.0,
                                   base=0, pattern=[[-1, P]], channel_multiplier=1).then_inc(made, 1)
            pool.affine_select(out=mask16[:, :], in_=mask16[:, :], compare_op=ALU.is_ge, fill=MASKED,
                               base=0, pattern=[[-1, P]], channel_multiplier=1).then_inc(made, 1)
            pool.wait_ge(made, 7)
    return ident, ident16, mask16, half, passed


def self_attention(nc, const, x, wqkv, cos, sin, attn_out):
    ident, ident16, mask16, half, passed = const
    W = 3 * P
    UNITS = [(h, g) for h in range(2) for g in range(S // BANK)]
    NU = len(UNITS)
    KB = [GQ * (g + 1) for _, g in UNITS]
    STEPS = [(u, kb) for u in range(NU) for kb in range(KB[u])]
    NS = len(STEPS)
    PER = NS // TB
    NQ = GQ * NU
    PARTS = [range(0, 3 * HB // 2), range(3 * HB // 2, 9 * HB // 4), range(9 * HB // 4, 3 * HB)]
    SLOTS = 4
    W_OF_STEP = {NS - 2: (2, (0, 1)), NS - 1: (2, (2, 3)), 0: (1, (4, 5)), 1: (1, (6, 7))}
    XS = GQ
    NT = NS + TB

    def steps_from(u):
        return sum(KB[:u])

    def next_queries(s, last):
        u, kb = STEPS[s]
        if KB[u] == GQ:
            then = [(u + 1, kb + 1)] if kb + 1 < GQ else []
        else:
            then = [(u + 1, kb // 2)] if kb % 2 == 0 else [(u + 2, 0)] if kb == KB[u] - 1 else []
        return [(unit // NU, unit % NU, i) for unit, i in then if unit < NU or not last]

    def tile_order(last):
        order = []
        for s in range(NS):
            order.append(("probs", s))
            if s % PER == 1 and (s < PER or not last):
                order.append(("qk", s // PER))
        return {key: i for i, key in enumerate(order)}

    with ExitStack() as scope:
        m = Memory(nc, scope)
        stats = m.sb("ln1_stats", [P, TB, 2, 6])
        mean_var = m.sb("ln1_mean_var", [P, TB, 2])
        rstd = m.sb("ln1_rstd", [P, TB])
        xt_hi = m.sb("xt_hi", [P, HB, S], F32R)
        xt_lo = m.sb("xt_lo", [P, HB, S], F32R)
        w_raw = m.sb("w_raw", [P, SLOTS, W])
        w_hi = m.sb("w_hi", [P, HB, W], F32R)
        w_lo = m.sb("w_lo", [P, HB, W], F32R)
        cos_sb = m.sb("cos_sb", [P, TB, 2, HD // 2])
        sin_sb = m.sb("sin_sb", [P, TB, 2, HD])
        r_cos = m.sb("r_cos", [P, 4, HD])
        r_sin = m.sb("r_sin", [P, 4, HD])
        rotated = m.sb("rotated", [P, 4, 2, HD])
        qk_hi = [m.sb(f"qk_hi{i}", [P, 4, S], F32R) for i in range(2)]
        q_lo = [m.sb(f"q_lo{i}", [P, 2, S], F32R) for i in range(2)]
        v = [m.sb(f"v{i}", [P, TB, 2, 2, HD], F32R) for i in range(2)]
        neg_max = m.sb("neg_max", [P, NQ])
        row_sum = m.sb("row_sum", [P, NQ])
        inv_sum = m.sb("inv_sum", [P, NQ])
        probs = [m.sb(f"probs{g}", [P, GQ, BANK * (g + 1)]) for g in range(S // BANK)]
        first_load = m.sb("first_load", [2, 1])
        x_tile = probs[1]
        pt_hi = m.sb("pt_hi", [P, 2, BANK], F32R)
        pt_lo = m.sb("pt_lo", [P, 2, BANK], F32R)
        out_t = m.sb("out_t", [P, 2, BANK])
        ps_s = m.ps("ps_s", [P, 2, 2 * BANK])
        ps_t = m.ps("ps_t", [P, 2, BANK])
        ps_o = m.ps("ps_o", [P, BANK])
        ps_qkv = m.ps("ps_qkv", [P, BANK])

        x_in = [m.sem(f"x_in{i}") for i in range(XS)]
        w_in = [m.sem(f"w_in{i}") for i in range(SLOTS)]
        tab_in = m.sem("tab_in")
        ln_step, ln_eps, ln_rstd = m.sem("ln_step"), m.sem("ln_eps"), m.sem("ln_rstd")
        xn_ok, xt_ok, xt_hi_ok, xt_lo_ok = (m.sem(n) for n in ("xn_ok", "xt_ok", "xt_hi_ok", "xt_lo_ok"))
        w_hi_ok, w_lo_ok, w_early = m.sem("w_hi_ok"), m.sem("w_lo_ok"), m.sem("w_early")
        qkv_ok, qkv_read = m.sem("qkv_ok"), m.sem("qkv_read")
        v_hi_ok, rot_step, rot_ok = m.sem("v_hi_ok"), m.sem("rot_step"), m.sem("rot_ok")
        tile_ok, tile_hi_ok, tile_lo_ok = m.sem("tile_ok"), m.sem("tile_hi_ok"), m.sem("tile_lo_ok")
        s_ok, max_ok, exp_ok = m.sem("s_ok"), m.sem("max_ok"), m.sem("exp_ok")
        inv_ok, norm_ok, pv_ok = m.sem("inv_ok"), m.sem("norm_ok"), m.sem("pv_ok")
        o_half, o_ok, o_out = m.sem("o_half"), m.sem("o_ok"), [m.dma_sem(f"o_out{i}") for i in range(2)]

        def first_tile(j):
            return j * NT + TB - 1

        ROUNDS = TB + 3
        FIRST_SCORES = {TB + 1: (0, 1), TB + 2: (2, 3, 4)}

        def for_pairs(eng, prologue, attention, drain):
            with eng.Fori(0, B) as b:
                j = b * NP
                prologue(b, j)
                attention(j, 0, True, False)
                with eng.Fori(0, (NP - 2) // 2) as two:
                    attention(j + two * 2 + 1, 1, False, False)
                    attention(j + two * 2 + 2, 0, False, False)
                attention(j + (NP - 1), 1, False, True)
                drain(j + (NP - 1))

        m.start_counts()
        block = scope.enter_context(nc.Block())

        @block.sync
        def _(sp):
            def load_w(pair, k):
                sp.dma_start(w_raw[:, k % SLOTS, :], wqkv[pair, k * P:(k + 1) * P, :]).then_inc(w_in[k % SLOTS], 16)

            def first_w(j, pair):
                for k in range(SLOTS):
                    sp.wait_ge(w_lo_ok, START + (j - 1) * HB + k + SLOTS + 1)
                    load_w(pair, k)

            def rest_of_w(j, pair):
                for k in range(SLOTS, HB):
                    sp.wait_ge(w_lo_ok, START + j * HB + k - SLOTS + 1)
                    load_w(pair, k)

            sp.dma_start(cos_sb[:, :, :, :], cos.rearrange("(t p) a d -> p t a d", p=P)).then_inc(tab_in, 16)
            sp.dma_start(sin_sb[:, :, :, :], sin.rearrange("(t p) a d -> p t a d", p=P)).then_inc(tab_in, 16)
            for k in range(SLOTS):
                load_w(0, k)
            with sp.Fori(0, B) as b:
                for t in range(TB):
                    if t < XS:
                        sp.wait_ge(tile_ok, START + b * NP * NT)
                    else:
                        sp.wait_ge(xt_ok, START + b * TB + t - XS + 1)
                    sp.dma_start(x_tile[:, t % XS, :], x[b, t * P:(t + 1) * P, :]).then_inc(x_in[t % XS], 16)
                    if t == XS - 1:
                        rest_of_w(b * NP, 0)
                with sp.Fori(1, NP) as pair:
                    first_w(b * NP + pair, pair)
                    rest_of_w(b * NP + pair, pair)
                first_w(b * NP + NP, 0)
            for k in range(SLOTS):
                sp.wait_ge(w_in[k], START + 16 * (2 * B * NP + 1))

        @block.gpsimd
        def _(pool):
            for i in range(2):
                pool.dma_start(first_load[i:i + 1, :], cos[0:1, 0, 0:1]).then_inc(o_out[i], LOADED)

            def rest_of_w(j, k):
                pool.wait_ge(w_hi_ok, START + j * HB + k + 1)
                pool.tensor_tensor(w_lo[:, k, :], w_raw[:, k % SLOTS, :], raw(w_hi[:, k, :]), ALU.subtract).then_inc(w_lo_ok, 1)

            def find_rstd(b, t):
                pool.wait_ge(ln_step, START + (b * TB + t) * 3 + 3)
                stand_alone(pool, passed)
                pool.tensor_scalar(rstd[:, t:t + 1], mean_var[:, t, 1:2], EPS, 1.0, ALU.add, ALU.mult).then_inc(ln_eps, 1)
                pool.wait_ge(ln_eps, START + b * TB + t + 1)
                pool.tensor_tensor(rstd[:, t:t + 1], rstd[:, t:t + 1], half[:, 0:1], ALU.pow).then_inc(ln_rstd, 1)

            def prologue(b, j):
                find_rstd(b, 0)
                for t in range(1, TB):
                    find_rstd(b, t)
                    if SLOTS + 2 * t <= HB:
                        rest_of_w(j, SLOTS + 2 * t - 2)
                        rest_of_w(j, SLOTS + 2 * t - 1)
                for k in range(SLOTS):
                    rest_of_w(j + 1, k)

            def store(b, pair, u):
                h, g = UNITS[u]
                pool.wait_ge(o_ok, START + (b * NP + pair) * NU + u + 1)
                pool.dma_start(attn_out[b, pair, h * HD:(h + 1) * HD, g * BANK:(g + 1) * BANK],
                               out_t[h * HD:(h + 1) * HD, u % 2, :]).then_inc(o_out[u % 2], 16)

            for k in range(SLOTS):
                rest_of_w(0, k)
            with pool.Fori(0, B) as b:
                prologue(b, b * NP)
                for k in range(SLOTS, HB):
                    rest_of_w(b * NP + 1, k)
                for u in range(NU - 1):
                    store(b, 0, u)
                for k in range(SLOTS):
                    rest_of_w(b * NP + 2, k)
                with pool.Fori(1, NP - 1) as pair:
                    for k in range(SLOTS, HB):
                        rest_of_w(b * NP + pair + 1, k)
                    store(b, pair - 1, NU - 1)
                    for u in range(NU - 1):
                        store(b, pair, u)
                    for k in range(SLOTS):
                        rest_of_w(b * NP + pair + 2, k)
                store(b, NP - 2, NU - 1)
                for u in range(NU):
                    store(b, NP - 1, u)
            for i in range(2):
                pool.wait_ge(o_out[i], LOADED + 16 * B * NP * NU // 2)

        @block.tensor
        def _(pe):
            def turn_x(b, t):
                pe.wait_ge(xn_ok, START + b * TB + t + 1)
                if t >= 2:
                    pe.wait_ge(xt_lo_ok, START + b * TB + t - 1)
                for k in range(HB):
                    mm = pe.transpose(ps_s[:, t % 2, k * P:(k + 1) * P], x_tile[:, t % XS, k * P:(k + 1) * P], ident[:, :])
                mm.then_inc(xt_ok, 1)

            def qkv(j, t, part, out):
                for n in part:
                    k, term = divmod(n, 3)
                    if t == 0 and term == 0:
                        pe.wait_ge(w_lo_ok, START + j * HB + k + 1)
                    a = slice(t * P, (t + 1) * P)
                    xs, ws = ((xt_hi, w_hi), (xt_hi, w_lo), (xt_lo, w_hi))[term]
                    mm = pe.matmul(out, xs[:, k, a], ws[:, k, :], start=(n == 0), stop=(n == 3 * HB - 1))
                    if t == TB - 1 and n == 3 * SLOTS - 1:
                        mm.then_inc(w_early, 1)
                if part[-1] == 3 * HB - 1:
                    mm.then_inc(qkv_ok, 1)

            def turn_qk(j, t, start, at):
                pe.wait_ge(rot_ok, START + j * TB + t + 1)
                pe.wait_ge(tile_lo_ok, START + (start + (at - 1 if at >= 2 else 0)))
                for r in range(4):
                    mm = pe.transpose(ps_t[:, at % 2, r * P:(r + 1) * P], rotated[:, r, :, :].rearrange("p a d -> p (a d)"), ident[:, :])
                mm.then_inc(tile_ok, 1)

            def scores(j, slot, u, i):
                h, g = UNITS[u]
                n = GQ * u + i
                qb = GQ * g + i
                keys = P * (qb + 1)
                for c in range(0, keys, BANK):
                    w = max(min(BANK, keys - c), 2 * P)
                    out = ps_s[:, n % 2, c:c + w]
                    pe.matmul(out, qk_hi[slot][:, h, qb * P:(qb + 1) * P], qk_hi[slot][:, 2 + h, c:c + w],
                              start=True, stop=False, skip_group_check=True)
                    pe.matmul(out, q_lo[slot][:, h, qb * P:(qb + 1) * P], qk_hi[slot][:, 2 + h, c:c + w],
                              start=False, stop=True, skip_group_check=True)
                mm = pe.matmul(ps_s[:, n % 2, qb * P:(qb + 1) * P], ident16[:, :], mask16[:, :],
                               start=False, stop=True, skip_group_check=True)
                mm.then_inc(s_ok, 1)

            def prologue(b, j):
                pe.wait_ge(exp_ok, START + j * NQ)
                pe.wait_ge(qkv_read, START + j * TB)
                pe.wait_ge(o_ok, START + j * NU)
                for i in range(ROUNDS):
                    if i < TB:
                        turn_x(b, i)
                    if i >= 4:
                        turn_qk(j, i - 4, j * NT, i - 4)
                    t = i - 2
                    if 0 <= t < TB:
                        pe.wait_ge(xt_lo_ok, START + b * TB + t + 1)
                        stand_alone(pe, passed)
                        if t >= 2:
                            pe.wait_ge(qkv_read, START + j * TB + t - 1)
                        qkv(j, t, range(3 * HB), (ps_qkv if t % 2 else ps_o)[:, 0:W])
                    for n in FIRST_SCORES.get(i, ()):
                        pe.wait_ge(tile_lo_ok, START + j * NT + n + 1 + (n % GQ == 0))
                        if n >= 2:
                            pe.wait_ge(exp_ok, START + j * NQ + n - 1)
                        scores(j, 0, n // GQ, n % GQ)

            def weigh_values(j, slot, s, tile):
                u, kb = STEPS[s]
                h, g = UNITS[u]
                pe.wait_ge(tile_lo_ok, START + tile)
                if kb == 0:
                    pe.wait_ge(o_ok, START + j * NU + u)
                off = P * max(0, kb - GQ * g)
                both = v[slot][:, kb, h, :, :].rearrange("p a d -> p (a d)")
                pe.matmul(ps_o[:, off:], both, pt_hi[:, s % 2, off:], start=(kb == 0), stop=False, skip_group_check=True)
                pe.matmul(ps_o[:, off:], both, pt_lo[:, s % 2, off:], start=False, stop=True,
                          skip_group_check=True).then_inc(pv_ok, 1)

            def attention(j, slot, first, last):
                tiles = tile_order(last)
                for s, (u, kb) in enumerate(STEPS):
                    h, g = UNITS[u]
                    group, place = divmod(s, PER)
                    if kb == 0:
                        pe.wait_ge(norm_ok, START + j * NQ + GQ * (u + 1))
                    at = tiles["probs", s]
                    pe.wait_ge(tile_lo_ok, START + first_tile(j) + (at - 1))
                    for i in range(max(0, kb - GQ * g), GQ):
                        mm = pe.transpose(ps_t[:, (TB - 1 + at) % 2, i * P:(i + 1) * P], probs[g][:, i, kb * P:(kb + 1) * P], ident[:, :])
                    mm.then_inc(tile_ok, 1)
                    for ahead, unit, i in next_queries(s, last):
                        if unit == 1 and not ahead:
                            pe.wait_ge(tile_lo_ok, START + (first_tile(j) + (tiles["qk", 0] + 1 if i == GQ - 1 else 0)))
                        elif unit == 1:
                            pe.wait_ge(tile_lo_ok, START + first_tile(j) + tiles["qk", GQ + 1] + 1)
                        elif unit == 0 and i == 0:
                            pe.wait_ge(tile_lo_ok, START + first_tile(j) + tiles["qk", GQ] + 1)
                        pe.wait_ge(exp_ok, START + (j + ahead) * NQ + GQ * unit + i - 1)
                        scores(j + ahead, (slot + ahead) % 2, unit, i)
                    if 0 < s and place < PER - 1:
                        weigh_values(j, slot, s - 1, first_tile(j) + tiles["probs", s - 1] + 1)
                    elif s == 0 and not first:
                        weigh_values(j - 1, 1 - slot, NS - 1, first_tile(j))
                    if place == 1 and group == 0:
                        turn_qk(j, TB - 1, j * NT, TB - 1 + tiles["qk", 0])
                    elif place == 1 and not last:
                        turn_qk(j + 1, group - 1, j * NT, TB - 1 + tiles["qk", group])
                    if not last:
                        if place == 0:
                            pe.wait_ge(qkv_read, START + j * TB + TB + group)
                        qkv(j + 1, group, PARTS[place], ps_qkv[:, 0:W])
                    if place == PER - 1:
                        weigh_values(j, slot, s - 1, first_tile(j) + tiles["probs", s - 1] + 1)

            def drain(j):
                weigh_values(j, 1, NS - 1, (j + 1) * NT)

            for_pairs(pe, prologue, attention, drain)

        @block.scalar
        def _(act):
            def split_w(j, k):
                act.wait_ge(w_in[k % SLOTS], START + 16 * (j * 2 + k // SLOTS + 1))
                act.activation(w_hi[:, k, :], w_raw[:, k % SLOTS, :], ACT.Copy).then_inc(w_hi_ok, 1)

            def split_x(b, t):
                act.wait_ge(xt_ok, START + b * TB + t + 1)
                act.activation(xt_hi[:, :, t * P:(t + 1) * P],
                               ps_s[:, t % 2, :].rearrange("p (k c) -> p k c", c=P), ACT.Copy).then_inc(xt_hi_ok, 1)

            def split_v(j, slot, t, bank):
                act.wait_ge(qkv_ok, START + j * TB + t + 1)
                act.activation(v[slot][:, t, :, 0, :], bank[:, 2 * P:W].rearrange("p (h d) -> p h d", d=HD), ACT.Copy).then_inc(v_hi_ok, 1)

            def split_qk(slot, t, start, at):
                act.wait_ge(tile_ok, START + start + (at + 1))
                act.activation(qk_hi[slot][:, :, t * P:(t + 1) * P],
                               ps_t[:, at % 2, :].rearrange("p (r c) -> p r c", c=P), ACT.Copy).then_inc(tile_hi_ok, 1)

            def exps(j, u, i):
                h, g = UNITS[u]
                n = GQ * u + i
                act.wait_ge(max_ok, START + j * NQ + n + 1)
                keys = P * (GQ * g + i + 1)
                act.activation(probs[g][:, i, 0:keys], ps_s[:, n % 2, 0:keys], ACT.Exp,
                               bias=neg_max[:, n:n + 1], accum_out=row_sum[:, n:n + 1]).then_inc(exp_ok, 1)

            def normalise(j, u, i):
                h, g = UNITS[u]
                n = GQ * u + i
                keys = P * (GQ * g + i + 1)
                act.wait_ge(inv_ok, START + j * NQ + n + 1)
                act.activation(probs[g][:, i, 0:keys], probs[g][:, i, 0:keys], ACT.Copy, scale=inv_sum[:, n:n + 1]).then_inc(norm_ok, 1)

            def lo_summand(j, u):
                h, g = UNITS[u]
                act.wait_ge(pv_ok, START + j * NS + steps_from(u + 1))
                act.wait_ge(o_out[u % 2], LOADED + (j * 2 + u // 2) * 16)
                act.activation(out_t[(1 - h) * HD:(2 - h) * HD, u % 2, :], ps_o[HD:P, :], ACT.Copy).then_inc(o_half, 1)

            def early_weights(j):
                act.wait_ge(w_early, START + j)
                for k in range(SLOTS):
                    split_w(j, k)

            def prologue(b, j):
                act.wait_ge(qkv_ok, START + j * TB)
                act.wait_ge(s_ok, START + j * NQ)
                act.wait_ge(pv_ok, START + j * NS)
                for i in range(ROUNDS):
                    for k in range(SLOTS + 2 * i, min(SLOTS + 2 * i + 2, HB)):
                        split_w(j, k)
                    if i < TB:
                        split_x(b, i)
                    if i >= 4:
                        split_qk(0, i - 4, j * NT, i - 4)
                    t = i - 2
                    if 0 <= t < TB:
                        split_v(j, 0, t, ps_qkv if t % 2 else ps_o)
                    for n in FIRST_SCORES.get(i, ()):
                        exps(j, n // GQ, n % GQ)
                        if n >= 1:
                            normalise(j, 0, n - 1)
                early_weights(j + 1)
                normalise(j, 1, 0)

            def attention(j, slot, first, last):
                tiles = tile_order(last)
                fresh = [] if first else [(j, 1, 0)]
                for s, (u, kb) in enumerate(STEPS):
                    h, g = UNITS[u]
                    group, place = divmod(s, PER)
                    at = tiles["probs", s]
                    act.wait_ge(tile_ok, START + first_tile(j) + (at + 1))
                    if s > 0:
                        act.wait_ge(pv_ok, START + j * NS + s - 1)
                    elif not first:
                        act.wait_ge(pv_ok, START + j * NS - 1)
                    off = P * max(0, kb - GQ * g)
                    act.activation(pt_hi[:, s % 2, off:], ps_t[:, (TB - 1 + at) % 2, off:], ACT.Copy).then_inc(tile_hi_ok, 1)
                    for args in fresh:
                        normalise(*args)
                    fresh = []
                    if kb == 0 and u > 0:
                        lo_summand(j, u - 1)
                    elif s == 0 and not first:
                        lo_summand(j - 1, NU - 1)
                    if place == PER - 1 and not last:
                        if group == 0:
                            act.wait_ge(pv_ok, START + j * NS)
                        split_v(j + 1, 1 - slot, group, ps_qkv)
                    if place == 1 and group == 0:
                        split_qk(slot, TB - 1, j * NT, TB - 1 + tiles["qk", 0])
                    elif place == 1 and not last:
                        if group == 1:
                            act.wait_ge(s_ok, START + j * NQ)
                        split_qk(1 - slot, group - 1, j * NT, TB - 1 + tiles["qk", group])
                    if s in W_OF_STEP and not last:
                        ahead, blocks = W_OF_STEP[s]
                        if ahead == 2:
                            act.wait_ge(w_early, START + j + 2)
                        else:
                            act.wait_ge(qkv_ok, START + j * TB + TB)
                        for k in blocks:
                            split_w(j + ahead, k)
                    for ahead, unit, i in next_queries(s, last):
                        exps(j + ahead, unit, i)
                        fresh.append((j + ahead, unit, i))

            def drain(j):
                lo_summand(j, NU - 1)

            for k in range(SLOTS):
                split_w(0, k)
            for_pairs(act, prologue, attention, drain)

        @block.vector
        def _(dve):
            dve.wait_ge(tab_in, START + 32)

            def moments(b, t):
                dve.wait_ge(x_in[t % XS], START + (b * (TB // XS) + t // XS) * 16 + 16)
                for c in range(2):
                    dve.bn_stats(stats[:, t, c, :], x_tile[:, t % XS, c * BANK:(c + 1) * BANK]).then_inc(ln_step, 1)
                dve.wait_ge(ln_step, START + (b * TB + t) * 3 + 2)
                stand_alone(dve, passed)
                dve.bn_aggr(mean_var[:, t, :], stats[:, t, :, :].rearrange("p a s -> p (a s)")).then_inc(ln_step, 1)

            def ln1(b, t):
                dve.wait_ge(ln_rstd, START + b * TB + t + 1)
                dve.tensor_scalar(x_tile[:, t % XS, :], x_tile[:, t % XS, :], mean_var[:, t, 0:1], rstd[:, t:t + 1],
                                  ALU.subtract, ALU.mult).then_inc(xn_ok, 1)

            def rest_of_x(b, t):
                dve.wait_ge(xt_hi_ok, START + b * TB + t + 1)
                dve.tensor_tensor(xt_lo[:, :, t * P:(t + 1) * P],
                                  ps_s[:, t % 2, :].rearrange("p (k c) -> p k c", c=P),
                                  raw(xt_hi[:, :, t * P:(t + 1) * P]), ALU.subtract).then_inc(xt_lo_ok, 1)

            def rotate(j, slot, t, bank, turned):
                n = j * TB + t
                dve.wait_ge(v_hi_ok, START + n + 1)
                half_d = HD // 2
                qk = bank[:, 0:2 * P].rearrange("p (a h d) -> p a h d", a=2, d=HD)
                s = r_sin[:, :, :].rearrange("p (a h) d -> p a h d", a=2)
                sb_ = sin_sb[:, t, :, :].unsqueeze(2).broadcast_to([P, 2, 2, HD])
                dve.wait_ge(rot_ok, START + n)
                dve.tensor_tensor(r_cos[:, :, :].rearrange("p (a h) (c d) -> p a (h c) d", a=2, c=2),
                                  bank[:, 0:2 * P].rearrange("p (a h d) -> p a h d", a=2, d=half_d),
                                  cos_sb[:, t, :, :].unsqueeze(2).broadcast_to([P, 2, 4, half_d]), ALU.mult).then_inc(rot_step, 1)
                dve.tensor_tensor(s[:, :, :, 0:half_d], qk[:, :, :, half_d:], sb_[:, :, :, 0:half_d], ALU.mult).then_inc(rot_step, 1)
                dve.tensor_tensor(s[:, :, :, half_d:], qk[:, :, :, 0:half_d], sb_[:, :, :, half_d:], ALU.mult).then_inc(rot_step, 1)
                dve.tensor_tensor(v[slot][:, t, :, 1, :], bank[:, 2 * P:W].rearrange("p (h d) -> p h d", d=HD),
                                  raw(v[slot][:, t, :, 0, :]), ALU.subtract).then_inc(qkv_read, 1)
                dve.wait_ge(rot_step, START + n * 3 + 3)
                dve.wait_ge(tile_ok, START + turned)
                dve.tensor_tensor(rotated[:, :, :, :],
                                  r_cos[:, :, :].unsqueeze(2).broadcast_to([P, 4, 2, HD]),
                                  r_sin[:, :, :].unsqueeze(2).broadcast_to([P, 4, 2, HD]), ALU.add).then_inc(rot_ok, 1)

            def rest_of_qk(slot, t, start, at):
                dve.wait_ge(tile_hi_ok, START + start + (at + 1))
                a = slice(t * P, (t + 1) * P)
                both = ps_t[:, at % 2, :].rearrange("p (r c) -> p r c", c=P)
                dve.tensor_tensor(q_lo[slot][:, :, a], both[:, 0:2, :], raw(qk_hi[slot][:, 0:2, a]), ALU.subtract)
                dve.tensor_tensor(qk_hi[slot][HD:P, 2:4, a], both[HD:P, 2:4, :], raw(qk_hi[slot][HD:P, 2:4, a]),
                                  ALU.subtract).then_inc(tile_lo_ok, 1)

            def maxima(j, u, i):
                h, g = UNITS[u]
                n = GQ * u + i
                dve.wait_ge(s_ok, START + j * NQ + n + 1)
                keys = P * (GQ * g + i + 1)
                dve.tensor_reduce(neg_max[:, n:n + 1], ps_s[:, n % 2, 0:keys], AX.X, ALU.max, negate=True).then_inc(max_ok, 1)

            def invert(j, u, i):
                n = GQ * u + i
                dve.wait_ge(exp_ok, START + j * NQ + n + 1)
                stand_alone(dve, passed)
                dve.reciprocal(inv_sum[:, n:n + 1], row_sum[:, n:n + 1]).then_inc(inv_ok, 1)

            def add_parts(j, u):
                h, g = UNITS[u]
                dve.wait_ge(o_half, START + j * NU + u + 1)
                dve.tensor_tensor(out_t[h * HD:(h + 1) * HD, u % 2, :], ps_o[0:HD, :],
                                  out_t[(1 - h) * HD:(2 - h) * HD, u % 2, :], ALU.add).then_inc(o_ok, 1)

            def prologue(b, j):
                moments(b, 0)
                for i in range(ROUNDS):
                    if i + 1 < TB:
                        moments(b, i + 1)
                    if i < TB:
                        ln1(b, i)
                    if 1 <= i <= TB:
                        rest_of_x(b, i - 1)
                    if i >= 4:
                        rest_of_qk(0, i - 4, j * NT, i - 4)
                    t = i - 3
                    if t >= 0:
                        rotate(j, 0, t, ps_qkv if t % 2 else ps_o, j * NT + t)
                    for n in FIRST_SCORES.get(i, ()):
                        maxima(j, n // GQ, n % GQ)
                        if n >= 1:
                            invert(j, 0, n - 1)
                invert(j, 1, 0)

            def attention(j, slot, first, last):
                tiles = tile_order(last)
                fresh = [] if first else [(j, 1, 0)]
                for s, (u, kb) in enumerate(STEPS):
                    h, g = UNITS[u]
                    group, place = divmod(s, PER)
                    for args in fresh:
                        invert(*args)
                    fresh = []
                    at = tiles["probs", s]
                    dve.wait_ge(tile_hi_ok, START + first_tile(j) + (at + 1))
                    off = P * max(0, kb - GQ * g)
                    dve.tensor_tensor(pt_lo[:, s % 2, off:], ps_t[:, (TB - 1 + at) % 2, off:], raw(pt_hi[:, s % 2, off:]),
                                      ALU.subtract).then_inc(tile_lo_ok, 1)
                    for ahead, unit, i in next_queries(s, last):
                        maxima(j + ahead, unit, i)
                        fresh.append((j + ahead, unit, i))
                    if kb == 0 and u > 0:
                        add_parts(j, u - 1)
                    elif s == 0 and not first:
                        add_parts(j - 1, NU - 1)
                    if place == PER - 1 and not last:
                        rotate(j + 1, 1 - slot, group, ps_qkv, first_tile(j) + tiles["qk", group] + 1)
                    if place == 1 and group == 0:
                        rest_of_qk(slot, TB - 1, j * NT, TB - 1 + tiles["qk", 0])
                    elif place == 1 and not last:
                        rest_of_qk(1 - slot, group - 1, j * NT, TB - 1 + tiles["qk", group])

            def drain(j):
                add_parts(j, NU - 1)

            for_pairs(dve, prologue, attention, drain)


def mix_features(nc, const, logits, x, attn_out, wo, ctx_t, xw, xbias, gate, rows, out):
    ident, ident16, mask16, half, passed = const
    HALVES = H // BANK
    with ExitStack() as scope:
        m = Memory(nc, scope)
        wo_hi = m.sb("wo_hi", [P, HB, H], F32R)
        wo_lo = m.sb("wo_lo", [P, HB, H], F32R)
        xw_hi = m.sb("xw_hi", [P, CB, 2 * D], F32R)
        xw_lo = m.sb("xw_lo", [P, CB, 2 * D], F32R)
        bias = m.sb("xattn_bias", [P, 2])
        gate_sb = m.sb("gate_sb", [P, HB, E])
        at_hi = m.sb("at_hi", [P, TB, S], F32R)
        at_lo = m.sb("at_lo", [P, TB, S], F32R)
        split = m.sb("split", [P, 4, H], F32R)
        qk = m.sb("xattn_qk", [P, 4, S], F32R)
        stage = m.sb("stage", [P, 2, H])
        work = m.sb("work", [P, 2, H])
        ctx_hi_sb, ctx_lo_sb = at_hi[:, 0:CB, :], at_lo[:, 0:CB, :]
        ctx_raw = [t[:, :, :].rearrange("p a (c n) -> p (a c) n", n=BANK) for t in (stage, work)]
        res = m.sb("residual", [P, 2, H])
        x3_t = m.sb("x3_t", [P, HB, P])
        small = m.sb("mix_small", [P, 8, 4])
        stats = m.sb("mix_stats", [P, 2, 2, 6])
        mean_var = m.sb("mix_mean_var", [P, 2, 2])
        rstd = m.sb("mix_rstd", [P, 2])
        ps_a = m.ps("ps_a", [P, H])
        ps_b = m.ps("ps_b", [P, H])
        ps_t2 = m.ps("ps_t2", [P, H])
        ps_r = m.ps("ps_r", [P, 2, BANK])
        ps_e = [ps_a, ps_b]
        ps_et = [ps_t2[:, :], ps_r[:, :, :].rearrange("p a n -> p (a n)")]

        zero_ok, zero_out = m.sem("zero_ok"), m.sem("zero_out")
        w_in = [m.sem(f"mix_w_in{i}") for i in range(4)]
        small_in = m.sem("mix_small_in")
        w_hi_ok, w_lo_ok = m.sem("mix_w_hi"), m.sem("mix_w_lo")
        ctx_in, ctx_hi, ctx_lo = [m.sem(f"ctx_in{n}") for n in range(2)], m.sem("ctx_hi"), m.sem("ctx_lo")
        proj_ok, proj_hi, proj_lo = m.sem("proj_ok"), m.sem("proj_hi"), m.sem("proj_lo")
        e_ok, emax_ok, eexp_ok, einv_ok, enorm_ok = (m.sem(n) for n in ("e_ok", "emax_ok", "eexp_ok", "einv_ok", "enorm_ok"))
        et_ok, et_hi, et_lo = m.sem("et_ok"), m.sem("et_hi"), m.sem("et_lo")
        ot_in, res_in = [m.sem(f"ot_in{i}") for i in range(2)], [m.sem(f"res_in{i}") for i in range(2)]
        ot_hi, ot_lo = m.sem("ot_hi"), m.sem("ot_lo")
        wo_ok, x1_ok = m.sem("wo_ok"), m.sem("x1_ok")
        ln_step, ln_eps, ln_rstd, ln_ok = (m.sem(n) for n in ("mix_ln_step", "mix_ln_eps", "mix_ln_rstd", "mix_ln_ok"))
        t2_ok, t2_hi, t2_lo = m.sem("t2_ok"), m.sem("t2_hi"), m.sem("t2_lo")
        xm_ok, x2_ok, x2_out, x3_out = m.sem("xm_ok"), m.sem("x2_ok"), m.sem("x2_out"), m.sem("x3_out")
        t3_ok, t3_read, r_ok, r_read = m.sem("t3_ok"), m.sem("t3_read"), m.sem("r_ok"), m.sem("r_read")

        order = [(2, 0)]
        for i in range(TB):
            order += [(2, i + 1)] * (i + 1 < TB) + [(3, i)]
        LN = {what: n for n, what in enumerate(order)}

        def raw_weights(k):
            return (stage, work)[k % 4 // 2][:, k % 2, :]

        m.start_counts()
        block = scope.enter_context(nc.Block())

        @block.sync
        def _(sp):
            sp.wait_ge(zero_ok, START + 1)
            sp.dma_start(rows[0:P, 0:H], res[:, 0, :]).then_inc(zero_out, 16)
            sp.dma_start(rows[0:P, H:H + E], res[:, 0, 0:E]).then_inc(zero_out, 16)
            sp.dma_start(out[0:P, :], res[:, 0, :]).then_inc(zero_out, 16)
            sp.dma_start(bias[:, :], xbias).then_inc(small_in, 16)
            sp.dma_start(gate_sb[:, :, :], gate.rearrange("(k p) e -> p k e", p=P)).then_inc(small_in, 16)
            for k in range(HB + 1):
                if k >= 4:
                    sp.wait_ge(w_lo_ok, START + k - 3)
                if k == 0:
                    sp.dma_start(raw_weights(k).rearrange("p (c d) -> p c d", d=2 * D),
                                 xw.rearrange("(c p) d -> p c d", p=P)).then_inc(w_in[k % 4], 16)
                else:
                    sp.dma_start(raw_weights(k), wo[(k - 1) * P:k * P, :]).then_inc(w_in[k % 4], 16)
            sp.wait_ge(w_lo_ok, START + HB + 1)
            sp.wait_ge(zero_out, START + 48)
            with sp.Fori(0, B) as b:
                for n in range(2):
                    if n == 0:
                        sp.wait_ge(ot_lo, START + b * TB)
                    else:
                        sp.wait_ge(t3_ok, START + b * TB)
                        stand_alone(sp, passed)
                        sp.wait_ge(x3_out, START + b * TB * 16)
                    stand_alone(sp, passed)
                    sp.dma_start(ctx_raw[n], ctx_t[b].rearrange("(c p) n -> p c n", p=P)[:, :, n * BANK:(n + 1) * BANK]).then_inc(ctx_in[n], 16)

                def load_attn(i):
                    if i >= 2:
                        sp.wait_ge(ot_lo, START + b * TB + i - 1)
                    sp.dma_start(stage[:, i % 2, :].rearrange("p (k c) -> p k c", c=P),
                                 attn_out[b].rearrange("k p c -> p k c")[:, :, i * P:(i + 1) * P]).then_inc(ot_in[i % 2], 16)

                def load_x(i):
                    sp.dma_start(res[:, i % 2, :], x[b, i * P:(i + 1) * P, :]).then_inc(res_in[i % 2], 16)

                load_x(0)
                load_x(1)
                sp.wait_ge(ctx_lo, START + (b * 2 + 1) * CB)
                stand_alone(sp, passed)
                load_attn(0)
                load_attn(1)
                for i in range(TB):
                    if i + 2 < TB:
                        load_attn(i + 2)
                    row = P + (b * TB + i) * P
                    sp.wait_ge(x2_ok, START + b * TB + i + 1)
                    sp.dma_start(out[bass.ds(row, P), :], res[:, i % 2, :]).then_inc(x2_out, 16)
                    sp.wait_ge(ln_ok, START + b * 2 * TB + LN[3, i] + 1)
                    sp.dma_start(rows[bass.ds(row, P), 0:H], work[:, 1, :]).then_inc(x3_out, 16)
                    sp.wait_ge(x2_out, START + (b * TB + i + 1) * 16)
                    stand_alone(sp, passed)
                    if i + 2 < TB:
                        load_x(i + 2)
            sp.wait_ge(x3_out, START + B * TB * 16)

        @block.gpsimd
        def _(pool):
            pool.memset(res[:, 0, :], 0.0).then_inc(zero_ok, 1)
            with pool.Fori(0, B) as b:
                for which, i in order:
                    n = b * 2 * TB + LN[which, i]
                    s = which - 2
                    pool.wait_ge(ln_step, START + n * 3 + 3)
                    stand_alone(pool, passed)
                    pool.tensor_scalar(rstd[:, s:s + 1], mean_var[:, s, 1:2], EPS, 1.0, ALU.add, ALU.mult).then_inc(ln_eps, 1)
                    pool.wait_ge(ln_eps, START + n + 1)
                    pool.tensor_tensor(rstd[:, s:s + 1], rstd[:, s:s + 1], half[:, 0:1], ALU.pow).then_inc(ln_rstd, 1)

        @block.tensor
        def _(pe):
            def split_product(out, a_hi, a_lo, w_hi, w_lo, first, last):
                pe.matmul(out, a_hi, w_hi, start=first, stop=False)
                pe.matmul(out, a_hi, w_lo, start=False, stop=False)
                return pe.matmul(out, a_lo, w_hi, start=False, stop=last)

            pe.wait_ge(w_lo_ok, START + HB + 1)
            pe.wait_ge(small_in, START + 32)
            with pe.Fori(0, B) as b:
                for n in range(2):
                    pe.wait_ge(ctx_lo, START + (b * 2 + n + 1) * CB)
                    for w in range(2):
                        pe.wait_ge(proj_lo, START + (b * 2 + n) * 2)
                        pe.wait_ge(r_read, START + b * TB)
                        pe.wait_ge(et_lo, START + b * TB)
                        half_n = slice(n * BANK, (n + 1) * BANK)
                        for c in range(CB):
                            mm = split_product(ps_r[:, w, :], xw_hi[:, c, w * D:(w + 1) * D], xw_lo[:, c, w * D:(w + 1) * D],
                                               ctx_hi_sb[:, c, half_n], ctx_lo_sb[:, c, half_n], c == 0, c == CB - 1)
                        mm.then_inc(proj_ok, 1)

                def energies(i):
                    if i >= 2:
                        pe.wait_ge(eexp_ok, START + b * TB + i - 1)
                    a = slice(i * P, (i + 1) * P)
                    for c in range(HALVES):
                        n = slice(c * BANK, (c + 1) * BANK)
                        mm = split_product(ps_e[i % 2][:, n], qk[:, 0, a], qk[:, 1, a], qk[:, 2, n], qk[:, 3, n], True, True)
                    mm.then_inc(e_ok, 1)

                def turn_attention(i):
                    pe.wait_ge(enorm_ok, START + b * TB + i + 1)
                    if i >= 2:
                        pe.wait_ge(et_lo, START + b * TB + i - 1)
                    else:
                        pe.wait_ge(t3_read, START + b * TB)
                    for k in range(TB):
                        mm = pe.transpose(ps_et[i % 2][:, k * P:(k + 1) * P], work[:, i % 2, k * P:(k + 1) * P], ident[:, :])
                    mm.then_inc(et_ok, 1)

                pe.wait_ge(proj_lo, START + (b + 1) * 4)
                pe.wait_ge(x1_ok, START + b * TB)
                pe.wait_ge(x2_ok, START + b * TB)
                def project(i, c):
                    pe.wait_ge(ot_lo, START + b * TB + i + 1)
                    if c == 0:
                        pe.wait_ge(x1_ok, START + b * TB + i)
                    n = slice(c * BANK, (c + 1) * BANK)
                    for k in range(HB):
                        a = slice(k * P, (k + 1) * P)
                        mm = split_product(ps_a[:, n], split[:, 0, a], split[:, 1, a], wo_hi[:, k, n], wo_lo[:, k, n], k == 0, k == HB - 1)
                    if c == HALVES - 1:
                        mm.then_inc(wo_ok, 1)

                def turn(which, i):
                    g = b * TB + i
                    pe.wait_ge(ln_ok, START + b * 2 * TB + LN[which, i] + 1)
                    if which == 2:
                        if i >= 2:
                            pe.wait_ge(t3_read, START + g - 1)
                        elif i == 0:
                            pe.wait_ge(et_lo, START + b * TB + TB)
                    else:
                        if i + 1 < TB:
                            pe.wait_ge(t2_lo, START + g + 2)
                        else:
                            pe.wait_ge(t3_read, START + g)
                    for k in range(HB):
                        mm = pe.transpose(ps_t2[:, k * P:(k + 1) * P], work[:, which - 2, k * P:(k + 1) * P], ident[:, :])
                    mm.then_inc(t2_ok if which == 2 else t3_ok, 1)

                def mix(i):
                    g = b * TB + i
                    pe.wait_ge(t2_lo, START + g + 1)
                    pe.wait_ge(x2_ok, START + g)
                    for c in range(HALVES):
                        n = slice(c * BANK, (c + 1) * BANK)
                        for k in range(TB):
                            a = slice(k * P, (k + 1) * P)
                            mm = split_product(ps_b[:, n], split[:, 2, a], split[:, 3, a], at_hi[:, k, n], at_lo[:, k, n], k == 0, k == TB - 1)
                    mm.then_inc(xm_ok, 1)

                def route_logits(i):
                    g = b * TB + i
                    pe.wait_ge(t3_read, START + g + 1)
                    pe.wait_ge(r_read, START + g)
                    for k in range(HB):
                        mm = pe.matmul(ps_r[:, 0, 0:E], x3_t[:, k, :], gate_sb[:, k, :], start=(k == 0), stop=(k == HB - 1))
                    mm.then_inc(r_ok, 1)

                energies(0)
                for i in range(TB):
                    if i + 1 < TB:
                        energies(i + 1)
                    else:
                        project(0, 0)
                        project(0, 1)
                    turn_attention(i)
                for i in range(TB):
                    if i + 1 < TB:
                        project(i + 1, 0)
                    turn(2, i)
                    if i + 1 < TB:
                        project(i + 1, 1)
                    if i >= 1:
                        turn(3, i - 1)
                    mix(i)
                    if i >= 1:
                        route_logits(i - 1)
                turn(3, TB - 1)
                route_logits(TB - 1)

        @block.scalar
        def _(act):
            for k in range(HB + 1):
                act.wait_ge(w_in[k % 4], START + (k // 4) * 16 + 16)
                dst = wo_hi[:, k - 1, :] if k else xw_hi[:, :, :].rearrange("p c d -> p (c d)")
                act.activation(dst, raw_weights(k), ACT.Copy).then_inc(w_hi_ok, 1)
            act.wait_ge(small_in, START + 32)
            with act.Fori(0, B) as b:
                for n in range(2):
                    act.wait_ge(ctx_in[n], START + b * 16 + 16)
                    if n == 0:
                        act.wait_ge(xm_ok, START + b * TB)
                    for c in range(CB):
                        act.activation(ctx_hi_sb[:, c, n * BANK:(n + 1) * BANK], ctx_raw[n][:, c, :], ACT.Copy).then_inc(ctx_hi, 1)
                for n in range(2):
                    for w in range(2):
                        act.wait_ge(proj_ok, START + (b * 2 + n) * 2 + w + 1)
                        act.activation(qk[:, 2 * w, n * BANK:(n + 1) * BANK], ps_r[:, w, :], ACT.Identity,
                                       bias=bias[:, w:w + 1]).then_inc(proj_hi, 1)

                def exps(i):
                    act.wait_ge(emax_ok, START + b * TB + i + 1)
                    if i >= 2:
                        act.wait_ge(et_ok, START + b * TB + i - 1)
                    else:
                        act.wait_ge(ctx_lo, START + (b + 1) * 2 * CB)
                    act.activation(work[:, i % 2, :], ps_e[i % 2][:, :], ACT.Exp, bias=small[:, i, 0:1],
                                   accum_out=small[:, i, 1:2]).then_inc(eexp_ok, 1)

                def split_attention(i):
                    act.wait_ge(et_ok, START + b * TB + i + 1)
                    act.activation(at_hi[:, :, i * P:(i + 1) * P], ps_et[i % 2].rearrange("p (k c) -> p k c", c=P),
                                   ACT.Copy).then_inc(et_hi, 1)

                def split_attn_out(i):
                    g = b * TB + i
                    act.wait_ge(ot_in[i % 2], START + (b * (TB // 2) + i // 2) * 16 + 16)
                    act.wait_ge(wo_ok, START + g)
                    act.activation(split[:, 0, :], stage[:, i % 2, :], ACT.Copy).then_inc(ot_hi, 1)

                exps(0)
                for i in range(TB):
                    if i + 1 < TB:
                        exps(i + 1)
                    else:
                        split_attn_out(1)
                    split_attention(i)
                    if i == 0:
                        split_attn_out(0)

                def split_ln2(i):
                    g = b * TB + i
                    act.wait_ge(t2_ok, START + g + 1)
                    act.wait_ge(xm_ok, START + g)
                    act.activation(split[:, 2, :], ps_t2[:, :], ACT.Copy).then_inc(t2_hi, 1)

                def copy_ln3(i):
                    g = b * TB + i
                    act.wait_ge(t3_ok, START + g + 1)
                    act.wait_ge(r_ok, START + g)
                    act.activation(x3_t[:, :, :].rearrange("p k c -> p (k c)"), ps_t2[:, :], ACT.Copy).then_inc(t3_read, 1)

                def copy_logits(i):
                    g = b * TB + i
                    act.wait_ge(r_ok, START + g + 1)
                    act.activation(logits[:, bass.ds(g, 1), :].rearrange("p a e -> p (a e)"), ps_r[:, 0, 0:E], ACT.Copy).then_inc(r_read, 1)

                for i in range(TB):
                    split_ln2(i)
                    if i + 2 < TB:
                        split_attn_out(i + 2)
                    if i >= 1:
                        copy_ln3(i - 1)
                        copy_logits(i - 1)
                copy_ln3(TB - 1)
                copy_logits(TB - 1)

        @block.vector
        def _(dve):
            for k in range(HB + 1):
                dve.wait_ge(w_hi_ok, START + k + 1)
                dst, hi = (wo_lo[:, k - 1, :], wo_hi[:, k - 1, :]) if k else (t[:, :, :].rearrange("p c d -> p (c d)") for t in (xw_lo, xw_hi))
                dve.tensor_tensor(dst, raw_weights(k), raw(hi), ALU.subtract).then_inc(w_lo_ok, 1)
            dve.wait_ge(small_in, START + 32)
            with dve.Fori(0, B) as b:
                for n in range(2):
                    for c in range(CB):
                        dve.wait_ge(ctx_hi, START + (b * 2 + n) * CB + c + 1)
                        a = slice(n * BANK, (n + 1) * BANK)
                        dve.tensor_tensor(ctx_lo_sb[:, c, a], ctx_raw[n][:, c, :], raw(ctx_hi_sb[:, c, a]), ALU.subtract).then_inc(ctx_lo, 1)
                for n in range(2):
                    for w in range(2):
                        dve.wait_ge(proj_hi, START + (b * 2 + n) * 2 + w + 1)
                        a = slice(n * BANK, (n + 1) * BANK)
                        dve.scalar_tensor_tensor(out=qk[:, 2 * w + 1, a], in0=ps_r[:, w, :], scalar=bias[:, w:w + 1],
                                                 in1=raw(qk[:, 2 * w, a]), op0=ALU.add, op1=ALU.subtract).then_inc(proj_lo, 1)

                def maxima(i):
                    dve.wait_ge(e_ok, START + b * TB + i + 1)
                    dve.tensor_reduce(small[:, i, 0:1], ps_e[i % 2][:, :], AX.X, ALU.max, negate=True).then_inc(emax_ok, 1)

                def normalise_rows(i):
                    dve.wait_ge(eexp_ok, START + b * TB + i + 1)
                    dve.reciprocal(small[:, i, 2:3], small[:, i, 1:2]).then_inc(einv_ok, 1)
                    dve.wait_ge(einv_ok, START + b * TB + i + 1)
                    dve.tensor_scalar(work[:, i % 2, :], work[:, i % 2, :], small[:, i, 2:3], None, ALU.mult).then_inc(enorm_ok, 1)

                def rest_of_attention(i):
                    dve.wait_ge(et_hi, START + b * TB + i + 1)
                    a = slice(i * P, (i + 1) * P)
                    dve.tensor_tensor(at_lo[:, :, a], ps_et[i % 2].rearrange("p (k c) -> p k c", c=P), raw(at_hi[:, :, a]),
                                      ALU.subtract).then_inc(et_lo, 1)

                def rest_of_attn_out(i):
                    dve.wait_ge(ot_hi, START + b * TB + i + 1)
                    dve.tensor_tensor(split[:, 1, :], stage[:, i % 2, :], raw(split[:, 0, :]), ALU.subtract).then_inc(ot_lo, 1)

                def layer_norm(which, i):
                    n = b * 2 * TB + LN[which, i]
                    s = which - 2
                    for c in range(HALVES):
                        dve.bn_stats(stats[:, s, c, :], res[:, i % 2, c * BANK:(c + 1) * BANK]).then_inc(ln_step, 1)
                    dve.wait_ge(ln_step, START + n * 3 + 2)
                    stand_alone(dve, passed)
                    dve.bn_aggr(mean_var[:, s, :], stats[:, s, :, :].rearrange("p a s -> p (a s)")).then_inc(ln_step, 1)
                    dve.wait_ge(ln_rstd, START + n + 1)
                    if which == 2 and i >= 1:
                        dve.wait_ge(t2_ok, START + b * TB + i)
                    if which == 3 and i >= 1:
                        dve.wait_ge(t3_ok, START + b * TB + i)
                        dve.wait_ge(x3_out, START + (b * TB + i) * 16)
                    dve.tensor_scalar(work[:, s, :], res[:, i % 2, :], mean_var[:, s, 0:1], rstd[:, s:s + 1],
                                      ALU.subtract, ALU.mult).then_inc(ln_ok, 1)

                def add_projection(i, between=None):
                    dve.wait_ge(wo_ok, START + b * TB + i + 1)
                    dve.wait_ge(res_in[i % 2], START + (b * (TB // 2) + i // 2) * 16 + 16)
                    dve.tensor_tensor(res[:, i % 2, :], ps_a[:, :], res[:, i % 2, :], ALU.add).then_inc(x1_ok, 1)
                    dve.wait_ge(x1_ok, START + b * TB + i + 1)
                    if between:
                        between(i + 1)
                    layer_norm(2, i)

                def rest_of_ln2(i):
                    dve.wait_ge(t2_hi, START + b * TB + i + 1)
                    dve.tensor_tensor(split[:, 3, :], ps_t2[:, :], raw(split[:, 2, :]), ALU.subtract).then_inc(t2_lo, 1)

                def add_mix(i):
                    dve.wait_ge(xm_ok, START + b * TB + i + 1)
                    dve.tensor_tensor(res[:, i % 2, :], ps_b[:, :], res[:, i % 2, :], ALU.add).then_inc(x2_ok, 1)
                    dve.wait_ge(x2_ok, START + b * TB + i + 1)
                    layer_norm(3, i)

                maxima(0)
                for i in range(TB):
                    normalise_rows(i)
                    if i + 1 < TB:
                        maxima(i + 1)
                    if i >= 1:
                        rest_of_attention(i - 1)
                    if i == 1:
                        rest_of_attn_out(0)
                add_projection(0, rest_of_attn_out)
                rest_of_attention(TB - 1)
                for i in range(TB):
                    rest_of_ln2(i)
                    if i + 1 < TB:
                        add_projection(i + 1)
                    if i + 2 < TB:
                        rest_of_attn_out(i + 2)
                    add_mix(i)


def route(nc, const, logits, lo16, hi16, starts, similarity, rows):
    ident, passed = const[0], const[-1]
    N = B * TB
    G = BANK // P
    R = BANK // E
    with ExitStack() as scope:
        m = Memory(nc, scope)
        top = m.sb("top_values", [P, N, TOPK])
        top_i = m.sb("top_index", [P, N, TOPK], U32)
        top_f = m.sb("top_index_f", [P, N, TOPK])
        rest = m.sb("rest", [P, N, E])
        prob = m.sb("prob", [P, N, E])
        first = m.sb("first", [P, N, E])
        hit = m.sb("hit", [P, N, E])
        sums = m.sb("sums", [P, 4, N])
        iota_e = m.sb("iota_e", [P, E])
        place = m.sb("place", [E, 1])
        picked = m.sb("picked", [P, 2, E], BF16)
        ones16 = m.sb("ones16", [P, P], BF16)
        before16 = m.sb("before16", [P, P], BF16)
        sim = m.sb("sim_sb", [E, E])
        cand = m.sb("cand", [E, E])
        is_first = m.sb("is_first", [E, E], I32)
        best = m.sb("best", [E, TOPK])
        best_i = m.sb("best_i", [E, TOPK], U32)
        s1 = m.sb("route_small", [E, 8])
        remap = m.sb("remap", [E, E])
        weight_t = m.sb("weight_t", [E, 2, BANK])
        weight = m.sb("weight", [P, N, E])
        routed16 = m.sb("routed16", [P, N, E], BF16)
        so_far16 = m.sb("so_far16", [P, N + 1, E], BF16)
        rank = m.sb("rank", [P, E, N], I32)
        part = m.sb("part", [P, E, N], I32)
        count = m.sb("count", [P, E], I32)
        blocks = m.sb("blocks", [P, E])
        ends = m.sb("ends", [P, E])
        zeros = m.sb("zeros", [P, E])
        ps_n = m.ps("ps_n", [P, BANK])
        ps_w = m.ps("ps_w", [P, 2, BANK])
        ps_x = m.ps("ps_x", [P, 2, BANK])
        ps_k = m.ps("ps_k", [P, 2, BANK])

        made, sim_in, sim_ok = m.sem("route_made"), m.sem("sim_in"), m.sem("sim_ok")
        step = m.sem("route_step")
        z_ok, exp_ok, picked_ok, votes_ok = (m.sem(n) for n in ("z_ok", "p_exp_ok", "picked_ok", "votes_ok"))
        remap_ok, wt_ok, wt_read, w2_ok, w2_read = (m.sem(n) for n in ("remap_ok", "wt_ok", "wt_read", "w2_ok", "w2_read"))
        w_out, routed_ok, rank_ok, rank_read = (m.sem(n) for n in ("w_out", "routed_ok", "rank_ok", "rank_read"))
        m.start_counts()
        block = scope.enter_context(nc.Block())

        @block.gpsimd
        def _(pool):
            pool.iota(iota_e[:, :], [[1, E]], base=0, channel_multiplier=0, allow_small_or_imprecise_dtypes=True).then_inc(made, 1)
            pool.iota(place[:, :], [[1, 1]], base=0, channel_multiplier=1, allow_small_or_imprecise_dtypes=True).then_inc(made, 1)
            pool.memset(ones16[:, :], 1.0).then_inc(made, 1)
            pool.memset(before16[:, :], 1.0).then_inc(made, 1)
            pool.memset(cand[:, :], -3e38).then_inc(made, 1)
            pool.memset(so_far16[:, 0, :], 0.0).then_inc(made, 1)
            pool.memset(zeros[:, :], 0.0).then_inc(made, 1)
            pool.memset(starts[:, 0:1], 0).then_inc(made, 1)
            pool.memset(lo16[:, E:, :], 0.0).then_inc(made, 1)
            pool.memset(hi16[:, E:, :], 0.0).then_inc(made, 1)
            pool.wait_ge(made, START + 10)
            pool.affine_select(out=before16[:, :], in_=before16[:, :], compare_op=ALU.is_gt, fill=0.0,
                               base=0, pattern=[[1, P]], channel_multiplier=-1).then_inc(made, 1)
            pool.wait_ge(sim_in, START + 16)
            pool.affine_select(out=sim[:, :], in_=sim[:, :], compare_op=ALU.not_equal, fill=1.0,
                               base=0, pattern=[[-1, E]], channel_multiplier=1).then_inc(sim_ok, 1)

        @block.sync
        def _(sp):
            sp.dma_start(sim[:, :], similarity).then_inc(sim_in, 16)
            sp.wait_ge(w2_read, START + N // G)
            sp.dma_start(rows[P:P + N * P, H:H + E].rearrange("(n p) e -> p n e", p=P), weight[:, :, :]).then_inc(w_out, 16)
            sp.wait_ge(w_out, START + 16)

        @block.scalar
        def _(act):
            act.wait_ge(z_ok, START + 1)
            act.activation(prob[:, :, :], prob[:, :, :], ACT.Exp).then_inc(exp_ok, 1)
            for g in range(N // G):
                act.wait_ge(wt_ok, START + g + 1)
                if g >= 2:
                    act.wait_ge(w2_ok, START + g - 1)
                act.activation(weight_t[:, g % 2, :], ps_w[0:E, g % 2, :], ACT.Copy).then_inc(wt_read, 1)

        @block.tensor
        def _(pe):
            pe.wait_ge(made, START + 11)
            pe.wait_ge(picked_ok, START + 1)
            pe.matmul(ps_n[0:E, 0:E], ones16[:, 0:E], picked[:, 0, :], start=True, stop=True)
            pe.matmul(ps_n[0:E, E:E + 1], picked[:, 0, :], ones16[:, 0:1], start=True, stop=True)
            pe.matmul(ps_n[0:E, E + 1:E + 2], picked[:, 1, :], ones16[:, 0:1], start=True, stop=True).then_inc(votes_ok, 1)
            pe.wait_ge(remap_ok, START + 1)

            def remapped(g):
                pe.wait_ge(wt_read, START + g + 1)
                if g >= 2:
                    pe.wait_ge(w2_read, START + g - 1)
                for i in range(G):
                    mm = pe.matmul(ps_x[:, g % 2, i * E:(i + 1) * E], weight_t[:, g % 2, i * P:(i + 1) * P], remap[:, :],
                                   start=True, stop=True)
                mm.then_inc(w2_ok, 1)

            for g in range(N // G):
                if g >= 2:
                    pe.wait_ge(wt_read, START + g - 1)
                for i in range(G):
                    mm = pe.transpose(ps_w[0:E, g % 2, i * P:(i + 1) * P], prob[:, g * G + i, :], ident[:, :])
                mm.then_inc(wt_ok, 1)
                if g >= 1:
                    remapped(g - 1)
            remapped(N // G - 1)
            pe.wait_ge(routed_ok, START + 1)
            for r in range(N // R):
                if r >= 2:
                    pe.wait_ge(rank_read, START + r - 1)
                a = slice(r * R, (r + 1) * R)
                pe.matmul(ps_k[:, r % 2, :], before16[:, :], routed16[:, a, :].rearrange("p n e -> p (n e)"), start=True, stop=False)
                pe.matmul(ps_k[:, r % 2, :], ones16[:, :], so_far16[:, a, :].rearrange("p n e -> p (n e)"),
                          start=False, stop=True).then_inc(rank_ok, 1)
            pe.matmul(ps_n[:, 0:E], ones16[:, :], so_far16[:, N, :], start=True, stop=True).then_inc(rank_ok, 1)

        @block.vector
        def _(dve):
            done = [0]

            def after(ins):
                done[0] += 1
                ins.then_inc(step, 1)
                dve.wait_ge(step, START + done[0])

            def each(ap, n):
                return ap.unsqueeze(2).broadcast_to([P, N, n])

            for n in range(N):
                ins = dve.max(top[:, n, :], logits[:, n, :])
            after(ins)
            dve.tensor_tensor(prob[:, :, :], logits[:, :, :], each(top[:, :, 0], E), ALU.subtract).then_inc(z_ok, 1)
            for n in range(N):
                dve.max_index(top_i[:, n, :], top[:, n, :], logits[:, n, :])
                ins = dve.match_replace(rest[:, n, :], top[:, n, :], logits[:, n, :], -3e38)
            after(ins)
            dve.tensor_copy(top_f[:, :, :], top_i[:, :, :])
            after(dve.tensor_tensor(rest[:, :, :], rest[:, :, :], logits[:, :, :], ALU.not_equal))
            dve.wait_ge(exp_ok, START + 1)
            after(dve.tensor_reduce(sums[:, 0, :], prob[:, :, :], AX.X, ALU.add))
            after(dve.reciprocal(sums[:, 1, :], sums[:, 0, :]))
            after(dve.tensor_tensor(prob[:, :, :], prob[:, :, :], each(sums[:, 1, :], E), ALU.mult))
            after(dve.tensor_tensor(prob[:, :, :], prob[:, :, :], rest[:, :, :], ALU.mult))
            after(dve.tensor_reduce(sums[:, 2, :], prob[:, :, :], AX.X, ALU.add))
            after(dve.tensor_scalar(sums[:, 2, :], sums[:, 2, :], 1e-12, None, ALU.max))
            after(dve.reciprocal(sums[:, 3, :], sums[:, 2, :]))
            after(dve.tensor_tensor(prob[:, :, :], prob[:, :, :], each(sums[:, 3, :], E), ALU.mult))
            dve.wait_ge(made, START + 11)
            experts = iota_e[:, :].unsqueeze(1).broadcast_to([P, N, E])
            after(dve.tensor_tensor(first[:, :, :], experts, each(top_f[:, :, 0], E), ALU.is_equal))
            for k in range(1, SELK):
                after(dve.tensor_tensor(hit[:, :, :], experts, each(top_f[:, :, k], E), ALU.is_equal))
                after(dve.tensor_tensor(first[:, :, :], first[:, :, :], hit[:, :, :], ALU.add))
            after(dve.tensor_tensor(hit[:, :, :], rest[:, :, :], first[:, :, :], ALU.subtract))
            with nc.allow_low_precision(reason="counts up to 32 are exact in bfloat16"):
                dve.tensor_reduce(picked[:, 0, :], first[:, :, :].rearrange("p n e -> p e n"), AX.X, ALU.add)
                dve.tensor_reduce(picked[:, 1, :], hit[:, :, :].rearrange("p n e -> p e n"), AX.X, ALU.add).then_inc(picked_ok, 1)
            dve.wait_ge(votes_ok, START + 1)
            dve.wait_ge(sim_ok, START + 1)
            after(dve.tensor_scalar(is_first[:, :], ps_n[0:E, 0:E], 0.5, None, ALU.is_ge))
            after(dve.copy_predicated(cand[:, :], is_first[:, :], sim[:, :]))
            after(dve.max(best[:, :], cand[:, :]))
            after(dve.max_index(best_i[:, :], best[:, :], cand[:, :]))
            dve.tensor_copy(s1[:, 0:1], best_i[:, 0:1])
            dve.tensor_scalar(s1[:, 1:2], ps_n[0:E, E:E + 1], 0.5, None, ALU.is_lt)
            dve.tensor_scalar(s1[:, 2:3], ps_n[0:E, E + 1:E + 2], 0.5, None, ALU.is_ge)
            after(dve.tensor_scalar(s1[:, 3:4], best[:, 0:1], 0.5, None, ALU.is_ge))
            dve.tensor_tensor(s1[:, 4:5], s1[:, 0:1], place[:, :], ALU.subtract)
            after(dve.tensor_tensor(s1[:, 5:6], s1[:, 1:2], s1[:, 2:3], ALU.mult))
            after(dve.tensor_tensor(s1[:, 5:6], s1[:, 5:6], s1[:, 3:4], ALU.mult))
            after(dve.tensor_tensor(s1[:, 4:5], s1[:, 4:5], s1[:, 5:6], ALU.mult))
            after(dve.tensor_tensor(s1[:, 6:7], s1[:, 4:5], place[:, :], ALU.add))
            dve.tensor_scalar(remap[:, :], iota_e[0:E, :], s1[:, 6:7], None, ALU.is_equal).then_inc(remap_ok, 1)
            for g in range(N // G):
                dve.wait_ge(w2_ok, START + g + 1)
                dve.tensor_copy(weight[:, g * G:(g + 1) * G, :],
                                ps_x[:, g % 2, 0:G * E].rearrange("p (n e) -> p n e", e=E)).then_inc(w2_read, 1)
            dve.wait_ge(w2_read, START + N // G)
            after(dve.tensor_scalar(routed16[:, :, :], weight[:, :, :], 0.0, None, ALU.is_gt))
            for n in range(N):
                ins = dve.tensor_tensor(so_far16[:, n + 1, :], so_far16[:, n, :], routed16[:, n, :], ALU.add)
                if n < N - 1:
                    after(ins)
            ins.then_inc(routed_ok, 1)
            for r in range(N // R):
                dve.wait_ge(rank_ok, START + r + 1)
                dve.tensor_copy(rank[:, :, r * R:(r + 1) * R],
                                ps_k[:, r % 2, :].rearrange("p (n e) -> p e n", e=E)).then_inc(rank_read, 1)
            dve.wait_ge(rank_ok, START + N // R + 1)
            after(dve.tensor_copy(count[:, :], ps_n[:, 0:E]))
            dve.wait_ge(rank_read, START + N // R)
            after(dve.tensor_scalar(part[:, :, :], rank[:, :, :], 7, None, ALU.arith_shift_right))
            dve.tensor_copy(hi16[:, 0:E, :], part[:, :, :])
            after(dve.tensor_scalar(count[:, :], count[:, :], P - 1, None, ALU.add))
            after(dve.tensor_scalar(part[:, :, :], rank[:, :, :], P - 1, None, ALU.bitwise_and))
            dve.scalar_tensor_tensor(out=lo16[:, 0:E, :], in0=part[:, :, :], scalar=1.0,
                                     in1=routed16[:, :, :].rearrange("p n e -> p e n"), op0=ALU.add, op1=ALU.mult)
            after(dve.tensor_scalar(count[:, :], count[:, :], 7, None, ALU.arith_shift_right))
            after(dve.tensor_scalar(blocks[:, :], count[:, :], 1.0, None, ALU.max))
            after(dve.tensor_tensor_scan(ends[:, :], zeros[:, :], blocks[:, :], 0.0, ALU.add, ALU.add))
            dve.tensor_copy(starts[:, 1:E + 1], ends[:, :])
            after(dve.tensor_copy(starts[:, E + 1:], ends[:, E - 1:E].broadcast_to([P, AHEAD])))


AHEAD = 3


def experts(nc, const, lo16, hi16, starts, w_gu, w_down, rows, out):
    ident, passed = const[0], const[-1]
    N = B * TB
    W = 2 * P
    NGU, NDN = 4 * FB, 2 * FB
    OWN, POOL_DN = 1, 2 * (FB - 1)
    NHI, NLO = NGU + NDN - OWN, NGU + NDN - POOL_DN
    CHUNKS = 2 * FB
    with ExitStack() as scope:
        m = Memory(nc, scope)
        gu_raw = m.sb("gu_raw", [P, FB, HB * W])
        dn_raw = m.sb("dn_raw", [P, FB, H])
        gu_hi = m.sb("gu_hi", [P, FB, HB * W], F32R)
        gu_lo = m.sb("gu_lo", [P, FB, HB * W], F32R)
        dn_hi = m.sb("dn_hi", [P, FB, H], F32R)
        dn_lo = m.sb("dn_lo", [P, FB, H], F32R)
        x_rows = m.sb("x_rows", [P, H + E])
        xe_hi = m.sb("xe_hi", [P, H], F32R)
        xe_lo = m.sb("xe_lo", [P, H], F32R)
        silu = m.sb("silu", [P, FB, P])
        act_h = m.sb("act_h", [P, FB, P])
        ht_hi = m.sb("ht_hi", [P, FB, P], F32R)
        ht_lo = m.sb("ht_lo", [P, FB, P], F32R)
        y_out = m.sb("y_out", [P, H])
        w_next = m.sb("w_next", [P, E])
        w_now = m.sb("w_now", [P, 1])
        warm = m.sb("warm", [P, 1])
        first_load = m.sb("first_load_e", [1, 1])
        gather_i = m.sb("gather_i", [P, 1], I32)
        scatter_i = m.sb("scatter_i", [P, 1], I32)
        table = m.sb("table", [P, 1 + N * TOPK + E + N], I32)
        own = m.sb("own", [P, 1])
        iota_lo = m.sb("iota_lo", [P, P], BF16)
        iota_hi = m.sb("iota_hi", [P, N], BF16)
        row_base = m.sb("row_base", [P, N, N], BF16)
        at_lo = m.sb("at_lo16", [P, N, P], BF16)
        at_hi = m.sb("at_hi16", [P, N, 2, N], BF16)
        found = m.sb("found", [P, 2, N])
        ps_gu = m.ps("ps_gu", [P, 2, BANK])
        ps_x1 = m.ps("ps_xe", [P, H])
        ps_y = m.ps("ps_y", [P, H])
        ps_h = m.ps("ps_h", [P, BANK])
        ps_l = m.ps("ps_l", [P, BANK])

        raw_in = [m.sem(f"raw_in{c}") for c in range(CHUNKS)]
        hi_ok, lo_ok, dn_lo_ok = m.sem("we_hi_ok"), m.sem("we_lo_ok"), m.sem("we_dn_lo_ok")
        own_hi = m.sem("we_own_hi")
        set_up = m.sem("set_up")
        mask_ok, list_a, list_ps, list_id, found_ok, list_ok = (
            m.sem(n) for n in ("mask_ok", "list_a", "list_ps", "list_id", "found_ok", "list_ok"))
        gidx_ok, xe_ps, xe_hi_ok, xe_lo_ok, wn_ok = (m.sem(n) for n in ("gidx_ok", "xe_ps", "xe_hi_ok", "xe_lo_ok", "wn_ok"))
        gu_ok, silu_ok, h_ok, h_ps, ht_hi_ok, ht_lo_ok = (m.sem(n) for n in ("gu_ok", "silu_ok", "h_ok", "h_ps", "ht_hi_ok", "ht_lo_ok"))
        dn_ok, sidx_ok, y_ok = (m.sem(n) for n in ("dn_ok", "sidx_ok", "y_ok"))
        rows_in, y_sent = m.dma_sem("rows_in"), m.dma_sem("y_sent")
        wnow_ok = m.sem("wnow_ok")

        def start_of(eng, e):
            return eng.value_load(starts[0:1, bass.ds(e, 1)], min_val=0, max_val=N * TOPK + E)

        def for_blocks(eng, body):
            with eng.Fori(0, E) as e:
                g0 = start_of(eng, e)
                g1 = start_of(eng, e + 1)
                body(e, g0, True)
                with eng.If(g1 - g0 > 1):
                    with eng.Fori(g0 + 1, g1) as g:
                        body(e, g, False)

        m.start_counts()
        block = scope.enter_context(nc.Block())

        @block.sync
        def _(sp):
            def load(e, c):
                if c < FB:
                    sp.dma_start(gu_raw[:, c, :].rearrange("p (k c) -> p k c", c=W),
                                 w_gu[e, c].rearrange("(k p) c -> p k c", p=P)).then_inc(raw_in[c], 16)
                else:
                    sp.dma_start(dn_raw[:, c - FB, :], w_down[e, (c - FB) * P:(c - FB + 1) * P, :]).then_inc(raw_in[c], 16)

            for c in range(CHUNKS):
                load(0, c)
            with sp.Fori(1, E) as e:
                for c in range(CHUNKS):
                    if c < FB:
                        sp.wait_ge(lo_ok, START + (e - 1) * NLO + 4 * (c + 1))
                    elif c < CHUNKS - 1:
                        sp.wait_ge(dn_lo_ok, START + (e - 1) * POOL_DN + 2 * (c - FB + 1))
                    else:
                        sp.wait_ge(lo_ok, START + e * NLO)
                    load(e, c)

        @block.gpsimd
        def _(pool):
            pool.dma_start(first_load[:, :], rows[0:1, 0:1]).then_inc(y_sent, LOADED)

            pool.iota(own[:, :], [[1, 1]], base=0, channel_multiplier=1, allow_small_or_imprecise_dtypes=True).then_inc(set_up, 1)
            pool.iota(iota_lo[:, :], [[1, P]], base=1, channel_multiplier=0, allow_small_or_imprecise_dtypes=True).then_inc(set_up, 1)
            pool.iota(iota_hi[:, :], [[1, N]], base=0, channel_multiplier=0, allow_small_or_imprecise_dtypes=True).then_inc(set_up, 1)
            pool.iota(row_base[:, :, :], [[P, N], [0, N]], base=P, channel_multiplier=0, allow_small_or_imprecise_dtypes=True).then_inc(set_up, 1)
            pool.iota(table[:, :], [[0, table.shape[1]]], base=0, channel_multiplier=1).then_inc(set_up, 1)
            pool.iota(scatter_i[:, :], [[0, 1]], base=0, channel_multiplier=1).then_inc(set_up, 1)

            def gather(n):
                pool.wait_ge(gidx_ok, START + n + 1)
                if not (isinstance(n, int) and n == 0):
                    pool.wait_ge(wn_ok, START + n)
                stand_alone(pool, passed)
                pool.indirect_dma_start(x_rows[:, :], None, rows, bass.IndirectOffsetOnAxis(ap=gather_i[:, 0:1], axis=0)).then_inc(rows_in, 16)

            gather(0)
            gather(1)

            def body(e, g, first):
                pool.wait_ge(y_ok, START + g + 1)
                pool.wait_ge(sidx_ok, START + g + 1)
                stand_alone(pool, passed)
                pool.indirect_dma_start(out, bass.IndirectOffsetOnAxis(ap=scatter_i[:, 0:1], axis=0), y_out[:, :], None,
                                        compute_op=ALU.add).then_inc(y_sent, 16)
                if first:
                    for n in range(POOL_DN):
                        pool.wait_ge(hi_ok, START + e * NHI + NGU - OWN + n + 1)
                        f, a = n // 2, slice(n % 2 * BANK, (n % 2 + 1) * BANK)
                        pool.tensor_tensor(dn_lo[:, f, a], dn_raw[:, f, a], raw(dn_hi[:, f, a]), ALU.subtract).then_inc(dn_lo_ok, 1)
                gather(g + 2)

            for_blocks(pool, body)
            total = start_of(pool, E)
            pool.wait_ge(y_ok, START + total + 1)
            pool.wait_ge(sidx_ok, START + total + 1)
            stand_alone(pool, passed)
            pool.indirect_dma_start(out, bass.IndirectOffsetOnAxis(ap=scatter_i[:, 0:1], axis=0), y_out[:, :], None,
                                    compute_op=ALU.add).then_inc(y_sent, 16)
            pool.wait_ge(y_sent, LOADED + (total + 1) * 16)
            pool.wait_ge(rows_in, (total + 2) * 16)

        @block.tensor
        def _(pe):
            def split_product(out, a_hi, a_lo, w_hi, w_lo, first, last):
                pe.matmul(out, a_hi, w_hi, start=first, stop=False)
                pe.matmul(out, a_hi, w_lo, start=False, stop=False)
                return pe.matmul(out, a_lo, w_hi, start=False, stop=last)

            def find_rows(n):
                pe.wait_ge(list_a, START + n + 1)
                pe.wait_ge(list_id, START + n)
                for i in range(N):
                    mm = pe.matmul(ps_l[:, 0:2 * N], at_lo[:, i, :], at_hi[:, i, :, :].rearrange("p a h -> p (a h)"),
                                   start=(i == 0), stop=(i == N - 1))
                mm.then_inc(list_ps, 1)

            def turn_rows(n):
                pe.wait_ge(rows_in, (n + 1) * 16)
                pe.wait_ge(xe_lo_ok, START + n * 2)
                for k in range(HB):
                    mm = pe.transpose(ps_x1[:, k * P:(k + 1) * P], x_rows[:, k * P:(k + 1) * P], ident[:, :])
                mm.then_inc(xe_ps, 1)

            find_rows(0)
            turn_rows(0)
            for n in range(1, AHEAD):
                find_rows(n)
            pe.wait_ge(set_up, START + 9)
            for k in range(HB):
                mm = pe.transpose(ps_y[:, k * P:(k + 1) * P], y_out[:, k * P:(k + 1) * P], ident[:, :])
            mm.then_inc(dn_ok, 1)

            def body(e, g, first):
                def first_layer(f):
                    pe.wait_ge(xe_lo_ok, START + g * 2 + 2)
                    if f == 2:
                        pe.wait_ge(h_ok, START + g * FB + 1)
                    else:
                        pe.wait_ge(h_ok, START + g * FB)
                    gw = slice(0, W)
                    for k in range(HB):
                        if first and k % 2 == 0:
                            pe.wait_ge(lo_ok, START + e * NLO + 4 * f + k // 2 + 1)
                        a = slice(k * P, (k + 1) * P)
                        c = slice(k * W, (k + 1) * W)
                        mm = split_product(ps_gu[:, f % 2, gw], xe_hi[:, a], xe_lo[:, a], gu_hi[:, f, c], gu_lo[:, f, c], k == 0, k == HB - 1)
                    mm.then_inc(gu_ok, 1)

                def turn_h(f):
                    pe.wait_ge(h_ok, START + g * FB + f + 1)
                    pe.wait_ge(ht_lo_ok, START + g * FB + f)
                    pe.transpose(ps_h[:, f * P:(f + 1) * P], act_h[:, f, :], ident[:, :]).then_inc(h_ps, 1)

                def second_layer(f):
                    pe.wait_ge(ht_lo_ok, START + g * FB + f + 1)
                    if f == 0:
                        pe.wait_ge(y_ok, START + g + 1)
                    for c in range(H // BANK):
                        if first:
                            if 2 * f < POOL_DN:
                                pe.wait_ge(dn_lo_ok, START + e * POOL_DN + 2 * f + c + 1)
                            else:
                                pe.wait_ge(lo_ok, START + e * NLO + NGU + 2 * f - POOL_DN + c + 1)
                        n = slice(c * BANK, (c + 1) * BANK)
                        mm = split_product(ps_y[:, n], ht_hi[:, f, :], ht_lo[:, f, :], dn_hi[:, f, n], dn_lo[:, f, n], f == 0, f == FB - 1)
                    if f == FB - 1:
                        mm.then_inc(dn_ok, 1)

                first_layer(0)
                first_layer(1)
                if first:
                    find_rows(e + AHEAD)
                turn_h(0)
                first_layer(2)
                turn_h(1)
                turn_rows(g + 1)
                turn_h(2)
                second_layer(0)
                second_layer(1)
                second_layer(2)

            for_blocks(pe, body)

        @block.scalar
        def _(act):
            def split_rows(n):
                act.wait_ge(xe_ps, START + n + 1)
                act.wait_ge(gu_ok, START + n * FB)
                for c in range(2):
                    a = slice(c * BANK, (c + 1) * BANK)
                    act.activation(xe_hi[:, a], ps_x1[:, a], ACT.Copy).then_inc(xe_hi_ok, 1)

            act.wait_ge(set_up, START + 9)
            split_rows(0)

            def finish(n):
                act.wait_ge(dn_ok, START + n + 1)
                act.wait_ge(sidx_ok, START + n + 1)
                act.wait_ge(y_sent, LOADED + n * 16)
                act.activation(y_out[:, :], ps_y[:, :], ACT.Copy, scale=w_now[:, 0:1]).then_inc(y_ok, 1)

            def body(e, g, first):
                def split(kind, f):
                    c = f if kind == "gu" else FB + f
                    act.wait_ge(raw_in[c], START + e * 16 + 16)
                    if kind == "gu":
                        act.wait_ge(gu_ok, START + g * FB)
                        for q in range(OWN if f == 0 else 0, 4):
                            a = slice(q * 2 * W, (q + 1) * 2 * W)
                            act.activation(gu_hi[:, f, a], gu_raw[:, f, a], ACT.Copy).then_inc(hi_ok, 1)
                    else:
                        act.wait_ge(dn_ok, START + g + 1)
                        for q in range(2):
                            a = slice(q * BANK, (q + 1) * BANK)
                            act.activation(dn_hi[:, f, a], dn_raw[:, f, a], ACT.Copy).then_inc(hi_ok, 1)

                def silu_of(f):
                    act.wait_ge(gu_ok, START + g * FB + f + 1)
                    act.wait_ge(h_ok, START + g * FB)
                    act.activation(silu[:, f, :], ps_gu[:, f % 2, 0:P], ACT.Silu).then_inc(silu_ok, 1)

                def split_h(f):
                    act.wait_ge(h_ps, START + g * FB + f + 1)
                    act.wait_ge(dn_ok, START + g + 1)
                    act.activation(ht_hi[:, f, :], ps_h[:, f * P:(f + 1) * P], ACT.Copy).then_inc(ht_hi_ok, 1)

                if first:
                    act.activation(warm[:, :], warm[:, :], ACT.Silu)
                    split("gu", 0)
                    split("gu", 1)
                finish(g)
                silu_of(0)
                if first:
                    split("gu", 2)
                silu_of(1)
                split_h(0)
                if first:
                    split("dn", 0)
                silu_of(2)
                split_h(1)
                if first:
                    split("dn", 1)
                split_h(2)
                if first:
                    split("dn", 2)
                split_rows(g + 1)

            for_blocks(act, body)
            finish(start_of(act, E))

        @block.vector
        def _(dve):
            dve.memset(y_out[:, :], 0.0).then_inc(set_up, 1)
            dve.memset(w_next[:, :], 0.0).then_inc(set_up, 1)
            dve.memset(warm[:, :], 0.0).then_inc(set_up, 1)
            dve.memset(w_now[:, :], 0.0).then_inc(sidx_ok, 1)
            dve.wait_ge(set_up, START + 9)

            LIST_PARTS = 4

            def start_list(n):
                dve.wait_ge(list_ps, START + n)
                hi = hi16[:, bass.ds(n, 1), :].rearrange("p a n -> p (a n)").unsqueeze(2)
                dve.tensor_tensor(at_hi[:, :, 1, :], iota_hi[:, :].unsqueeze(1).broadcast_to([P, N, N]),
                                  hi.broadcast_to([P, N, N]), ALU.is_equal).then_inc(mask_ok, 1)

            def list_part(n, part):
                a, w = part * N // LIST_PARTS, N // LIST_PARTS
                lo = lo16[:, bass.ds(n, 1), a:a + w].rearrange("p a n -> p (a n)").unsqueeze(2)
                dve.tensor_tensor(at_lo[:, a:a + w, :], iota_lo[:, :].unsqueeze(1).broadcast_to([P, w, P]),
                                  lo.broadcast_to([P, w, P]), ALU.is_equal)

            def end_list(n):
                dve.wait_ge(mask_ok, START + n * 2 + 1)
                dve.tensor_scalar(at_hi[:, :, 0, :], at_hi[:, :, 1, :], own[:, 0:1], None, ALU.mult).then_inc(mask_ok, 1)
                dve.wait_ge(mask_ok, START + n * 2 + 2)
                dve.tensor_tensor(at_hi[:, :, 1, :], at_hi[:, :, 1, :], row_base[:, :, :], ALU.mult).then_inc(list_a, 1)

            def make_list(n):
                start_list(n)
                for part in range(LIST_PARTS):
                    list_part(n, part)
                end_list(n)

            def finish_list(n):
                dve.wait_ge(list_ps, START + n + 1)
                dve.tensor_reduce(found[:, 0, :], ps_l[:, 0:2 * N].rearrange("p (a h) -> p h a", a=2), AX.X, ALU.add).then_inc(list_id, 1)
                dve.wait_ge(list_id, START + n + 1)
                dve.tensor_scalar(found[:, 1, :], found[:, 0, :], 0.0, own[:, 0:1], ALU.is_equal, ALU.mult).then_inc(found_ok, 1)
                dve.wait_ge(found_ok, START + n + 1)
                at = start_of(dve, n)
                dve.tensor_tensor(table[:, bass.ds(at + 1, N)], found[:, 0, :], found[:, 1, :], ALU.add).then_inc(list_ok, 1)
                dve.wait_ge(list_ok, START + n + 1)

            def gather_index(n):
                if not (isinstance(n, int) and n == 0):
                    dve.wait_ge(rows_in, n * 16)
                dve.tensor_copy(gather_i[:, :], table[:, bass.ds(n + 1, 1)]).then_inc(gidx_ok, 1)

            def rest_of_rows(n):
                for c in range(2):
                    dve.wait_ge(xe_hi_ok, START + n * 2 + c + 1)
                    a = slice(c * BANK, (c + 1) * BANK)
                    dve.tensor_tensor(xe_lo[:, a], ps_x1[:, a], raw(xe_hi[:, a]), ALU.subtract).then_inc(xe_lo_ok, 1)

            def keep_weights(n):
                dve.wait_ge(xe_ps, START + n + 1)
                dve.tensor_copy(w_next[:, :], x_rows[:, H:H + E]).then_inc(wn_ok, 1)

            make_list(0)
            finish_list(0)
            gather_index(0)
            make_list(1)
            keep_weights(0)
            finish_list(1)
            gather_index(1)
            rest_of_rows(0)
            for n in range(2, AHEAD):
                make_list(n)
                finish_list(n)
            make_list(AHEAD)

            def body(e, g, first):
                def rest_of(f):
                    for q in range(4):
                        a = slice(q * BANK, (q + 1) * BANK)
                        if 4 * f + q < OWN:
                            dve.wait_ge(raw_in[0], START + e * 16 + 16)
                            dve.wait_ge(gu_ok, START + g * FB)
                            dve.tensor_copy(gu_hi[:, f, a], gu_raw[:, f, a]).then_inc(own_hi, 1)
                            dve.wait_ge(own_hi, START + e * OWN + q + 1)
                        else:
                            dve.wait_ge(hi_ok, START + e * NHI + 4 * f + q - OWN + 1)
                        dve.tensor_tensor(gu_lo[:, f, a], gu_raw[:, f, a], raw(gu_hi[:, f, a]), ALU.subtract).then_inc(lo_ok, 1)

                def rest_of_dn(n):
                    dve.wait_ge(hi_ok, START + e * NHI + NGU - OWN + n + 1)
                    f, a = n // 2, slice(n % 2 * BANK, (n % 2 + 1) * BANK)
                    dve.tensor_tensor(dn_lo[:, f, a], dn_raw[:, f, a], raw(dn_hi[:, f, a]), ALU.subtract).then_inc(lo_ok, 1)

                def multiply(f):
                    dve.wait_ge(silu_ok, START + g * FB + f + 1)
                    dve.wait_ge(h_ps, START + g * FB)
                    dve.tensor_tensor(act_h[:, f, :], ps_gu[:, f % 2, P:W], silu[:, f, :], ALU.mult).then_inc(h_ok, 1)

                def rest_of_h(f):
                    dve.wait_ge(ht_hi_ok, START + g * FB + f + 1)
                    dve.tensor_tensor(ht_lo[:, f, :], ps_h[:, f * P:(f + 1) * P], raw(ht_hi[:, f, :]), ALU.subtract).then_inc(ht_lo_ok, 1)

                after = e + AHEAD + 1
                if first:
                    rest_of(0)
                    rest_of(1)
                multiply(0)
                if first:
                    rest_of(2)
                multiply(1)
                rest_of_h(0)
                if first:
                    start_list(after)
                    list_part(after, 0)
                multiply(2)
                rest_of_h(1)
                if first:
                    list_part(after, 1)
                rest_of_h(2)
                if first:
                    for n in range(POOL_DN, NDN):
                        rest_of_dn(n)
                dve.wait_ge(y_ok, START + g + 1)
                dve.wait_ge(wn_ok, START + g + 1)
                stand_alone(dve, passed)
                dve.tensor_copy(w_now[:, :], w_next[:, bass.ds(e, 1)]).then_inc(wnow_ok, 1)
                dve.wait_ge(wnow_ok, START + g + 1)
                keep_weights(g + 1)
                gather_index(g + 2)
                rest_of_rows(g + 1)
                dve.wait_ge(y_sent, LOADED + (g + 1) * 16)
                dve.tensor_copy(scatter_i[:, :], table[:, bass.ds(g + 1, 1)]).then_inc(sidx_ok, 1)
                if first:
                    finish_list(e + AHEAD)
                    for part in range(2, LIST_PARTS):
                        list_part(after, part)
                    end_list(after)

            for_blocks(dve, body)


def rope_tables():
    inv = 1.0 / 10000.0 ** (np.arange(0, HD, 2, dtype=np.float32) / HD)
    freqs = np.einsum("i,j->ij", np.arange(S, dtype=np.float32), inv)
    emb = np.concatenate((freqs, freqs), axis=-1)
    c, s = np.cos(emb).astype(np.float32), np.sin(emb).astype(np.float32)
    s[:, :HD // 2] *= -1
    scale = np.float32(HD ** -0.5)
    c = c[:, :HD // 2]
    return (np.ascontiguousarray(np.stack([c * scale, c], 1)), np.ascontiguousarray(np.stack([s * scale, s], 1)))


def host_layout(i):
    i = {n: np.asarray(a) for n, a in i.items()}
    qkv = np.stack([i[f"L0_attn_W{n}"].T.reshape(H, NP, P) for n in "qkv"], 2)
    cos, sin = rope_tables()
    tidy = np.ascontiguousarray
    return {
        "x": i["x"],
        "wqkv": tidy(qkv.transpose(1, 0, 2, 3).reshape(NP, H, 3 * P)),
        "cos": cos, "sin": sin,
        "wo": tidy(i["L0_attn_Wo"].T),
        "ctx_t": tidy(i["ctx_1024"].transpose(0, 2, 1)),
        "xw": tidy(np.concatenate([i["L0_xattn_Wq"].T, i["L0_xattn_Wk"].T], 1)),
        "xbias": tidy(np.stack([i["L0_xattn_bq"], i["L0_xattn_bk"]], 1)),
        "gate": tidy(i["L0_ffn_gate_weight"].T),
        "similarity": i["L0_ffn_similarity"],
        "w_gu": tidy(i["L0_ffn_gate_up_proj"].reshape(E, 2, FB, P, H).transpose(0, 2, 4, 1, 3).reshape(E, FB, H, 2 * P)),
        "w_down": tidy(i["L0_ffn_down_proj"].transpose(0, 2, 1)),
    }


def build(nc, x, wqkv, cos, sin, wo, ctx_t, xw, xbias, gate, similarity, w_gu, w_down, out):
    attn_out = nc.dram_tensor("attn_out", (B, NP, P, S), F32, kind="Internal").ap()
    rows = nc.dram_tensor("rows", (P + B * S, H + E), F32, kind="Internal").ap()
    with ExitStack() as scope:
        m = Memory(nc, scope)
        const = constants(nc, m)
        self_attention(nc, const, x, wqkv, cos, sin, attn_out)
        logits = m.sb("logits", [P, B * TB, E])
        mix_features(nc, const, logits, x, attn_out, wo, ctx_t, xw, xbias, gate, rows, out)
        lo16 = m.sb("lo16", [P, E + AHEAD + 1, B * TB], BF16)
        hi16 = m.sb("hi16", [P, E + AHEAD + 1, B * TB], BF16)
        starts = m.sb("starts", [P, E + 1 + AHEAD], I32)
        route(nc, const, logits, lo16, hi16, starts, similarity, rows)
        experts(nc, const, lo16, hi16, starts, w_gu, w_down, rows, out)


def kernel(**inputs):
    import concourse.bacc as bacc
    from concourse.bass_utils import run_bass_kernel_spmd

    nc = bacc.Bacc("TRN2", target_bir_lowering=False, num_devices=1)
    arrays = host_layout(inputs)
    args = {n: nc.dram_tensor(n, a.shape, mybir.dt.from_np(a.dtype), kind="ExternalInput").ap() for n, a in arrays.items()}
    out = nc.dram_tensor("out", (P + B * S, H), F32, kind="ExternalOutput").ap()
    build(nc, **args, out=out)
    r = run_bass_kernel_spmd(nc, [arrays], core_ids=[0])
    return r.results[0]["out"][P:].reshape(B, S, H)
```
